# Optimizing a Trainium2 kernel written in Bass

```python
import numpy as np
import jax
import jax.numpy as jnp

def _softmax(x, axis=-1):
    return jax.nn.softmax(x, axis=axis)

def _gelu(x):
    return jax.nn.gelu(x, approximate=True)

def _silu(x):
    return jax.nn.silu(x)

def _sigmoid(x):
    return jax.nn.sigmoid(x)

def _layernorm(x, axis=-1, eps=1e-05):
    m = jnp.mean(x, axis=axis, keepdims=True)
    v = jnp.var(x, axis=axis, keepdims=True)
    return (x - m) / jnp.sqrt(v + eps)

def _scatter_add(tgt, idx, src, axis=0):
    return tgt.at[idx].add(src)

def _segment_sum(src, seg, n):
    return jax.ops.segment_sum(src, seg, n)
kernel_name = 'mk_gps_d1_gnn_r8_1dfabd'

def setup_inputs(seed: int=0):
    np.random.seed(seed)
    _w = jnp.asarray

    def _rec_inputs():
        import jax
        import jax.numpy as jnp
        _gk = jax.random.key(seed)
        x = -0.0003713 + 1 * jax.random.normal(jax.random.fold_in(_gk, 1), (6250, 256), jnp.float32)
        _s = jax.random.randint(jax.random.fold_in(_gk, 2), (50000,), 0, 6250, jnp.int32)
        _d = jax.random.randint(jax.random.fold_in(_gk, 3), (50000,), 0, 6250, jnp.int32)
        _loop = jnp.arange(6250, dtype=jnp.int32)
        src = jnp.concatenate([_s, _d, _loop])
        dst = jnp.concatenate([_d, _s, _loop])
        _o = jnp.argsort(dst, stable=True)
        src = src[_o]
        dst = dst[_o]
        edge_attr_64 = -5.16925e-05 + 1.00005 * jax.random.normal(jax.random.fold_in(_gk, 12), (106250, 64), jnp.float32)
        return (x, src, dst, edge_attr_64)
    x, src, dst, edge_attr_64 = _rec_inputs()

    def _L0_gnn_setup():
        import jax, jax.numpy as jnp
        import numpy as np
        N = 6250
        E = 200000
        IN_F = 256
        EDGE_F = 64
        HALF = IN_F // 2
        BASE = IN_F + HALF
        OUT_F = 256
        NEG_SLOPE = 0.01
        key = jax.random.key(seed)
        ks = jax.random.split(key, 10)
        x = jax.random.normal(ks[0], (N, IN_F), dtype=jnp.float32)
        edge_index = jax.random.randint(ks[1], (2, E), 0, N, dtype=jnp.int64)
        edge_attr = jax.random.normal(ks[2], (E, EDGE_F), dtype=jnp.float32)
        batch = jnp.sort(jax.random.randint(ks[3], (N,), 0, 512, dtype=jnp.int64))
        W_edge = jax.random.normal(ks[4], (EDGE_F, HALF), dtype=jnp.float32) * 0.05
        b_edge = jnp.zeros((HALF,), dtype=jnp.float32)
        W_conv = jax.random.normal(ks[5], (BASE, OUT_F), dtype=jnp.float32) * 0.05
        b_conv = jnp.zeros((OUT_F,), dtype=jnp.float32)
        W_res = jax.random.normal(ks[6], (BASE, OUT_F), dtype=jnp.float32) * 0.05
        b_res = jnp.zeros((OUT_F,), dtype=jnp.float32)
        return {'x': x, 'edge_index': edge_index, 'edge_attr': edge_attr, 'batch': batch, 'W_edge': W_edge, 'b_edge': b_edge, 'W_conv': W_conv, 'b_conv': b_conv, 'W_res': W_res, 'b_res': b_res}
    _L0_gnn_all = _L0_gnn_setup()
    _L0_gnn_in = {k: v for k, v in _L0_gnn_all.items() if k in ('W_edge', 'b_edge', 'W_conv', 'b_conv', 'W_res', 'b_res')}
    del _L0_gnn_all

    def _L0_mix_setup():
        import jax, jax.numpy as jnp
        import numpy as np
        D_MODEL = 256
        NHEAD = 8
        D_HEAD = D_MODEL // NHEAD
        DIM_FF = 1024
        B, L = (4, 2048)
        LN_EPS = 1e-05

        def _layernorm(x, g, b):
            mu = jnp.mean(x, axis=-1, keepdims=True)
            var = jnp.mean((x - mu) ** 2, axis=-1, keepdims=True)
            return (x - mu) * jax.lax.rsqrt(var + LN_EPS) * g + b

        def _phi(x):
            return jnp.where(x > 0, x + 1.0, jnp.exp(x))
        key = jax.random.key(seed)
        ks = jax.random.split(key, 16)
        s_in = 1.0 / np.sqrt(D_MODEL)
        s_ff = 1.0 / np.sqrt(DIM_FF)
        inp = {'x': jax.random.normal(ks[0], (B, L, D_MODEL), dtype=jnp.float32), 'Wq': jax.random.normal(ks[1], (D_MODEL, D_MODEL), dtype=jnp.float32) * s_in, 'bq': jnp.zeros((D_MODEL,), jnp.float32), 'Wk': jax.random.normal(ks[2], (D_MODEL, D_MODEL), dtype=jnp.float32) * s_in, 'bk': jnp.zeros((D_MODEL,), jnp.float32), 'Wv': jax.random.normal(ks[3], (D_MODEL, D_MODEL), dtype=jnp.float32) * s_in, 'bv': jnp.zeros((D_MODEL,), jnp.float32), 'Wo': jax.random.normal(ks[4], (D_MODEL, D_MODEL), dtype=jnp.float32) * s_in, 'bo': jnp.zeros((D_MODEL,), jnp.float32), 'W1': jax.random.normal(ks[5], (D_MODEL, DIM_FF), dtype=jnp.float32) * s_in, 'b1': jnp.zeros((DIM_FF,), jnp.float32), 'W2': jax.random.normal(ks[6], (DIM_FF, D_MODEL), dtype=jnp.float32) * s_ff, 'b2': jnp.zeros((D_MODEL,), jnp.float32), 'ln1_g': jnp.ones((D_MODEL,), jnp.float32), 'ln1_b': jnp.zeros((D_MODEL,), jnp.float32), 'ln2_g': jnp.ones((D_MODEL,), jnp.float32), 'ln2_b': jnp.zeros((D_MODEL,), jnp.float32)}
        return inp
    _L0_mix_all = _L0_mix_setup()
    _L0_mix_in = {k: v for k, v in _L0_mix_all.items() if k in ('Wq', 'bq', 'Wk', 'bk', 'Wv', 'bv', 'Wo', 'bo', 'W1', 'b1', 'W2', 'b2', 'ln1_g', 'ln1_b', 'ln2_g', 'ln2_b')}
    del _L0_mix_all

    def _L0_ffn_setup():
        import jax, jax.numpy as jnp
        import numpy as np
        B, S, D, E, H, K = (4, 512, 256, 8, 512, 2)
        key = jax.random.key(seed)
        ks = jax.random.split(key, 6)
        x = jax.random.normal(ks[0], (B, S, D), jnp.float32)
        Wg = jax.random.normal(ks[1], (D, E), jnp.float32) * 0.02
        bg = jnp.zeros((E,), jnp.float32)
        W1 = jax.random.normal(ks[2], (E, D, H), jnp.float32) * 0.02
        b1 = jnp.zeros((E, H), jnp.float32)
        W2 = jax.random.normal(ks[3], (E, H, D), jnp.float32) * 0.02
        b2 = jnp.zeros((E, D), jnp.float32)
        return {'x': x, 'Wg': Wg, 'bg': bg, 'W1': W1, 'b1': b1, 'W2': W2, 'b2': b2}
    _L0_ffn_all = _L0_ffn_setup()
    _L0_ffn_in = {k: v for k, v in _L0_ffn_all.items() if k in ('Wg', 'bg', 'W1', 'b1', 'W2', 'b2')}
    del _L0_ffn_all
    return {'x': x, 'src': src, 'dst': dst, 'edge_attr_64': edge_attr_64, 'L0_gnn_W_edge': _L0_gnn_in['W_edge'], 'L0_gnn_b_edge': _L0_gnn_in['b_edge'], 'L0_gnn_W_conv': _L0_gnn_in['W_conv'], 'L0_gnn_b_conv': _L0_gnn_in['b_conv'], 'L0_gnn_W_res': _L0_gnn_in['W_res'], 'L0_gnn_b_res': _L0_gnn_in['b_res'], 'L0_mix_Wq': _L0_mix_in['Wq'], 'L0_mix_bq': _L0_mix_in['bq'], 'L0_mix_Wk': _L0_mix_in['Wk'], 'L0_mix_bk': _L0_mix_in['bk'], 'L0_mix_Wv': _L0_mix_in['Wv'], 'L0_mix_bv': _L0_mix_in['bv'], 'L0_mix_Wo': _L0_mix_in['Wo'], 'L0_mix_bo': _L0_mix_in['bo'], 'L0_mix_W1': _L0_mix_in['W1'], 'L0_mix_b1': _L0_mix_in['b1'], 'L0_mix_W2': _L0_mix_in['W2'], 'L0_mix_b2': _L0_mix_in['b2'], 'L0_mix_ln1_g': _L0_mix_in['ln1_g'], 'L0_mix_ln1_b': _L0_mix_in['ln1_b'], 'L0_mix_ln2_g': _L0_mix_in['ln2_g'], 'L0_mix_ln2_b': _L0_mix_in['ln2_b'], 'L0_ffn_Wg': _L0_ffn_in['Wg'], 'L0_ffn_bg': _L0_ffn_in['bg'], 'L0_ffn_W1': _L0_ffn_in['W1'], 'L0_ffn_b1': _L0_ffn_in['b1'], 'L0_ffn_W2': _L0_ffn_in['W2'], 'L0_ffn_b2': _L0_ffn_in['b2']}

def reference(x, src, dst, edge_attr_64, L0_gnn_W_edge, L0_gnn_b_edge, L0_gnn_W_conv, L0_gnn_b_conv, L0_gnn_W_res, L0_gnn_b_res, L0_mix_Wq, L0_mix_bq, L0_mix_Wk, L0_mix_bk, L0_mix_Wv, L0_mix_bv, L0_mix_Wo, L0_mix_bo, L0_mix_W1, L0_mix_b1, L0_mix_W2, L0_mix_b2, L0_mix_ln1_g, L0_mix_ln1_b, L0_mix_ln2_g, L0_mix_ln2_b, L0_ffn_Wg, L0_ffn_bg, L0_ffn_W1, L0_ffn_b1, L0_ffn_W2, L0_ffn_b2):
    import jax
    import jax.numpy as jnp

    def _L0_gnn_ref(x, edge_index, edge_attr, batch, W_edge, b_edge, W_conv, b_conv, W_res, b_res):
        import jax, jax.numpy as jnp
        import numpy as np
        N = 6250
        E = 200000
        IN_F = 256
        EDGE_F = 64
        HALF = IN_F // 2
        BASE = IN_F + HALF
        OUT_F = 256
        NEG_SLOPE = 0.01
        n = x.shape[0]
        src, dst = (edge_index[0], edge_index[1])
        per_node = jax.ops.segment_sum(edge_attr, src, num_segments=n)
        per_node = jax.nn.leaky_relu(per_node @ W_edge + b_edge, negative_slope=NEG_SLOPE)
        h = jnp.concatenate([x, per_node], axis=1)
        identity = h
        hw = h @ W_conv
        ones = jnp.ones((src.shape[0],), dtype=hw.dtype)
        deg = jax.ops.segment_sum(ones, dst, num_segments=n) + 1.0
        dinv = jax.lax.rsqrt(deg)
        norm = dinv[src] * dinv[dst]
        agg = jax.ops.segment_sum(norm[:, None] * hw[src], dst, num_segments=n)
        out = agg + (dinv * dinv)[:, None] * hw + b_conv
        out = out + identity @ W_res + b_res
        return jax.nn.relu(out)

    def _L0_mix_ref(x, Wq, bq, Wk, bk, Wv, bv, Wo, bo, W1, b1, W2, b2, ln1_g, ln1_b, ln2_g, ln2_b):
        import jax, jax.numpy as jnp
        import numpy as np
        D_MODEL = 256
        NHEAD = 8
        D_HEAD = D_MODEL // NHEAD
        DIM_FF = 1024
        B, L = (4, 2048)
        LN_EPS = 1e-05

        def _layernorm(x, g, b):
            mu = jnp.mean(x, axis=-1, keepdims=True)
            var = jnp.mean((x - mu) ** 2, axis=-1, keepdims=True)
            return (x - mu) * jax.lax.rsqrt(var + LN_EPS) * g + b

        def _phi(x):
            return jnp.where(x > 0, x + 1.0, jnp.exp(x))
        Bq, Lq, _ = x.shape
        q = (x @ Wq + bq).reshape(Bq, Lq, NHEAD, D_HEAD)
        k = (x @ Wk + bk).reshape(Bq, Lq, NHEAD, D_HEAD)
        v = (x @ Wv + bv).reshape(Bq, Lq, NHEAD, D_HEAD)
        q_phi = _phi(q)
        k_phi = _phi(k)
        kv = jnp.einsum('blhd,blhe->bhde', k_phi, v)
        k_sum = k_phi.sum(axis=1)
        z = 1.0 / (jnp.einsum('blhd,bhd->blh', q_phi, k_sum) + 1e-06)
        out = jnp.einsum('blhd,bhde,blh->blhe', q_phi, kv, z)
        out = out.reshape(Bq, Lq, D_MODEL) @ Wo + bo
        x = _layernorm(x + out, ln1_g, ln1_b)
        ff = jax.nn.relu(x @ W1 + b1) @ W2 + b2
        x = _layernorm(x + ff, ln2_g, ln2_b)
        return x

    def _L0_ffn_ref(x, Wg, bg, W1, b1, W2, b2):
        import jax, jax.numpy as jnp
        import numpy as np
        B, S, D, E, H, K = (4, 512, 256, 8, 512, 2)
        Bv, Sv, Dv = x.shape
        gate_scores = x @ Wg + bg
        _, idx = jax.lax.top_k(gate_scores, K)
        mask = jax.nn.one_hot(idx, E, dtype=x.dtype).sum(axis=-2)
        xf = x.reshape(-1, Dv)
        mf = mask.reshape(-1, E)
        h = jax.nn.gelu(jnp.einsum('td,edh->teh', xf, W1) + b1[None], approximate=False)
        y = jnp.einsum('teh,ehd->ted', h, W2) + b2[None]
        out = jnp.einsum('ted,te->td', y, mf)
        return out.reshape(Bv, Sv, Dv)
    edge_index = jnp.stack([src, dst])
    batch0 = jnp.zeros((6250,), jnp.int32)
    xn = _layernorm(x, axis=-1)
    x = x + _L0_gnn_ref(xn, edge_index, edge_attr_64, batch0, L0_gnn_W_edge, L0_gnn_b_edge, L0_gnn_W_conv, L0_gnn_b_conv, L0_gnn_W_res, L0_gnn_b_res) + _L0_mix_ref(xn[None], L0_mix_Wq, L0_mix_bq, L0_mix_Wk, L0_mix_bk, L0_mix_Wv, L0_mix_bv, L0_mix_Wo, L0_mix_bo, L0_mix_W1, L0_mix_b1, L0_mix_W2, L0_mix_b2, L0_mix_ln1_g, L0_mix_ln1_b, L0_mix_ln2_g, L0_mix_ln2_b)[0]
    x = x + _L0_ffn_ref(_layernorm(x, axis=-1)[None], L0_ffn_Wg, L0_ffn_bg, L0_ffn_W1, L0_ffn_b1, L0_ffn_W2, L0_ffn_b2)[0]
    return x

_drawn_inputs = setup_inputs


def setup_inputs(seed=0):
    import zlib

    import numpy as np

    out = dict(_drawn_inputs(seed))
    spreads = {'L0_gnn_b_edge': (0.0, 0.381),
     'L0_gnn_b_conv': (0.0, 0.1),
     'L0_gnn_b_res': (0.0, 0.1),
     'L0_mix_bq': (0.0, 0.8),
     'L0_mix_bk': (0.0, 0.8),
     'L0_mix_bv': (0.0, 0.1),
     'L0_mix_bo': (0.0, 0.1),
     'L0_mix_b1': (0.0, 0.1),
     'L0_mix_b2': (0.0, 0.1),
     'L0_mix_ln1_g': (1.0, 0.2),
     'L0_mix_ln1_b': (0.0, 0.1),
     'L0_mix_ln2_g': (1.0, 0.2),
     'L0_mix_ln2_b': (0.0, 0.1),
     'L0_ffn_bg': (0.0, 0.1),
     'L0_ffn_b1': (0.0, 0.476),
     'L0_ffn_b2': (0.0, 0.1)}
    factors = {'L0_mix_Wq': 8.0, 'L0_mix_Wk': 8.0, 'L0_mix_Wv': 6.224}
    for name, (base, spread) in spreads.items():
        noise = np.random.default_rng([zlib.crc32(name.encode()), seed]).standard_normal(out[name].shape)
        drawn = base * np.exp(spread * noise) if base else spread * noise
        out[name] = jnp.asarray(drawn.astype(out[name].dtype))
    for name, factor in factors.items():
        out[name] = (out[name] * factor).astype(out[name].dtype)
    return out
```

```python
from contextlib import ExitStack

import concourse.bass as bass
from concourse import mybir

F32 = mybir.dt.float32
BF16 = mybir.dt.bfloat16
I32 = mybir.dt.int32
U32 = mybir.dt.uint32
ALU = mybir.AluOpType
ACT = mybir.ActivationFunctionType
AX_X = mybir.AxisListType.X

P = 128
N = 6250
NT = -(-N // P)
NP = NT * P
LAST = N - (NT - 1) * P
E = 106250
CH = 16
NCH = -(-E // (P * CH))
ET = NCH * CH
EP = ET * P
D = 256
KD = D // P
EF = 64
FF = 1024
KF = FF // P
NEXP = 8
HID = 512
KH = HID // P
HEAD = 32
NTAB = 4
TROWS = NP + P
QUADS = ET // 4
RQ = 8
GRP = 4
NG = NT // GRP
BG = 7
LN_EPS = 1e-5
LRELU = 0.01
LOADS = 26 * 16
TC = ET // 8


def wait(eng, sem, value):
    if isinstance(value, int) and value <= 0:
        return
    eng.wait_ge(sem, value)


def build(nc, A, out):
    with ExitStack() as ctx:
        def sb(name, shape, dt=F32):
            return ctx.enter_context(nc.sbuf_tensor(name, shape, dt))

        def bank(name, shape=(P, 512), dt=F32):
            return ctx.enter_context(nc.psum_tensor(name, list(shape), dt))

        def sem(name):
            return ctx.enter_context(nc.semaphore(name))

        def dram(name, shape, dt=F32):
            return nc.dram_tensor(name, shape, dt).ap()

        table = [dram(f"table{r}", (TROWS, EF)) for r in range(NTAB)]
        xn_d = dram("xn_d", (NP, D))
        xnT_d = dram("xnT_d", (NP, D))
        mix_d = dram("mix_d", (NP, D))
        g_d = dram("g_d", (NP, D))
        base_d = dram("base_d", (NP, D))

        def rows(t, b, n=1):
            if n == 1:
                return t[bass.ds(b * P, P), :]
            return t[bass.ds(b * P, n * P), :].rearrange("(n p) d -> p n d", p=P)

        ident = sb("ident", [P, P])
        before = sb("before", [P, P])
        raw_iota = sb("raw_iota", [P, P], I32)
        raw_iotb = sb("raw_iotb", [P, NT], I32)
        raw_iotq = sb("raw_iotq", [1, QUADS], I32)
        raw_iotp = sb("raw_iotp", [P, 1], I32)
        iota_r = sb("iota_r", [P, P])
        iota_b = sb("iota_b", [P, NT])
        iota_q = sb("iota_q", [1, QUADS])
        trash = sb("trash", [P, 1])
        node0 = sb("node0", [P, NT])
        ones = sb("ones", [P, P])
        headmask = sb("headmask", [P, P])
        zero_bf = sb("zero_bf", [P, D], BF16)
        raw_i = sb("raw_i", [P, ET], I32)
        src_pm = sb("src_pm", [P, ET])
        src_t = sb("src_t", [P, ET], I32)
        dst_t = sb("dst_t", [P, ET])
        dst_r = sb("dst_r", [P, ET])
        dst_b = sb("dst_b", [P, ET])
        attr = sb("attr", [P, 2, 8, EF])
        src_st = sb("src_st", [P, CH])
        idx_st = sb("idx_st", [P, CH], I32)
        eq = sb("eq", [P, 2, 4, P])
        dup = sb("dup", [P, 4, P])
        cnt = sb("cnt", [P, CH])
        shift = sb("shift", [P, 8])
        sums = sb("sums", [P, 2, 8, EF])
        oh_r = sb("oh_r", [P, CH, P], BF16)
        oh_b = sb("oh_b", [P, CH, NT], BF16)
        deg = sb("deg", [P, NT])
        dinv = sb("dinv", [P, NT])
        cum = sb("cum", [P, NT])
        cum_f = sb("cum_f", [P, NT])
        cum_i = sb("cum_i", [P, NT], I32)
        qtab = sb("qtab", [1, NT + 1], I32)
        qlast = sb("qlast", [1, NT])
        nb = sb("nb", [1, QUADS])
        needtab = sb("needtab", [1, QUADS], I32)
        ring = sb("ring", [P, 4 * RQ, D])
        ringf = ring[:].rearrange("p s d -> p (s d)")
        bw = BG * D
        part4 = ringf[:, 0:bw].rearrange("p (r n f) -> p r n f", r=NTAB, n=BG)
        xT_g = ringf[:, bw:2 * bw].rearrange("p (n k r) -> p n k r", n=BG, k=KD)
        g_out = ringf[:, 2 * bw:3 * bw].rearrange("p (n d) -> p n d", n=BG)
        b_out = ringf[:, 3 * bw:4 * bw].rearrange("p (n d) -> p n d", n=BG)
        o = TROWS // P * EF
        edge_in = [ringf[0:TC, o + n * 8 * P:o + (n + 1) * 8 * P].bitcast(I32).rearrange("r (c q) -> r c q", c=8)
                   for n in range(2)]
        edge_f = ringf[0:TC, o + 16 * P:o + 18 * P].rearrange("r (s q) -> r s q", s=2)
        gidx = sb("gidx", [P, 2, 16], I32)
        arena = sb("arena", [P, NEXP * KH * D])
        o = 0
        w_kv = arena[:, o:o + KD * 512].rearrange("p (k n) -> p k n", k=KD); o += KD * 512
        w_q = arena[:, o:o + KD * D].rearrange("p (k n) -> p k n", k=KD); o += KD * D
        w_o = arena[:, o:o + KD * D].rearrange("p (k n) -> p k n", k=KD); o += KD * D
        w_1 = arena[:, o:o + KD * FF].rearrange("p (k n) -> p k n", k=KD); o += KD * FF
        w_2 = arena[:, o:o + KF * D].rearrange("p (k n) -> p k n", k=KF); o += KF * D
        f_2 = arena[:].rearrange("p (e k n) -> p e k n", e=NEXP, k=KH)
        f_1 = sb("f_1", [P, NEXP, KD, HID])
        w_cr = sb("w_cr", [P, 3, 512])
        w_e = sb("w_e", [EF, P])
        w_g = sb("w_g", [P, KD, NEXP])
        bc = {n: sb("bc_" + n, [P, D]) for n in ("bk", "bv", "bo", "b2", "g1", "c1", "g2", "c2", "bc", "br")}
        bg_bc = sb("bg_bc", [P, NEXP])
        bq_c = sb("bq_c", [P, KD])
        b1_c = sb("b1_c", [P, KF])
        be_c = sb("be_c", [P, 1])
        fb1_c = sb("fb1_c", [P, NEXP * KH])
        fb2 = sb("fb2", [NEXP, D])
        xg = sb("xg", [P, GRP, D])
        xng = sb("xng", [P, GRP, D])
        xT_st = sb("xT_st", [P, GRP, KD, P])
        kb = sb("kb", [P, 2, D])
        ke = sb("ke", [P, 2, D])
        va = sb("va", [P, 2, KD, P + 1])
        kv_acc = sb("kv_acc", [P, KD, P + 1])
        kv_bd = sb("kv_bd", [P, KD, P])
        ks_bd = sb("ks_bd", [P, KD, P])
        xT2 = sb("xT2", [P, KD, P])
        xn2 = sb("xn2", [P, D])
        x2 = sb("x2", [P, D])
        qm = sb("qm", [P, KD, P])
        qp = sb("qp", [P, KD, P])
        on = sb("on", [P, KD, P])
        y1 = sb("y1", [P, D])
        y1T = sb("y1T", [P, KD, P])
        hT = sb("hT", [P, KF, P])
        zt = sb("zt", [P, D])
        mixo = sb("mixo", [P, D])
        part = sb("part", [P, BG, P])
        partT = sb("partT", [P, P])
        e1 = sb("e1", [P, P])
        eT = sb("eT", [P, P])
        stats = sb("stats", [P, GRP, 6])
        mv = sb("mv", [P, GRP, 2])
        rs = sb("rs", [P, 4, NT])
        rs_i = sb("rs_i", [P, NT], I32)
        oh = sb("oh", [P, 4, P])
        acc, outb, xl = xg[:, 0:2], xg[:, 2], xg[:, 3]
        score = sb("score", [P, NEXP])
        top = sb("top", [P, 8])
        topi = sb("topi", [P, 8], U32)
        topf = sb("topf", [P, 8])
        mask = sb("mask", [P, NEXP])
        mask1 = sb("mask1", [P, NEXP])
        maskT = sb("maskT", [NEXP, P])

        ps0, ps1, ps2, ps3, ps4, ps5, ps6, ps7 = [bank(f"ps{i}") for i in range(8)]
        psT = [ps0, ps1]

        loaded, const_ready, idents, edges_in, edge_rows, edge_ps, edge_cols = (
            sem(n) for n in ("loaded", "const_ready", "idents", "edges_in", "edge_rows", "edge_ps", "edge_cols"))
        zeros_ready, tables_zero = sem("zeros_ready"), sem("tables_zero")
        attr_in = [sem(f"attr_in{h}") for h in range(2)]
        src_staged, src_bc, eq_ready, seg_summed, sums_ready, idx_ready = (
            sem(n) for n in ("src_staged", "src_bc", "eq_ready", "seg_summed", "sums_ready", "idx_ready"))
        scat = [sem(f"scat{r}") for r in range(NTAB)]
        oh_ready, deg_mm, deg_added = sem("oh_ready"), sem("deg_mm"), sem("deg_added")
        x_in, xn_ready, xT_ps, xT_ready, xn_out, xnT_out = (
            sem(n) for n in ("x_in", "xn_ready", "xT_ps", "xT_ready", "xn_out", "xnT_out"))
        kv_proj, kmin_ready, kexp_ready, phi_ready, kv_mm, kv_added, bd_ready = (
            sem(n) for n in ("kv_proj", "kmin_ready", "kexp_ready", "phi_ready", "kv_mm", "kv_added", "bd_ready"))
        xT2_in, xn2_in, x2_in, q_mm, qp_ready, qm_ready, qe_ready, qphi_ready = (
            sem(n) for n in ("xT2_in", "xn2_in", "x2_in", "q_mm", "qp_ready", "qm_ready", "qe_ready", "qphi_ready"))
        nd_mm, o_ready, o_mm, y1_ready, y1T_ps, y1T_ready, h_mm, relu_ready, z_mm, mix_ready, mix_out = (
            sem(n) for n in ("nd_mm", "o_ready", "o_mm", "y1_ready", "y1T_ps", "y1T_ready", "h_mm",
                             "relu_ready", "z_mm", "mix_ready", "mix_out"))
        dinv_ready, count_mm, tab_ready = sem("dinv_ready"), sem("count_mm"), sem("tab_ready")
        part_in, xTg_in, part_ready, pT_ps, pT_ready, e_mm, e_ready, eT_ready, c_mm, gb_ready, g_out_s, b_out_s = (
            sem(n) for n in ("part_in", "xTg_in", "part_ready", "pT_ps", "pT_ready", "e_mm", "e_ready",
                             "eT_ready", "c_mm", "gb_ready", "g_stored", "base_stored"))
        f2_in = sem("f2_in")
        gat = [sem(f"gat{j}") for j in range(4)]
        gidx_ready, pool_mark = sem("gidx_ready"), sem("pool_mark")
        dstl_ready, oneh_ready, agg_half, agg_done, agg_read = (
            sem(n) for n in ("dstl_ready", "oneh_ready", "agg_half", "agg_done", "agg_read"))
        base_in, mixr_in, xl_ready, xlT_ps, xlT_ready, gate_mm, mask_ready, maskT_ps, maskT_ready, bias_mm = (
            sem(n) for n in ("base_in", "mixr_in", "xl_ready", "xlT_ps", "xlT_ready", "gate_mm",
                             "mask_ready", "maskT_ps", "maskT_ready", "bias_mm"))
        eh_mm, gelu_ready, ey_mm, comb_done, out_ready, stored = (
            sem(n) for n in ("eh_mm", "gelu_ready", "ey_mm", "comb_done", "out_ready", "stored"))

        attr_pm = A["edge_attr_64"].rearrange("(p t) f -> p t f", p=P)
        block = ctx.enter_context(nc.Block())

        @block.sync
        def _(sp):
            n = [0]

            def load(dst, src):
                sp.dma_start(dst, src).then_inc(loaded, 16)
                n[0] += 16

            sp.dma_start(raw_i[:], A["src"].rearrange("(p t) -> p t", p=P)).then_inc(edges_in, 16)
            for n_, name in enumerate(("dst", "src")):
                sp.dma_start(edge_in[n_], A[name].rearrange("(c r q) -> r c q", c=8, q=P)).then_inc(edges_in, 16)
            load(w_kv[:, :, 0:D], A["L0_mix_Wk"].rearrange("(k p) n -> p k n", p=P))
            load(w_kv[:, :, D:], A["L0_mix_Wv"].rearrange("(k p) n -> p k n", p=P))
            load(w_q, A["L0_mix_Wq"].rearrange("(k p) n -> p k n", p=P))
            load(w_o, A["L0_mix_Wo"].rearrange("(k p) n -> p k n", p=P))
            load(w_1, A["L0_mix_W1"].rearrange("(k p) n -> p k n", p=P))
            load(w_2, A["L0_mix_W2"].rearrange("(k p) n -> p k n", p=P))
            load(w_cr[:, :, 0:D], A["L0_gnn_W_conv"].rearrange("(k p) n -> p k n", p=P))
            load(w_cr[:, :, D:], A["L0_gnn_W_res"].rearrange("(k p) n -> p k n", p=P))
            load(w_e[:], A["L0_gnn_W_edge"])
            load(w_g[:], A["L0_ffn_Wg"].rearrange("(k p) n -> p k n", p=P))
            for b, name in (("bk", "L0_mix_bk"), ("bv", "L0_mix_bv"), ("bo", "L0_mix_bo"), ("b2", "L0_mix_b2"),
                            ("g1", "L0_mix_ln1_g"), ("c1", "L0_mix_ln1_b"), ("g2", "L0_mix_ln2_g"),
                            ("c2", "L0_mix_ln2_b"), ("bc", "L0_gnn_b_conv"), ("br", "L0_gnn_b_res")):
                load(bc[b][:], A[name].unsqueeze(0).to_broadcast([P, D]))
            load(bg_bc[:], A["L0_ffn_bg"].unsqueeze(0).to_broadcast([P, NEXP]))
            with nc.allow_non_contiguous_dma(reason="small bias columns"):
                load(bq_c[:], A["L0_mix_bq"].rearrange("(k p) -> p k", p=P))
                load(b1_c[:], A["L0_mix_b1"].rearrange("(k p) -> p k", p=P))
                load(be_c[:], A["L0_gnn_b_edge"].rearrange("(p k) -> p k", k=1))
                load(fb1_c[:], A["L0_ffn_b1"].rearrange("e (k p) -> p (e k)", p=P))
            load(fb2[:], A["L0_ffn_b2"])
            assert n[0] == LOADS
            sp.wait_ge(zeros_ready, 1)
            for t in table:
                sp.dma_start(t.rearrange("(p n) f -> p (n f)", p=P), ringf[:, 0:TROWS // P * EF]).then_inc(tables_zero, 16)
            for e in range(NEXP):
                sp.dma_start(f_1[:, e], A["L0_ffn_W1"][e].rearrange("(k p) h -> p k h", p=P)).then_inc(f2_in, 16)

            def chunk_loads(i):
                for h in range(2):
                    wait(sp, seg_summed, 4 * i - 4 + 2 * h + 2)
                    sp.dma_start(attr[:, h], attr_pm[:, bass.ds(i * CH + 8 * h, 8), :]).then_inc(attr_in[h], 16)

            def pass1_loads(i, tiles):
                wait(sp, xn_ready, i)
                sp.dma_start(xg[:, 0:tiles] if tiles > 1 else xg[:, 0, :],
                             rows(A["x"], i * GRP, tiles)).then_inc(x_in, 16)

            def pass2_loads(b):
                wait(sp, q_mm, b)
                sp.dma_start(xT2[:].rearrange("p k r -> p (k r)"), rows(xnT_d, b)).then_inc(xT2_in, 16)
                wait(sp, y1_ready, b)
                sp.dma_start(xn2[:], rows(xn_d, b)).then_inc(xn2_in, 16)
                wait(sp, mix_ready, b)
                sp.dma_start(x2[:], rows(A["x"], b)).then_inc(x2_in, 16)

            chunk_loads(0)
            pass1_loads(0, GRP)
            with sp.Fori(1, NG) as i:
                chunk_loads(i)
                pass1_loads(i, GRP)
            pass1_loads(NG, 1)
            sp.wait_ge(xn_out, 16 * (NG + 1))
            sp.wait_ge(xnT_out, 16 * (NG + 1))
            chunk_loads(NG)
            pass2_loads(0)
            with sp.Fori(NG + 1, NCH) as i:
                chunk_loads(i)
                pass2_loads(i - NG)
            with sp.Fori(NCH - NG, NT) as b:
                pass2_loads(b)
            sp.wait_ge(z_mm, NT)
            for e in range(NEXP):
                sp.dma_start(f_2[:, e], A["L0_ffn_W2"][e].rearrange("(k p) n -> p k n", p=P)).then_inc(f2_in, 16)
            for s in scat:
                sp.wait_ge(s, 16 * ET // NTAB)

            def gcn_loads(i):
                wait(sp, part_ready, i)
                for r in range(NTAB):
                    sp.dma_start(part4[:, r], rows(table[r], i * BG, BG)).then_inc(part_in, 16)
                wait(sp, c_mm, BG * i)
                sp.dma_start(xT_g.rearrange("p n k r -> p n (k r)"), rows(xnT_d, i * BG, BG)).then_inc(xTg_in, 16)

            gcn_loads(0)
            with sp.Fori(1, NT // BG) as i:
                gcn_loads(i)

        @block.gpsimd
        def _(pool):
            g = nc.gpsimd
            g.memset(ones[:], 1.0).then_inc(idents, 1)
            g.memset(zero_bf[:], 0.0).then_inc(idents, 1)
            g.iota(raw_iota[:], pattern=[[1, P]], base=0, channel_multiplier=0).then_inc(idents, 1)
            g.iota(raw_iotb[:], pattern=[[P, NT]], base=0, channel_multiplier=0).then_inc(idents, 1)
            g.iota(raw_iotq[:], pattern=[[1, QUADS]], base=0, channel_multiplier=0).then_inc(idents, 1)
            g.iota(raw_iotp[:], pattern=[[0, 1]], base=NP, channel_multiplier=1).then_inc(idents, 1)
            pool.wait_ge(idents, 6)
            g.affine_select(out=before[:], in_=ones[:], compare_op=ALU.is_gt, fill=0.0, base=0,
                            pattern=[[-1, P]], channel_multiplier=1).then_inc(idents, 1)
            g.affine_select(out=ident[:], in_=ones[:], compare_op=ALU.is_equal, fill=0.0, base=0,
                            pattern=[[-1, P]], channel_multiplier=1).then_inc(idents, 1)

            def alone(s, value):
                if isinstance(value, int):
                    return wait(pool, s, value)
                pool.wait_ge(s, value)
                pool.sem_inc(pool_mark, 1)

            def scatter_chunk(i):
                for h in range(2):
                    alone(idx_ready, 2 * i + h + 1)
                    for j in range(8):
                        if j % 4 == 0:
                            alone(sums_ready, 4 * i + 2 * h + j // 4 + 1)
                        alone(scat[j % NTAB], 16 * (4 * i + 2 * h + j // 4))
                        g.indirect_dma_start(
                            out=table[j % NTAB],
                            out_offset=bass.IndirectOffsetOnAxis(ap=idx_st[:, 8 * h + j:8 * h + j + 1], axis=0),
                            in_=sums[:, h, j, :], in_offset=None, bounds_check=TROWS - 1,
                            compute_op=ALU.add).then_inc(scat[j % NTAB], 16)

            pool.wait_ge(tables_zero, 16 * NTAB)
            scatter_chunk(0)
            with pool.Fori(1, NCH) as i:
                scatter_chunk(i)

            pool.wait_ge(tab_ready, 1)
            pool.wait_ge(g_out_s, 16 * (NT // BG))
            pool.wait_ge(b_out_s, 16 * (NT // BG))

            def gather(i):
                for h in range(2):
                    for jj in range(4):
                        alone(gat[jj], 16 * (RQ * i - RQ + 4 * h + 4))
                    g.tensor_copy(gidx[:, h], src_t[:, bass.ds(i * 4 * RQ + 16 * h, 16)]).then_inc(gidx_ready, 1)
                    alone(gidx_ready, 2 * i + h + 1)
                    for k in range(4 * h, 4 * h + 4):
                        q = RQ * i + k
                        if not isinstance(i, int):
                            alone(agg_half, pool.value_load(needtab[0:1, bass.ds(q, 1)], min_val=2, max_val=2 * (QUADS + NT) + 2))
                        for jj in range(4):
                            alone(gat[jj], 16 * q)
                            s = 4 * (k - 4 * h) + jj
                            g.indirect_dma_start(
                                out=ring[:, 4 * k + jj, :], out_offset=None, in_=g_d,
                                in_offset=bass.IndirectOffsetOnAxis(ap=gidx[:, h, s:s + 1], axis=0),
                            ).then_inc(gat[jj], 16)

            gather(0)
            with pool.Fori(1, QUADS // RQ) as i:
                gather(i)

        @block.tensor
        def _(pe):
            T = nc.tensor

            def mm(o, l, r, first, last):
                return T.matmul(o, l, r, start=first, stop=last)

            pe.wait_ge(loaded, LOADS)
            pe.wait_ge(idents, 8)
            for t in range(2):
                for c in range(8):
                    k = 8 * t + c
                    wait(pe, edge_cols, k - 1)
                    pe.wait_ge(edge_rows, k + 1)
                    T.transpose(psT[k % 2][:, 0:TC], edge_f[:, k % 2, :], ident[0:TC, 0:TC]).then_inc(edge_ps, 1)

            def src_rows(i, k):
                wait(pe, src_staged, i + 1)
                wait(pe, eq_ready, 4 * i + k - 1)
                for j in range(4):
                    ins = T.transpose(psT[k % 2][:, j * P:(j + 1) * P],
                                      src_st[:, 4 * k + j:4 * k + j + 1].to_broadcast([P, P]), ident[:])
                ins.then_inc(src_bc, 1)

            def seg_sum(i, k):
                if k % 2 == 0:
                    wait(pe, attr_in[k // 2], 16 * (i + 1))
                wait(pe, eq_ready, 4 * i + k + 1)
                wait(pe, sums_ready, 4 * i + k)
                for j in range(4):
                    ins = mm(ps2[:, j * EF:(j + 1) * EF], eq[:, k % 2, j, :],
                             attr[:, k // 2, 4 * (k % 2) + j, :], True, True)
                ins.then_inc(seg_summed, 1)

            def chunk(i):
                src_rows(i, 0)
                wait(pe, oh_ready, i + 1)
                wait(pe, deg_added, i)
                for t in range(CH):
                    ins = mm(ps5[:, 0:NT], oh_r[:, t, :], oh_b[:, t, :], t == 0, t == CH - 1)
                ins.then_inc(deg_mm, 1)
                for k in range(4):
                    if k < 3:
                        src_rows(i, k + 1)
                    seg_sum(i, k)

            def pass1(i, tiles):
                def turn(j):
                    wait(pe, xT_ready, GRP * i + j - 1)
                    for k in range(KD):
                        ins = T.transpose([ps6, ps7][j % 2][:, k * P:(k + 1) * P],
                                          xng[:, j, k * P:(k + 1) * P], ident[:])
                    ins.then_inc(xT_ps, 1)

                def project(j):
                    wait(pe, xT_ready, GRP * i + j + 1)
                    wait(pe, kmin_ready, GRP * i + j)
                    for k in range(KD):
                        ins = mm(ps3[:, 0:512], xT_st[:, j, k, :], w_kv[:, k, :], k == 0, k == KD - 1)
                    ins.then_inc(kv_proj, 1)

                def kv(j):
                    n = P if tiles > 1 else LAST
                    wait(pe, phi_ready, GRP * i + j + 1)
                    wait(pe, kv_added, GRP * i + j)
                    for c in range(KD):
                        ins = mm(ps4[:, c * (P + 1):(c + 1) * (P + 1)], kb[0:n, j % 2, c * P:(c + 1) * P],
                                 va[0:n, j % 2, c, :], True, True)
                    ins.then_inc(kv_mm, 1)

                wait(pe, xn_ready, i + 1)
                turn(0)
                for j in range(tiles):
                    if j + 1 < tiles:
                        turn(j + 1)
                    project(j)
                    if j:
                        kv(j - 1)
                kv(tiles - 1)

            def pass2(b):
                wait(pe, xT2_in, 16 * (b + 1))
                for m in range(KD):
                    for k in range(KD):
                        ins = mm(ps3[:, m * P:(m + 1) * P], w_q[:, k, m * P:(m + 1) * P], xT2[:, k, :], k == 0, k == KD - 1)
                ins.then_inc(q_mm, 1)
                wait(pe, qphi_ready, b + 1)
                for m in range(KD):
                    mm(ps4[:, m * P:(m + 1) * P], kv_bd[:, m, :], qp[:, m, :], True, True)
                    ins = mm(ps4[:, D + m * P:D + (m + 1) * P], ks_bd[:, m, :], qp[:, m, :], True, True)
                ins.then_inc(nd_mm, 1)
                wait(pe, o_ready, b + 1)
                for k in range(KD):
                    ins = mm(ps3[:, D:2 * D], on[:, k, :], w_o[:, k, :], k == 0, k == KD - 1)
                ins.then_inc(o_mm, 1)
                wait(pe, y1_ready, b + 1)
                for k in range(KD):
                    ins = T.transpose(ps4[:, k * P:(k + 1) * P], y1[:, k * P:(k + 1) * P], ident[:])
                ins.then_inc(y1T_ps, 1)
                wait(pe, y1T_ready, b + 1)
                for m in range(KF):
                    for k in range(KD):
                        ins = mm([ps6, ps7][m // 4][:, (m % 4) * P:(m % 4 + 1) * P], w_1[:, k, m * P:(m + 1) * P],
                                 y1T[:, k, :], k == 0, k == KD - 1)
                    if m % 4 == 3:
                        ins.then_inc(h_mm, 1)
                for m in range(KF):
                    if m % 4 == 0:
                        wait(pe, relu_ready, 2 * b + m // 4 + 1)
                    ins = mm(ps4[:, D:2 * D], hT[:, m, :], w_2[:, m, :], m == 0, m == KF - 1)
                ins.then_inc(z_mm, 1)

            chunk(0)
            pass1(0, GRP)
            with pe.Fori(1, NG) as i:
                chunk(i)
                pass1(i, GRP)
            pass1(NG, 1)
            pe.wait_ge(bd_ready, 1)
            chunk(NG)
            pass2(0)
            with pe.Fori(NG + 1, NCH) as i:
                chunk(i)
                pass2(i - NG)
            with pe.Fori(NCH - NG, NT) as b:
                pass2(b)

            pe.wait_ge(deg_added, NCH)
            mm(ps5[:, 0:NT], ones[:], deg[:], True, True).then_inc(count_mm, 1)

            def gcn(i):
                def turn(j):
                    wait(pe, pT_ready, BG * i + j)
                    T.transpose(ps5[:, 0:P], part[:, j, :], ident[:]).then_inc(pT_ps, 1)

                wait(pe, part_ready, i + 1)
                wait(pe, xTg_in, 16 * (i + 1))
                for j in range(BG):
                    t = BG * i + j
                    turn(j)
                    wait(pe, gb_ready, t)
                    for k in range(KD):
                        mm(ps6[:], xT_g[:, j, k, :], w_cr[:, k, :], k == 0, False)
                    wait(pe, pT_ready, t + 1)
                    mm(ps4[:, 0:P], w_e[:], partT[0:EF, :], True, True).then_inc(e_mm, 1)
                    wait(pe, eT_ready, t + 1)
                    mm(ps6[:], eT[:], w_cr[:, KD, :], False, True).then_inc(c_mm, 1)

            pe.wait_ge(tab_ready, 1)
            gcn(0)
            with pe.Fori(1, NT // BG) as i:
                gcn(i)

            pe.wait_ge(f2_in, 16 * 2 * NEXP)
            pe.sem_inc(agg_half, 2)

            def aggregate(b):
                lo = pe.value_load(qtab[0:1, bass.ds(b, 1)], min_val=0, max_val=QUADS - 1)
                hi = pe.value_load(qtab[0:1, bass.ds(b + 1, 1)], min_val=0, max_val=QUADS - 1)
                wait(pe, agg_read, b)
                mm(ps0[:, 0:D], zero_bf[:, 0:P], zero_bf[:], True, False)
                with pe.Fori(lo, hi + 1) as q:
                    for h in range(2):
                        pe.wait_ge(oneh_ready, (q + b) * 2 + h + 1)
                        for jj in (2 * h, 2 * h + 1):
                            pe.wait_ge(gat[jj], q * 16 + 16)
                            ins = mm(ps0[:, 0:D], oh[:, jj, :], ringf[:, bass.ds((q % RQ) * (4 * D) + jj * D, D)],
                                     False, False)
                        ins.then_inc(agg_half, 1)
                mm(ps0[:, 0:D], zero_bf[:, 0:P], zero_bf[:], False, True).then_inc(agg_done, 1)

            def experts(b):
                wait(pe, xl_ready, b + 1)
                for k in range(KD):
                    ins = T.transpose(ps2[:, k * P:(k + 1) * P], xl[:, k * P:(k + 1) * P], ident[:])
                ins.then_inc(xlT_ps, 1)
                wait(pe, xlT_ready, b + 1)
                for k in range(KD):
                    ins = mm(ps2[:, 384:384 + NEXP], xT2[:, k, :], w_g[:, k, :], k == 0, k == KD - 1)
                ins.then_inc(gate_mm, 1)

                def up(e):
                    for m in range(KH):
                        for k in range(KD):
                            ins = mm([ps6, ps7][e % 2][:, m * P:(m + 1) * P], f_1[:, e, k, m * P:(m + 1) * P],
                                     xT2[:, k, :], k == 0, k == KD - 1)
                    ins.then_inc(eh_mm, 1)

                def down(e):
                    wait(pe, gelu_ready, NEXP * b + e + 1)
                    wait(pe, comb_done, NEXP * b + e - 1)
                    for m in range(KH):
                        ins = mm([ps3, ps4][e % 2][:, 0:D], hT[:, (e % 2) * KH + m, :], f_2[:, e, m, :], m == 0, m == KH - 1)
                    ins.then_inc(ey_mm, 1)

                up(0)
                up(1)
                wait(pe, mask_ready, b + 1)
                T.transpose(ps2[0:NEXP, D:D + P], mask[:], ident[:]).then_inc(maskT_ps, 1)
                for e in range(NEXP):
                    down(e)
                    if e + 2 < NEXP:
                        up(e + 2)
                    if e == 0:
                        wait(pe, maskT_ready, b + 1)
                        wait(pe, out_ready, b)
                        mm(ps5[:, 0:D], maskT[:], fb2[:], True, True).then_inc(bias_mm, 1)

            aggregate(0)
            aggregate(1)
            experts(0)
            with pe.Fori(1, NT - 1) as b:
                aggregate(b + 1)
                experts(b)
            experts(NT - 1)

        @block.scalar
        def _(act):
            S = nc.scalar
            act.wait_ge(loaded, LOADS)
            act.wait_ge(const_ready, 1)

            def chunk(i):
                for k in range(4):
                    if k % 2 == 0:
                        h = k // 2
                        for s in scat:
                            wait(act, s, 16 * (4 * i - 4 + 2 * h + 2))
                    wait(act, seg_summed, 4 * i + k + 1)
                    S.copy(sums[:, k // 2, 4 * (k % 2):4 * (k % 2) + 4, :],
                           ps2[:, 0:4 * EF].rearrange("p (j f) -> p j f", j=4)).then_inc(sums_ready, 1)

            def pass1(i, tiles):
                def turned(j):
                    if j == 0:
                        wait(act, xnT_out, 16 * i)
                    wait(act, xT_ps, GRP * i + j + 1)
                    S.copy(xT_st[:, j].rearrange("p k r -> p (k r)"), [ps6, ps7][j % 2][:, 0:D]).then_inc(xT_ready, 1)

                turned(0)
                for j in range(tiles):
                    if j + 1 < tiles:
                        turned(j + 1)
                    wait(act, kmin_ready, GRP * i + j + 1)
                    S.activation(ke[:, j % 2, :], ke[:, j % 2, :], ACT.Exp).then_inc(kexp_ready, 1)
                wait(act, xT_ready, GRP * i + tiles)
                act.dma_start(rows(xn_d, i * GRP, tiles), xng[:, 0:tiles] if tiles > 1 else xng[:, 0, :]).then_inc(xn_out, 16)
                act.dma_start(rows(xnT_d, i * GRP, tiles),
                              xT_st[:].rearrange("p n k r -> p n (k r)") if tiles > 1
                              else xT_st[:, 0].rearrange("p k r -> p (k r)")).then_inc(xnT_out, 16)

            def pass2(b):
                wait(act, qm_ready, b + 1)
                for m in range(KD):
                    ins = S.activation(qp[:, m, :], ps3[:, m * P:(m + 1) * P], ACT.Relu, bias=bq_c[:, m:m + 1])
                ins.then_inc(qp_ready, 1)
                S.activation(qm[:], qm[:], ACT.Exp).then_inc(qe_ready, 1)
                wait(act, y1T_ps, b + 1)
                S.copy(y1T[:].rearrange("p k r -> p (k r)"), ps4[:, 0:D]).then_inc(y1T_ready, 1)
                for m in range(KF):
                    if m % 4 == 0:
                        wait(act, h_mm, 2 * b + m // 4 + 1)
                    ins = S.activation(hT[:, m, :], [ps6, ps7][m // 4][:, (m % 4) * P:(m % 4 + 1) * P], ACT.Relu,
                                       bias=b1_c[:, m:m + 1])
                    if m % 4 == 3:
                        ins.then_inc(relu_ready, 1)
                wait(act, mix_ready, b + 1)
                act.dma_start(rows(mix_d, b), mixo[:]).then_inc(mix_out, 16)

            chunk(0)
            pass1(0, GRP)
            with act.Fori(1, NG) as i:
                chunk(i)
                pass1(i, GRP)
            pass1(NG, 1)
            chunk(NG)
            pass2(0)
            with act.Fori(NG + 1, NCH) as i:
                chunk(i)
                pass2(i - NG)
            with act.Fori(NCH - NG, NT) as b:
                pass2(b)

            def gcn(i):
                for j in range(BG):
                    t = BG * i + j
                    wait(act, pT_ps, t + 1)
                    S.copy(partT[:], ps5[:, 0:P]).then_inc(pT_ready, 1)
                    wait(act, e_mm, t + 1)
                    S.activation(e1[:], ps4[:, 0:P], ACT.Identity, bias=be_c[:, 0:1]).then_inc(e_ready, 1)
                wait(act, gb_ready, BG * i + BG)
                act.dma_start(rows(g_d, i * BG, BG), g_out).then_inc(g_out_s, 16)
                act.dma_start(rows(base_d, i * BG, BG), b_out).then_inc(b_out_s, 16)

            gcn(0)
            with act.Fori(1, NT // BG) as i:
                gcn(i)

            act.wait_ge(mix_out, 16 * NT)
            act.wait_ge(b_out_s, 16 * (NT // BG))

            def tile_loads(b):
                act.dma_start(xn2[:], rows(base_d, b)).then_inc(base_in, 16)
                act.dma_start(x2[:], rows(mix_d, b)).then_inc(mixr_in, 16)

            def experts(b, more=True):
                wait(act, xl_ready, b + 1)
                if more:
                    tile_loads(b + 1)
                wait(act, xlT_ps, b + 1)
                S.copy(xT2[:].rearrange("p k r -> p (k r)"), ps2[:, 0:D]).then_inc(xlT_ready, 1)

                def gelu(e):
                    wait(act, eh_mm, NEXP * b + e + 1)
                    wait(act, ey_mm, NEXP * b + e - 1)
                    for m in range(KH):
                        ins = S.activation(hT[:, (e % 2) * KH + m, :], [ps6, ps7][e % 2][:, m * P:(m + 1) * P], ACT.Gelu,
                                           bias=fb1_c[:, e * KH + m:e * KH + m + 1])
                    ins.then_inc(gelu_ready, 1)

                gelu(0)
                wait(act, maskT_ps, b + 1)
                S.copy(maskT[:], ps2[0:NEXP, D:D + P]).then_inc(maskT_ready, 1)
                for e in range(1, NEXP):
                    gelu(e)
                wait(act, out_ready, b + 1)
                act.dma_start(rows(out, b), outb).then_inc(stored, 16)

            tile_loads(0)
            experts(0)
            with act.Fori(1, NT - 1) as b:
                experts(b)
            experts(NT - 1, more=False)
            act.wait_ge(stored, 16 * NT)

        @block.vector
        def _(dve):
            V = nc.vector

            def rsqrt(result, v, n, eps):
                a, y, t = rs[:, 0, 0:n], rs[:, 1, 0:n], rs[:, 2, 0:n]
                half = rs_i[:, 0:n]
                V.tensor_scalar(a, v, float(eps), None, ALU.add)
                dve.drain()
                V.tensor_single_scalar(half, a.bitcast(I32), 1, op=ALU.arith_shift_right)
                V.tensor_scalar(a, a, -0.5, None, ALU.mult)
                dve.drain()
                V.tensor_scalar(y.bitcast(I32), half, -1.0, float(0x5F3759DF), ALU.mult, ALU.add)
                dve.drain()
                for step in range(4):
                    V.tensor_tensor(t, y, y, ALU.mult)
                    dve.drain()
                    V.tensor_tensor(t, t, a, ALU.mult)
                    dve.drain()
                    V.scalar_tensor_tensor(out=result if step == 3 else y, in0=t, scalar=1.5, in1=y,
                                           op0=ALU.add, op1=ALU.mult)
                    dve.drain()

            def normalise(dst, src):
                V.bn_stats(stats[:, 0, :], src)
                dve.drain()
                V.bn_aggr(mv[:, 0, :], stats[:, 0, :])
                dve.drain()
                rsqrt(rs[:, 3, 0:1], mv[:, 0, 1:2], 1, LN_EPS)
                return V.tensor_scalar(dst, src, mv[:, 0, 0:1], rs[:, 3, 0:1], ALU.subtract, ALU.mult)

            dve.wait_ge(idents, 8)
            V.memset(ringf[:, 0:TROWS // P * EF], 0.0).then_inc(zeros_ready, 1)
            V.memset(headmask[:], 0.0)
            dve.drain()
            for h in range(P // HEAD):
                s = slice(HEAD * h, HEAD * h + HEAD)
                V.memset(headmask[s, s], 1.0)
            V.tensor_copy(iota_r[:], raw_iota[:])
            V.tensor_copy(node0[:], raw_iotb[:])
            V.tensor_copy(iota_q[:], raw_iotq[:])
            V.tensor_copy(trash[:], raw_iotp[:])
            V.tensor_copy(iota_b[:], raw_iota[:, 0:NT])
            V.memset(deg[:], 0.0)
            V.memset(kv_acc[:], 0.0)
            V.memset(part[:], 0.0)
            V.memset(va[:], 1.0)
            V.memset(qtab[:], 0)
            dve.wait_ge(loaded, LOADS)
            V.tensor_tensor(bc["bc"][:], bc["bc"][:], bc["br"][:], ALU.add)
            dve.drain()
            V.engine_nop().then_inc(const_ready, 1)
            dve.wait_ge(edges_in, 48)
            V.tensor_copy(src_pm[:], raw_i[:])
            for t in range(2):
                for c in range(8):
                    k = 8 * t + c
                    wait(dve, edge_ps, k - 1)
                    V.tensor_copy(edge_f[:, k % 2, :], edge_in[t][:, c, :]).then_inc(edge_rows, 1)
                    dve.wait_ge(edge_ps, k + 1)
                    cols = slice(c * TC, (c + 1) * TC)
                    if t == 0:
                        V.tensor_copy(dst_t[:, cols], psT[k % 2][:, 0:TC]).then_inc(edge_cols, 1)
                    else:
                        V.tensor_scalar(src_t[:, cols], psT[k % 2][:, 0:TC], float(NP - 1), None,
                                        ALU.min).then_inc(edge_cols, 1)
            dve.drain()
            raw2 = raw_i[:]
            V.tensor_copy(raw2, dst_t[:])
            dve.drain()
            V.tensor_single_scalar(raw2, raw2, 7, op=ALU.arith_shift_right)
            dve.drain()
            V.tensor_copy(dst_b[:], raw2)
            dve.drain()
            V.scalar_tensor_tensor(out=dst_r[:], in0=dst_b[:], scalar=-float(P), in1=dst_t[:], op0=ALU.mult, op1=ALU.add)
            dve.drain()

            def chunk(i):
                c0 = i * CH
                V.tensor_copy(src_st[:], src_pm[:, bass.ds(c0, CH)]).then_inc(src_staged, 1)
                wait(dve, deg_mm, i)
                V.tensor_tensor(oh_r[:], iota_r[:].unsqueeze(1).to_broadcast([P, CH, P]),
                                dst_r[:, bass.ds(c0, CH)].unsqueeze(2).to_broadcast([P, CH, P]), ALU.is_equal)
                V.tensor_tensor(oh_b[:], iota_b[:].unsqueeze(1).to_broadcast([P, CH, NT]),
                                dst_b[:, bass.ds(c0, CH)].unsqueeze(2).to_broadcast([P, CH, NT]),
                                ALU.is_equal).then_inc(oh_ready, 1)
                for k in range(4):
                    wait(dve, src_bc, 4 * i + k + 1)
                    wait(dve, seg_summed, 4 * i + k - 1)
                    V.tensor_tensor(eq[:, k % 2], psT[k % 2][:].rearrange("p (j e) -> p j e", j=4),
                                    src_st[:, 4 * k:4 * k + 4].unsqueeze(2).to_broadcast([P, 4, P]),
                                    ALU.is_equal).then_inc(eq_ready, 1)
                    dve.drain()
                    V.tensor_tensor(dup[:], eq[:, k % 2], before[:].unsqueeze(1).to_broadcast([P, 4, P]), ALU.mult)
                    dve.drain()
                    V.tensor_reduce(cnt[:, 4 * k:4 * k + 4], dup[:], AX_X, ALU.add)
                    if k % 2:
                        h = k // 2
                        s = slice(8 * h, 8 * h + 8)
                        dve.drain()
                        V.tensor_scalar(shift[:], src_st[:, s], -1.0, trash[:, 0:1], ALU.mult, ALU.add)
                        V.tensor_scalar(cnt[:, s], cnt[:, s], 1.0, None, ALU.min)
                        dve.drain()
                        V.tensor_tensor(shift[:], shift[:], cnt[:, s], ALU.mult)
                        dve.drain()
                        for q in scat:
                            wait(dve, q, 16 * (4 * i - 4 + 2 * h + 2))
                        V.tensor_tensor(idx_st[:, s], src_st[:, s], shift[:], ALU.add).then_inc(idx_ready, 1)
                wait(dve, deg_mm, i + 1)
                V.tensor_tensor(deg[:], deg[:], ps5[:, 0:NT], ALU.add).then_inc(deg_added, 1)

            def pass1(i, tiles):
                wait(dve, x_in, 16 * (i + 1))
                for j in range(tiles):
                    V.bn_stats(stats[:, j, :], xg[:, j, :])
                dve.drain()
                for j in range(tiles):
                    V.bn_aggr(mv[:, j, :], stats[:, j, :])
                dve.drain()
                rsqrt(rs[:, 3, 0:tiles], mv[:, 0:tiles, 1], tiles, LN_EPS)
                wait(dve, xn_out, 16 * i)
                for j in range(tiles):
                    ins = V.tensor_scalar(xng[:, j, :], xg[:, j, :], mv[:, j, 0:1], rs[:, 3, j:j + 1], ALU.subtract, ALU.mult)
                ins.then_inc(xn_ready, 1)

                def front(j):
                    wait(dve, kv_proj, GRP * i + j + 1)
                    wait(dve, kv_mm, GRP * i + j - 1)
                    V.tensor_tensor(kb[:, j % 2], ps3[:, 0:D], bc["bk"][:], ALU.add)
                    V.tensor_tensor(va[:, j % 2, :, 0:P], ps3[:, D:].rearrange("p (c e) -> p c e", c=KD),
                                    bc["bv"][:].rearrange("p (c e) -> p c e", c=KD), ALU.add)
                    dve.drain()
                    V.tensor_scalar(ke[:, j % 2], kb[:, j % 2], 0.0, None, ALU.min).then_inc(kmin_ready, 1)

                def back(j):
                    wait(dve, kexp_ready, GRP * i + j + 1)
                    V.scalar_tensor_tensor(out=kb[:, j % 2], in0=kb[:, j % 2], scalar=0.0, in1=ke[:, j % 2],
                                           op0=ALU.max, op1=ALU.add).then_inc(phi_ready, 1)

                def add(j):
                    wait(dve, kv_mm, GRP * i + j + 1)
                    V.tensor_tensor(kv_acc[:], kv_acc[:], ps4[:, 0:KD * (P + 1)].rearrange("p (c e) -> p c e", c=KD),
                                    ALU.add).then_inc(kv_added, 1)

                front(0)
                for j in range(tiles):
                    back(j)
                    if j + 1 < tiles:
                        front(j + 1)
                    add(j)
                    dve.drain()

            def pass2(b):
                wait(dve, q_mm, b + 1)
                for m in range(KD):
                    ins = V.tensor_scalar(qm[:, m, :], ps3[:, m * P:(m + 1) * P], bq_c[:, m:m + 1], 0.0, ALU.add, ALU.min)
                ins.then_inc(qm_ready, 1)
                wait(dve, qe_ready, b + 1)
                wait(dve, qp_ready, b + 1)
                V.tensor_tensor(qp[:], qp[:], qm[:], ALU.add).then_inc(qphi_ready, 1)
                wait(dve, nd_mm, b + 1)
                den = qm[:].rearrange("p k r -> p (k r)")
                V.tensor_scalar(den, ps4[:, D:2 * D], 1e-6, None, ALU.add)
                dve.drain()
                V.reciprocal(den, den)
                wait(dve, xn2_in, 16 * (b + 1))
                V.tensor_tensor(xn2[:], xn2[:], bc["bo"][:], ALU.add)
                dve.drain()
                V.tensor_tensor(on[:].rearrange("p k r -> p (k r)"), ps4[:, 0:D], den, ALU.mult).then_inc(o_ready, 1)
                wait(dve, o_mm, b + 1)
                V.tensor_tensor(zt[:], ps3[:, D:2 * D], xn2[:], ALU.add)
                dve.drain()
                normalise(zt[:], zt[:])
                dve.drain()
                V.tensor_tensor(zt[:], zt[:], bc["g1"][:], ALU.mult)
                dve.drain()
                V.tensor_tensor(y1[:], zt[:], bc["c1"][:], ALU.add).then_inc(y1_ready, 1)
                dve.drain()
                V.tensor_tensor(zt[:], y1[:], bc["b2"][:], ALU.add)
                dve.drain()
                wait(dve, z_mm, b + 1)
                V.tensor_tensor(zt[:], ps4[:, D:2 * D], zt[:], ALU.add)
                dve.drain()
                normalise(zt[:], zt[:])
                dve.drain()
                V.tensor_tensor(zt[:], zt[:], bc["g2"][:], ALU.mult)
                wait(dve, x2_in, 16 * (b + 1))
                V.tensor_tensor(x2[:], x2[:], bc["c2"][:], ALU.add)
                dve.drain()
                wait(dve, mix_out, 16 * b)
                V.tensor_tensor(mixo[:], zt[:], x2[:], ALU.add).then_inc(mix_ready, 1)

            chunk(0)
            pass1(0, GRP)
            with dve.Fori(1, NG) as i:
                chunk(i)
                pass1(i, GRP)
            pass1(NG, 1)
            for c in range(KD):
                V.tensor_tensor(kv_bd[:, c, :], kv_acc[:, c, 0:P], headmask[:], ALU.mult)
                ins = V.tensor_scalar(ks_bd[:, c, :], headmask[:], kv_acc[:, c, P:P + 1], None, ALU.mult)
            ins.then_inc(bd_ready, 1)
            chunk(NG)
            pass2(0)
            with dve.Fori(NG + 1, NCH) as i:
                chunk(i)
                pass2(i - NG)
            with dve.Fori(NCH - NG, NT) as b:
                pass2(b)

            dve.drain()
            rsqrt(dinv[:], deg[:], NT, 1.0)
            dve.wait_ge(count_mm, 1)
            V.tensor_copy(cum_f[:], ps5[:, 0:NT])
            dve.drain()
            V.tensor_tensor_scan(cum[:], ones[:, 0:NT], cum_f[:], 0.0, ALU.mult, ALU.add)
            dve.drain()
            V.tensor_scalar(cum_i[:], cum[:], 1.0, -1.0, ALU.max, ALU.add)
            dve.drain()
            V.tensor_single_scalar(cum_i[:], cum_i[:], 9, op=ALU.arith_shift_right)
            dve.drain()
            V.tensor_copy(qtab[:, 1:NT + 1], cum_i[0:1, :])
            V.tensor_copy(qlast[:], cum_i[0:1, :])
            dve.drain()
            step = QUADS // 16
            wide = oh_r[0:1].rearrange("p t e -> p (t e)").bitcast(F32)[:, 0:step * NT].rearrange("p (q b) -> p q b", b=NT)
            for c in range(16):
                s = slice(c * step, (c + 1) * step)
                V.tensor_tensor(wide, iota_q[:, s].unsqueeze(2).to_broadcast([1, step, NT]),
                                qlast[:].unsqueeze(1).to_broadcast([1, step, NT]), ALU.is_gt)
                dve.drain()
                V.tensor_reduce(nb[:, s], wide, AX_X, ALU.add)
                dve.drain()
            V.tensor_tensor(nb[:], nb[:], iota_q[:], ALU.add)
            V.memset(needtab[:], 2)
            dve.drain()
            V.tensor_scalar(needtab[:, RQ:], nb[:, 1:QUADS - RQ + 1], 2.0, 2.0, ALU.mult, ALU.add).then_inc(tab_ready, 1)

            def gcn(i):
                wait(dve, part_in, 16 * NTAB * (i + 1))
                wait(dve, c_mm, BG * i)
                V.tensor_tensor(part[:, :, 0:EF], part4[:, 0], part4[:, 1], ALU.add)
                V.tensor_tensor(part4[:, 2], part4[:, 2], part4[:, 3], ALU.add)
                dve.drain()
                V.tensor_tensor(part[:, :, 0:EF], part[:, :, 0:EF], part4[:, 2], ALU.add).then_inc(part_ready, 1)
                wait(dve, g_out_s, 16 * i)
                wait(dve, b_out_s, 16 * i)
                for j in range(BG):
                    t = BG * i + j
                    wait(dve, e_ready, t + 1)
                    V.scalar_tensor_tensor(out=eT[:], in0=e1[:], scalar=LRELU, in1=e1[:], op0=ALU.mult,
                                           op1=ALU.max).then_inc(eT_ready, 1)
                    wait(dve, c_mm, t + 1)
                    di = dinv[:, bass.ds(t, 1)]
                    V.tensor_scalar(g_out[:, j, :], ps6[:, 0:D], di, None, ALU.mult)
                    V.tensor_tensor(zt[:], ps6[:, D:], bc["bc"][:], ALU.add)
                    dve.drain()
                    V.scalar_tensor_tensor(out=b_out[:, j, :], in0=g_out[:, j, :], scalar=di, in1=zt[:],
                                           op0=ALU.mult, op1=ALU.add).then_inc(gb_ready, 1)
                    dve.drain()

            gcn(0)
            with dve.Fori(1, NT // BG) as i:
                gcn(i)

            def onehots(b):
                lo = dve.value_load(qtab[0:1, bass.ds(b, 1)], min_val=0, max_val=QUADS - 1)
                hi = dve.value_load(qtab[0:1, bass.ds(b + 1, 1)], min_val=0, max_val=QUADS - 1)
                V.tensor_scalar(dst_r[:], dst_t[:], node0[:, bass.ds(b, 1)], None, ALU.subtract)
                dve.drain()
                with dve.Fori(lo, hi + 1) as q:
                    for h in range(2):
                        dve.wait_ge(agg_half, (q + b) * 2 + h + 1)
                        V.tensor_tensor(oh[:, 2 * h:2 * h + 2], iota_r[:].unsqueeze(1).to_broadcast([P, 2, P]),
                                        dst_r[:, bass.ds(q * 4 + 2 * h, 2)].unsqueeze(2).to_broadcast([P, 2, P]),
                                        ALU.is_equal).then_inc(oneh_ready, 1)

            def node_out(b):
                if isinstance(b, int):
                    a = acc[:, b % 2, :]
                else:
                    a = acc.rearrange("p s d -> p (s d)")[:, bass.ds((b % 2) * D, D)]
                wait(dve, agg_done, b + 1)
                wait(dve, base_in, 16 * (b + 1))
                wait(dve, mixr_in, 16 * (b + 1))
                V.scalar_tensor_tensor(out=zt[:], in0=ps0[:, 0:D], scalar=dinv[:, bass.ds(b, 1)], in1=xn2[:],
                                       op0=ALU.mult, op1=ALU.add).then_inc(agg_read, 1)
                dve.drain()
                wait(dve, xlT_ps, b)
                V.scalar_tensor_tensor(out=a, in0=zt[:], scalar=0.0, in1=x2[:], op0=ALU.max, op1=ALU.add)
                dve.drain()
                normalise(xl, a).then_inc(xl_ready, 1)

            def route(b):
                wait(dve, gate_mm, b + 1)
                V.tensor_tensor(score[:], ps2[:, 384:384 + NEXP], bg_bc[:], ALU.add)
                dve.drain()
                V.max(top[:], score[:])
                dve.drain()
                V.max_index(topi[:], top[:], score[:])
                dve.drain()
                V.tensor_copy(topf[:], topi[:])
                dve.drain()
                V.tensor_scalar(mask1[:], iota_r[:, 0:NEXP], topf[:, 0:1], None, ALU.is_equal)
                dve.drain()
                V.scalar_tensor_tensor(out=mask[:], in0=iota_r[:, 0:NEXP], scalar=topf[:, 1:2], in1=mask1[:],
                                       op0=ALU.is_equal, op1=ALU.add).then_inc(mask_ready, 1)

            def combine(b):
                if isinstance(b, int):
                    a = acc[:, b % 2, :]
                else:
                    a = acc.rearrange("p s d -> p (s d)")[:, bass.ds((b % 2) * D, D)]
                for e in range(NEXP):
                    dve.drain()
                    wait(dve, ey_mm, NEXP * b + e + 1)
                    V.scalar_tensor_tensor(out=a, in0=[ps3, ps4][e % 2][:, 0:D], scalar=mask[:, e:e + 1], in1=a,
                                           op0=ALU.mult, op1=ALU.add).then_inc(comb_done, 1)
                dve.drain()
                wait(dve, bias_mm, b + 1)
                wait(dve, stored, 16 * b)
                V.tensor_tensor(outb, a, ps5[:, 0:D], ALU.add).then_inc(out_ready, 1)

            onehots(0)
            node_out(0)
            onehots(1)
            route(0)
            node_out(1)
            combine(0)
            with dve.Fori(1, NT - 1) as b:
                onehots(b + 1)
                route(b)
                node_out(b + 1)
                combine(b)
            route(NT - 1)
            combine(NT - 1)


_INS = ["x", "src", "dst", "edge_attr_64", "L0_gnn_W_edge", "L0_gnn_b_edge", "L0_gnn_W_conv", "L0_gnn_b_conv",
        "L0_gnn_W_res", "L0_gnn_b_res", "L0_mix_Wq", "L0_mix_bq", "L0_mix_Wk", "L0_mix_bk", "L0_mix_Wv", "L0_mix_bv",
        "L0_mix_Wo", "L0_mix_bo", "L0_mix_W1", "L0_mix_b1", "L0_mix_W2", "L0_mix_b2", "L0_mix_ln1_g", "L0_mix_ln1_b",
        "L0_mix_ln2_g", "L0_mix_ln2_b", "L0_ffn_Wg", "L0_ffn_bg", "L0_ffn_W1", "L0_ffn_b1", "L0_ffn_W2", "L0_ffn_b2"]


def kernel(**inputs):
    import numpy as np
    import concourse.bacc as bacc
    from concourse.bass_utils import run_bass_kernel_spmd

    def padded(a, n, value):
        tail = np.full((n - a.shape[0],) + a.shape[1:], value, a.dtype)
        return np.concatenate([a, tail])

    nc = bacc.Bacc("TRN2", target_bir_lowering=False, num_devices=1)
    arrays, aps = {}, {}
    for name in _INS:
        a = np.ascontiguousarray(inputs[name])
        if name == "x":
            a = padded(a, NP, 0)
        elif name in ("src", "dst"):
            a = padded(a, EP, NP)
        elif name == "edge_attr_64":
            a = padded(a, EP, 0)
        arrays[f"in_{name}"] = a
        aps[name] = nc.dram_tensor(f"in_{name}", a.shape, mybir.dt.from_np(a.dtype), kind="ExternalInput").ap()
    out = nc.dram_tensor("out", (NP, D), F32, kind="ExternalOutput").ap()
    build(nc, aps, out)
    result = run_bass_kernel_spmd(nc, [arrays], core_ids=[0])
    return result.results[0]["out"][:N]
```

```python
from contextlib import ExitStack

import concourse.bass as bass
from concourse import mybir

F32 = mybir.dt.float32
F32R = mybir.dt.float32r
BF16 = mybir.dt.bfloat16
I32 = mybir.dt.int32
U32 = mybir.dt.uint32
ALU = mybir.AluOpType
ACT = mybir.ActivationFunctionType
AX_X = mybir.AxisListType.X

P = 128
N = 6250
NT = -(-N // P)
NP = NT * P
LAST = N - (NT - 1) * P
E = 106250
CH = 16
NCH = -(-E // (P * CH))
ET = NCH * CH
EP = ET * P
D = 256
KD = D // P
EF = 64
FF = 1024
KF = FF // P
NEXP = 8
HID = 512
KH = HID // P
HEAD = 32
NTAB = 4
TROWS = NP + P
QUADS = ET // 4
RQ = 8
GRP = 4
NG = NT // GRP
NF = NG // 2
assert NG == 2 * NF
BG = 7
LN_EPS = 1e-5
LRELU = 0.01
INSERT = (5, 12, 19, 26)
LOADS = 26 * 16
TC = ET // 8


def wait(eng, sem, value):
    if isinstance(value, int) and value <= 0:
        return
    eng.wait_ge(sem, value)


def build(nc, A, out):
    with ExitStack() as ctx:
        def sb(name, shape, dt=F32):
            return ctx.enter_context(nc.sbuf_tensor(name, shape, dt))

        def bank(name, shape=(P, 512), dt=F32):
            return ctx.enter_context(nc.psum_tensor(name, list(shape), dt))

        def sem(name):
            return ctx.enter_context(nc.semaphore(name))

        early = ctx.enter_context(ExitStack())

        def sa(name, shape, dt=F32):
            return early.enter_context(nc.sbuf_tensor(name, shape, dt))

        def dram(name, shape, dt=F32):
            return nc.dram_tensor(name, shape, dt).ap()

        table = [dram(f"table{r}", (TROWS, EF)) for r in range(NTAB)]
        xn_d = dram("xn_d", (NP, D))
        xnT_d = dram("xnT_d", (NP, D))
        mix_d = dram("mix_d", (NP, D))
        g_d = dram("g_d", (NP, D))
        f_d = [dram(f"f{part}_d", (2 * NEXP, P, 1024)) for part in ("hi", "lo")]
        base_d = dram("base_d", (NP, D))

        def rows(t, b, n=1):
            if n == 1:
                return t[bass.ds(b * P, P), :]
            return t[bass.ds(b * P, n * P), :].rearrange("(n p) d -> p n d", p=P)

        ident = sb("ident", [P, P])
        iota_r = sb("iota_r", [P, P])
        node0 = sb("node0", [P, NT])
        zero_bf = sb("zero_bf", [P, 512], BF16)
        src_t = sb("src_t", [P, ET], I32)
        dst_t = sb("dst_t", [P, ET])
        dinv = sb("dinv", [P, NT])
        qtab = sb("qtab", [1, NT + 1], I32)
        needtab = sb("needtab", [1, QUADS], I32)
        bg_bc = sb("bg_bc", [P, NEXP])
        fb1_c = sb("fb1_c", [P, NEXP * KH])
        fb2 = sb("fb2", [NEXP, D])
        wg_hi = sb("wg_hi", [P, KD, NEXP], F32R)
        wg_lo = sb("wg_lo", [P, KD, NEXP], F32R)
        stats = sb("stats", [P, GRP, 6])
        mv = sb("mv", [P, GRP, 2])
        rs = sb("rs", [P, 4, NT])
        rs_i = sb("rs_i", [P, NT], I32)
        zt = sa("zt", [P, D])
        before = sa("before", [P, P])
        raw_iota = sa("raw_iota", [P, P], I32)
        raw_iotb = sa("raw_iotb", [P, NT], I32)
        raw_iotq = sa("raw_iotq", [1, QUADS], I32)
        raw_iotp = sa("raw_iotp", [P, 1], I32)
        iota_bf = sa("iota_bf", [P, P], BF16)
        iota_q = sa("iota_q", [1, QUADS])
        trash = sa("trash", [P, 1])
        ones = sa("ones", [P, P])
        headmask = sa("headmask", [P, P])
        w_g = sa("w_g", [P, KD, NEXP])
        w_kv = sa("w_kv", [P, KD, 512])
        w_q = sa("w_q", [P, KD, D])
        w_o = sa("w_o", [P, KD, D])
        w_1 = sa("w_1", [P, KD, FF])
        w_2 = sa("w_2", [P, KF, D])
        w_cr = sa("w_cr", [P, 3, 512])
        w_e = sa("w_e", [EF, P])
        bc = {n: sa("bc_" + n, [P, D]) for n in ("bk", "bv", "bo", "b2", "g1", "c1", "g2", "c2", "bc", "br")}
        bq_c = sa("bq_c", [P, KD])
        b1_c = sa("b1_c", [P, KF])
        be_c = sa("be_c", [P, 1])
        raw_i = sa("raw_i", [P, ET], I32)
        src_pm = sa("src_pm", [P, ET])
        dst_r = sa("dst_r", [P, ET], BF16)
        dst_b = sa("dst_b", [P, ET], BF16)
        attr = sa("attr", [P, 2, 8, EF])
        src_st = sa("src_st", [P, CH])
        idx_st = sa("idx_st", [P, CH], I32)
        eq = sa("eq", [P, 2, 4, P])
        dup = sa("dup", [P, 2, 4, P], BF16)
        one_bf = sa("one_bf", [P, 1], BF16)
        cnt = sa("cnt", [P, CH])
        shift = sa("shift", [P, 2, 8])
        again = sa("again", [P, 2, 8])
        sums = sa("sums", [P, 2, 8, EF])
        oh_r = sa("oh_r", [P, CH, P], BF16)
        oh_b = sa("oh_b", [P, CH, NT], BF16)
        deg = sa("deg", [P, NT])
        cum = sa("cum", [P, NT])
        cum_f = sa("cum_f", [P, NT])
        cum_i = sa("cum_i", [P, NT], I32)
        qlast = sa("qlast", [1, NT])
        nb = sa("nb", [1, QUADS])
        stage = sa("stage", [P, 3 * BG * D])
        bw = BG * D
        part4 = stage[:, 0:bw].rearrange("p (r n f) -> p r n f", r=NTAB, n=BG)
        xT_g = stage[:, bw:2 * bw].rearrange("p (n k r) -> p n k r", n=BG, k=KD)
        b_out = stage[:, 2 * bw:3 * bw].rearrange("p (n d) -> p n d", n=BG)
        g_st = sa("g_st", [P, BG, D])
        edge_raw = sa("edge_raw", [TC, 2, 8 * P], I32)
        edge_in = [edge_raw[:, n].rearrange("r (c q) -> r c q", c=8) for n in range(2)]
        edge_f = stage[0:TC, 0:2 * P].rearrange("r (s q) -> r s q", s=2)
        wst = sa("wst", [P, 2, 1024])
        whi = sa("whi", [P, 2, 1024], F32R)
        wlo = sa("wlo", [P, 2, 1024], F32R)
        xg = sa("xg", [P, GRP, D])
        xng = sa("xng", [P, GRP, D])
        xT_st = sa("xT_st", [P, GRP, KD, P])
        kb = sa("kb", [P, 2, D])
        ke = sa("ke", [P, 2, D])
        va = sa("va", [P, 2, KD, P + 1])
        kv_acc = sa("kv_acc", [P, KD, P + 1])
        kv_bd = sa("kv_bd", [P, KD, P])
        ks_bd = sa("ks_bd", [P, KD, P])
        xT2 = sa("xT2", [P, KD, P])
        xn2 = sa("xn2", [P, D])
        x2 = sa("x2", [P, D])
        qm = sa("qm", [P, KD, P])
        qp = sa("qp", [P, KD, P])
        on = sa("on", [P, KD, P])
        y1 = sa("y1", [P, D])
        y1T = sa("y1T", [P, KD, P])
        hT = sa("hT", [P, KF, P])
        mixo = sa("mixo", [P, D])
        part = sa("part", [P, BG, P])
        partT = sa("partT", [P, P])
        e1 = sa("e1", [P, P])
        eT = sa("eT", [P, P])
        early.close()
        f_1 = [sb(f"f1_{n}", [P, NEXP, KD * HID], F32R) for n in ("hi", "lo")]
        f_2 = [sb(f"f2_{n}", [P, NEXP, KH * D], F32R) for n in ("hi", "lo")]
        ring = sb("ring", [P, 4 * RQ * D])
        gidx = sb("gidx", [P, 2, 2 * RQ], I32)
        oh = sb("oh", [P, 4, P])
        base_t = sb("base_t", [P, D])
        mix_t = sb("mix_t", [P, D])
        x_in4 = sb("x_in4", [P, GRP, D])
        xl4 = sb("xl4", [P, GRP, D])
        xlT = [sb(f"xlT_{n}", [P, KD, 512], F32R) for n in ("hi", "lo")]
        acc = sb("acc", [P, GRP, D])
        hf = sb("hf", [P, 512])
        hhl = [sb(f"h_{n}", [P, 2, 512], F32R) for n in ("hi", "lo")]
        score = sb("score", [P, GRP, NEXP])
        top = sb("top", [P, GRP, 8])
        topi = sb("topi", [P, GRP, 8], U32)
        topf = top[:]
        mask = sb("mask", [P, GRP, NEXP])
        mask1 = score[:]
        maskT = acc[0:NEXP].rearrange("p n d -> p (n d)")[:, 0:512]

        ps0, ps1, ps2, ps3, ps4, ps5, ps6, ps7 = [bank(f"ps{i}") for i in range(8)]
        psT = [ps0, ps1]

        loaded, const_ready, idents, edges_in, edge_rows, edge_ps, edge_cols = (
            sem(n) for n in ("loaded", "const_ready", "idents", "edges_in", "edge_rows", "edge_ps", "edge_cols"))
        zeros_ready, tables_zero = sem("zeros_ready"), sem("tables_zero")
        attr_in = [sem(f"attr_in{h}") for h in range(2)]
        dup_ready = sem("dup_ready")
        src_staged, src_bc, eq_ready, seg_summed, sums_ready, idx_ready = (
            sem(n) for n in ("src_staged", "src_bc", "eq_ready", "seg_summed", "sums_ready", "idx_ready"))
        scat = [sem(f"scat{r}") for r in range(NTAB)]
        oh_ready, deg_mm, deg_added = sem("oh_ready"), sem("deg_mm"), sem("deg_added")
        x_in, xn_ready, xT_ps, xT_ready, xn_out, xnT_out = (
            sem(n) for n in ("x_in", "xn_ready", "xT_ps", "xT_ready", "xn_out", "xnT_out"))
        kv_proj, kmin_ready, kexp_ready, phi_ready, kv_mm, kv_added, bd_ready = (
            sem(n) for n in ("kv_proj", "kmin_ready", "kexp_ready", "phi_ready", "kv_mm", "kv_added", "bd_ready"))
        xT2_in, xn2_in, x2_in, q_mm, qp_ready, qm_ready, qe_ready, qphi_ready = (
            sem(n) for n in ("xT2_in", "xn2_in", "x2_in", "q_mm", "qp_ready", "qm_ready", "qe_ready", "qphi_ready"))
        nd_mm, o_ready, o_mm, y1_ready, y1T_ps, y1T_ready, h_mm, relu_ready, z_mm, mix_ready, mix_out = (
            sem(n) for n in ("nd_mm", "o_ready", "o_mm", "y1_ready", "y1T_ps", "y1T_ready", "h_mm",
                             "relu_ready", "z_mm", "mix_ready", "mix_out"))
        dinv_ready, count_mm, tab_ready = sem("dinv_ready"), sem("count_mm"), sem("tab_ready")
        part_in, xTg_in, part_ready, pT_ps, pT_ready, e_mm, e_ready, eT_ready, c_mm, gb_ready, g_out_s, b_out_s = (
            sem(n) for n in ("part_in", "xTg_in", "part_ready", "pT_ps", "pT_ready", "e_mm", "e_ready",
                             "eT_ready", "c_mm", "gb_ready", "g_stored", "base_stored"))
        f_in = sem("f_in")
        wst_in = [sem(f"wst_in{n}") for n in range(2)]
        whi_ready, wlo_ready = sem("whi_ready"), sem("wlo_ready")
        f_out = [sem(f"f_out{n}") for n in range(2)]
        gat = [sem(f"gat{j}") for j in range(4)]
        gidx_ready, pool_mark = sem("gidx_ready"), sem("pool_mark")
        dstl_ready, oneh_ready, agg_half, agg_done, agg_read = (
            sem(n) for n in ("dstl_ready", "oneh_ready", "agg_half", "agg_done", "agg_read"))
        base_in, mixr_in, nodein_read, xl_ready, xlT_ps, xlThi_ready, xlTlo_ready = (
            sem(n) for n in ("base_in", "mixr_in", "nodein_read", "xl_ready", "xlT_ps", "xlThi_ready", "xlTlo_ready"))
        gate_mm, mask_ready, maskT_ps, maskT_ready, bias_mm, acc_ready = (
            sem(n) for n in ("gate_mm", "mask_ready", "maskT_ps", "maskT_ready", "bias_mm", "acc_ready"))
        up_mm, gelu_ready, lo_ready, dn_mm, comb_done, stored = (
            sem(n) for n in ("up_mm", "gelu_ready", "lo_ready", "dn_mm", "comb_done", "stored"))

        attr_pm = A["edge_attr_64"].rearrange("(p t) f -> p t f", p=P)
        block = ctx.enter_context(nc.Block())

        @block.sync
        def _(sp):
            n = [0]

            def load(dst, src):
                sp.dma_start(dst, src).then_inc(loaded, 16)
                n[0] += 16

            sp.dma_start(raw_i[:], A["src"].rearrange("(p t) -> p t", p=P)).then_inc(edges_in, 16)
            for n_, name in enumerate(("dst", "src")):
                sp.dma_start(edge_in[n_], A[name].rearrange("(c r q) -> r c q", c=8, q=P)).then_inc(edges_in, 16)
            load(w_kv[:, :, 0:D], A["L0_mix_Wk"].rearrange("(k p) n -> p k n", p=P))
            load(w_kv[:, :, D:], A["L0_mix_Wv"].rearrange("(k p) n -> p k n", p=P))
            load(w_q[:], A["L0_mix_Wq"].rearrange("(k p) n -> p k n", p=P))
            load(w_o[:], A["L0_mix_Wo"].rearrange("(k p) n -> p k n", p=P))
            load(w_1[:], A["L0_mix_W1"].rearrange("(k p) n -> p k n", p=P))
            load(w_2[:], A["L0_mix_W2"].rearrange("(k p) n -> p k n", p=P))
            load(w_cr[:, :, 0:D], A["L0_gnn_W_conv"].rearrange("(k p) n -> p k n", p=P))
            load(w_cr[:, :, D:], A["L0_gnn_W_res"].rearrange("(k p) n -> p k n", p=P))
            load(w_e[:], A["L0_gnn_W_edge"])
            load(w_g[:], A["L0_ffn_Wg"].rearrange("(k p) n -> p k n", p=P))
            for b, name in (("bk", "L0_mix_bk"), ("bv", "L0_mix_bv"), ("bo", "L0_mix_bo"), ("b2", "L0_mix_b2"),
                            ("g1", "L0_mix_ln1_g"), ("c1", "L0_mix_ln1_b"), ("g2", "L0_mix_ln2_g"),
                            ("c2", "L0_mix_ln2_b"), ("bc", "L0_gnn_b_conv"), ("br", "L0_gnn_b_res")):
                load(bc[b][:], A[name].unsqueeze(0).to_broadcast([P, D]))
            load(bg_bc[:], A["L0_ffn_bg"].unsqueeze(0).to_broadcast([P, NEXP]))
            with nc.allow_non_contiguous_dma(reason="small bias columns"):
                load(bq_c[:], A["L0_mix_bq"].rearrange("(k p) -> p k", p=P))
                load(b1_c[:], A["L0_mix_b1"].rearrange("(k p) -> p k", p=P))
                load(be_c[:], A["L0_gnn_b_edge"].rearrange("(p k) -> p k", k=1))
                load(fb1_c[:], A["L0_ffn_b1"].rearrange("e (k p) -> p (e k)", p=P))
            load(fb2[:], A["L0_ffn_b2"])
            assert n[0] == LOADS
            sp.wait_ge(zeros_ready, 1)
            for t in table:
                sp.dma_start(t.rearrange("(p n) f -> p (n f)", p=P), stage[:, 0:TROWS // P * EF]).then_inc(tables_zero, 16)

            def pass1_loads(i, tiles):
                wait(sp, xn_ready, i)
                sp.dma_start(xg[:, 0:tiles] if tiles > 1 else xg[:, 0, :],
                             rows(A["x"], i * GRP, tiles)).then_inc(x_in, 16)

            def attr_load(i, h):
                wait(sp, seg_summed, 4 * i - 4 + 2 * h + 2)
                sp.dma_start(attr[:, h], attr_pm[:, bass.ds(i * CH + 8 * h, 8), :]).then_inc(attr_in[h], 16)

            def pass2_loads(b, i=None):
                wait(sp, q_mm, b)
                sp.dma_start(xT2[:].rearrange("p k r -> p (k r)"), rows(xnT_d, b)).then_inc(xT2_in, 16)
                if i is not None:
                    attr_load(i, 0)
                wait(sp, y1_ready, b)
                sp.dma_start(xn2[:], rows(xn_d, b)).then_inc(xn2_in, 16)
                if i is not None:
                    attr_load(i, 1)
                wait(sp, mix_ready, b)
                sp.dma_start(x2[:], rows(A["x"], b)).then_inc(x2_in, 16)

            def first_loads(i):
                for h in range(2):
                    attr_load(i, h)
                    pass1_loads(2 * i + h, GRP)

            first_loads(0)
            for n_ in range(2 * NEXP):
                e = n_ // 2
                wait(sp, wlo_ready, n_ - 1)
                src = A["L0_ffn_W1"][e] if n_ % 2 == 0 else A["L0_ffn_W2"][e]
                sp.dma_start(wst[:, n_ % 2].rearrange("p (k n) -> p k n", k=KD if n_ % 2 == 0 else KH),
                             src.rearrange("(k p) n -> p k n", p=P)).then_inc(wst_in[n_ % 2], 16)
            with sp.Fori(1, NF) as i:
                first_loads(i)
            pass1_loads(NG, 1)
            sp.wait_ge(xn_out, 16 * (NG + 1))
            sp.wait_ge(xnT_out, 16 * (NG + 1))
            pass2_loads(0, NF)
            pass2_loads(1, NF + 1)
            with sp.Fori(NF + 2, NCH) as i:
                pass2_loads(i - NF, i)
            with sp.Fori(NCH - NF, NT) as b:
                pass2_loads(b)
            for s in scat:
                sp.wait_ge(s, 16 * ET // NTAB)

            def gcn_loads(i):
                wait(sp, part_ready, i)
                for r in range(NTAB):
                    sp.dma_start(part4[:, r], rows(table[r], i * BG, BG)).then_inc(part_in, 16)
                wait(sp, c_mm, BG * i)
                sp.dma_start(xT_g.rearrange("p n k r -> p n (k r)"), rows(xnT_d, i * BG, BG)).then_inc(xTg_in, 16)

            gcn_loads(0)
            with sp.Fori(1, NT // BG) as i:
                gcn_loads(i)

            sp.wait_ge(g_out_s, 16 * (NT // BG))
            sp.wait_ge(b_out_s, 16 * (NT // BG))
            sp.wait_ge(mix_out, 16 * NT)
            for s in f_out:
                sp.wait_ge(s, 32 * NEXP)

            def tile_loads(b):
                wait(sp, nodein_read, b)
                sp.dma_start(base_t[:], rows(base_d, b)).then_inc(base_in, 16)
                sp.dma_start(mix_t[:], rows(mix_d, b)).then_inc(mixr_in, 16)

            def store(g, tiles):
                wait(sp, comb_done, NEXP * g + NEXP)
                sp.dma_start(rows(out, g * GRP, tiles), acc[:, 0:tiles] if tiles > 1 else acc[:, 0, :]).then_inc(stored, 16)

            tile_loads(0)
            for part_ in range(2):
                for t, w in enumerate((f_1, f_2)):
                    sp.dma_start(w[part_][:].bitcast(F32), f_d[part_].rearrange("(e t) p n -> t p e n", t=2)[t]).then_inc(f_in, 16)
            for t in range(1, GRP):
                tile_loads(t)
            with sp.Fori(0, NG - 1) as g:
                for t in range(GRP):
                    tile_loads(g * GRP + GRP + t)
                store(g, GRP)
            tile_loads(NT - 1)
            store(NG - 1, GRP)
            store(NG, 1)
            sp.wait_ge(stored, 16 * (NG + 1))

        @block.gpsimd
        def _(pool):
            g = nc.gpsimd
            g.memset(ones[:], 1.0).then_inc(idents, 1)
            g.memset(zero_bf[:], 0.0).then_inc(idents, 1)
            g.iota(raw_iota[:], pattern=[[1, P]], base=0, channel_multiplier=0).then_inc(idents, 1)
            g.iota(raw_iotb[:], pattern=[[P, NT]], base=0, channel_multiplier=0).then_inc(idents, 1)
            g.iota(raw_iotq[:], pattern=[[1, QUADS]], base=0, channel_multiplier=0).then_inc(idents, 1)
            g.iota(raw_iotp[:], pattern=[[0, 1]], base=NP, channel_multiplier=1).then_inc(idents, 1)
            pool.wait_ge(idents, 6)
            g.affine_select(out=before[:], in_=ones[:], compare_op=ALU.is_gt, fill=0.0, base=0,
                            pattern=[[1, P]], channel_multiplier=-1).then_inc(idents, 1)
            g.affine_select(out=ident[:], in_=ones[:], compare_op=ALU.is_equal, fill=0.0, base=0,
                            pattern=[[-1, P]], channel_multiplier=1).then_inc(idents, 1)

            def alone(s, value):
                if isinstance(value, int):
                    return wait(pool, s, value)
                pool.wait_ge(s, value)
                pool.sem_inc(pool_mark, 1)

            def scatter_chunk(i):
                for h in range(2):
                    alone(idx_ready, 2 * i + h + 1)
                    for j in range(8):
                        if j % 4 == 0:
                            alone(sums_ready, 4 * i + 2 * h + j // 4 + 1)
                        alone(scat[j % NTAB], 16 * (4 * i + 2 * h + j // 4))
                        g.indirect_dma_start(
                            out=table[j % NTAB],
                            out_offset=bass.IndirectOffsetOnAxis(ap=idx_st[:, 8 * h + j:8 * h + j + 1], axis=0),
                            in_=sums[:, h, j, :], in_offset=None, bounds_check=TROWS - 1,
                            compute_op=ALU.add).then_inc(scat[j % NTAB], 16)

            pool.wait_ge(tables_zero, 16 * NTAB)
            scatter_chunk(0)
            with pool.Fori(1, NCH) as i:
                scatter_chunk(i)

            pool.wait_ge(tab_ready, 1)
            pool.wait_ge(g_out_s, 16 * (NT // BG))
            pool.wait_ge(b_out_s, 16 * (NT // BG))

            def gather(i):
                for h in range(2):
                    for jj in range(4):
                        alone(gat[jj], 16 * (RQ * i - RQ + RQ // 2 * (h + 1)))
                    g.tensor_copy(gidx[:, h], src_t[:, bass.ds(i * 4 * RQ + 2 * RQ * h, 2 * RQ)]).then_inc(gidx_ready, 1)
                    alone(gidx_ready, 2 * i + h + 1)
                    for k in range(RQ // 2 * h, RQ // 2 * (h + 1)):
                        q = RQ * i + k
                        if not isinstance(i, int):
                            alone(agg_half, pool.value_load(needtab[0:1, bass.ds(q, 1)], min_val=2, max_val=2 * (QUADS + NT) + 2))
                        for jj in range(4):
                            alone(gat[jj], 16 * q)
                            s = 4 * (k - RQ // 2 * h) + jj
                            g.indirect_dma_start(
                                out=ring[:, (4 * k + jj) * D:(4 * k + jj + 1) * D], out_offset=None,
                                in_=g_d, in_offset=bass.IndirectOffsetOnAxis(ap=gidx[:, h, s:s + 1], axis=0),
                            ).then_inc(gat[jj], 16)

            gather(0)
            with pool.Fori(1, QUADS // RQ) as i:
                gather(i)

        @block.tensor
        def _(pe):
            T = nc.tensor

            def mm(o, l, r, first, last):
                return T.matmul(o, l, r, start=first, stop=last)

            pe.wait_ge(loaded, LOADS)
            pe.wait_ge(idents, 8)
            for t in range(2):
                for c in range(8):
                    k = 8 * t + c
                    wait(pe, edge_cols, k - 1)
                    pe.wait_ge(edge_rows, k + 1)
                    T.transpose(psT[k % 2][:, 0:TC], edge_f[:, k % 2, :], ident[0:TC, 0:TC]).then_inc(edge_ps, 1)

            def src_rows(i, k):
                wait(pe, src_staged, i + 1)
                wait(pe, eq_ready, 4 * i + k - 1)
                for j in range(4):
                    ins = T.transpose(psT[k % 2][:, j * P:(j + 1) * P],
                                      src_st[:, 4 * k + j:4 * k + j + 1].to_broadcast([P, P]), ident[:])
                ins.then_inc(src_bc, 1)

            def seg_sum(i, k):
                if k % 2 == 0:
                    wait(pe, attr_in[k // 2], 16 * (i + 1))
                wait(pe, dup_ready, 4 * i + k + 1)
                wait(pe, sums_ready, 4 * i + k)
                for j in range(4):
                    mm(ps2[:, j * EF:(j + 1) * EF], eq[:, k % 2, j, :], attr[:, k // 2, 4 * (k % 2) + j, :], True, True)
                    ins = mm(ps2[:, 4 * EF + j:4 * EF + j + 1], dup[:, k % 2, j, :], one_bf[:], True, True)
                ins.then_inc(seg_summed, 1)

            def degrees(i):
                wait(pe, oh_ready, i + 1)
                wait(pe, deg_added, i)
                for t in range(CH):
                    ins = mm(ps5[:, 0:NT], oh_r[:, t, :], oh_b[:, t, :], t == 0, t == CH - 1)
                ins.then_inc(deg_mm, 1)

            def pass1(i, tiles, c=None, k=0):
                def turn(j):
                    wait(pe, xT_ready, GRP * i + j - 1)
                    for k in range(KD):
                        ins = T.transpose([ps6, ps7][j % 2][:, k * P:(k + 1) * P],
                                          xng[:, j, k * P:(k + 1) * P], ident[:])
                    ins.then_inc(xT_ps, 1)

                def project(j):
                    wait(pe, xT_ready, GRP * i + j + 1)
                    wait(pe, kmin_ready, GRP * i + j)
                    for k in range(KD):
                        ins = mm(ps3[:, 0:512], xT_st[:, j, k, :], w_kv[:, k, :], k == 0, k == KD - 1)
                    ins.then_inc(kv_proj, 1)

                def kv(j):
                    n = P if tiles > 1 else LAST
                    wait(pe, phi_ready, GRP * i + j + 1)
                    wait(pe, kv_added, GRP * i + j)
                    for c in range(KD):
                        ins = mm(ps4[:, c * (P + 1):(c + 1) * (P + 1)], kb[0:n, j % 2, c * P:(c + 1) * P],
                                 va[0:n, j % 2, c, :], True, True)
                    ins.then_inc(kv_mm, 1)

                if c is not None:
                    src_rows(c, k)
                    if k == 0:
                        degrees(c)
                wait(pe, xn_ready, i + 1)
                turn(0)
                for j in range(tiles):
                    if j + 1 < tiles:
                        turn(j + 1)
                    project(j)
                    if j:
                        kv(j - 1)
                    if c is not None and j == 0:
                        src_rows(c, k + 1)
                    if c is not None and j == 1:
                        seg_sum(c, k)
                kv(tiles - 1)
                if c is not None:
                    seg_sum(c, k + 1)

            def down(b, i):
                wait(pe, mix_ready, b)
                wait(pe, deg_added, i + 1)
                for m in range(KF):
                    if m % 4 == 0:
                        wait(pe, relu_ready, 2 * b + m // 4 + 1)
                    ins = mm(ps5[:, D:2 * D], hT[:, m, :], w_2[:, m, :], m == 0, m == KF - 1)
                ins.then_inc(z_mm, 1)

            def pass2(b, i=None):
                wait(pe, xT2_in, 16 * (b + 1))
                wait(pe, y1_ready, b)
                for m in range(KD):
                    for k in range(KD):
                        ins = mm(ps3[:, m * P:(m + 1) * P], w_q[:, k, m * P:(m + 1) * P], xT2[:, k, :], k == 0, k == KD - 1)
                ins.then_inc(q_mm, 1)
                if i is not None:
                    src_rows(i, 0)
                    src_rows(i, 1)
                wait(pe, qphi_ready, b + 1)
                for m in range(KD):
                    mm(ps4[:, m * P:(m + 1) * P], kv_bd[:, m, :], qp[:, m, :], True, True)
                    ins = mm(ps4[:, D + m * P:D + (m + 1) * P], ks_bd[:, m, :], qp[:, m, :], True, True)
                ins.then_inc(nd_mm, 1)
                if not isinstance(b, int) or b:
                    down(b - 1, i - 1 if i is not None else NCH - 1)
                if i is not None:
                    seg_sum(i, 0)
                    src_rows(i, 2)
                wait(pe, o_ready, b + 1)
                for k in range(KD):
                    ins = mm(ps3[:, D:2 * D], on[:, k, :], w_o[:, k, :], k == 0, k == KD - 1)
                ins.then_inc(o_mm, 1)
                if i is not None:
                    seg_sum(i, 1)
                    src_rows(i, 3)
                wait(pe, y1_ready, b + 1)
                for k in range(KD):
                    ins = T.transpose(ps4[:, k * P:(k + 1) * P], y1[:, k * P:(k + 1) * P], ident[:])
                ins.then_inc(y1T_ps, 1)
                wait(pe, y1T_ready, b + 1)
                for m in range(KF):
                    for k in range(KD):
                        ins = mm([ps6, ps7][m // 4][:, (m % 4) * P:(m % 4 + 1) * P], w_1[:, k, m * P:(m + 1) * P],
                                 y1T[:, k, :], k == 0, k == KD - 1)
                    if m % 4 == 3:
                        ins.then_inc(h_mm, 1)
                if i is not None:
                    seg_sum(i, 2)
                    seg_sum(i, 3)
                if i is not None:
                    degrees(i)

            def first_step(i):
                for h in range(2):
                    pass1(2 * i + h, GRP, i, 2 * h)

            first_step(0)
            with pe.Fori(1, NF) as i:
                first_step(i)
            pass1(NG, 1)
            pe.wait_ge(bd_ready, 1)
            pass2(0, NF)
            pass2(1, NF + 1)
            with pe.Fori(NF + 2, NCH) as i:
                pass2(i - NF, i)
            with pe.Fori(NCH - NF, NT) as b:
                pass2(b)

            down(NT - 1, NCH - 1)
            pe.wait_ge(deg_added, NCH)
            pe.wait_ge(mix_ready, NT)
            mm(ps5[:, 0:NT], ones[:], deg[:], True, True).then_inc(count_mm, 1)

            def gcn(i):
                def turn(j):
                    wait(pe, pT_ready, BG * i + j)
                    T.transpose(ps5[:, 0:P], part[:, j, :], ident[:]).then_inc(pT_ps, 1)

                wait(pe, part_ready, i + 1)
                wait(pe, xTg_in, 16 * (i + 1))
                for j in range(BG):
                    t = BG * i + j
                    turn(j)
                    wait(pe, gb_ready, t)
                    for k in range(KD):
                        mm(ps6[:], xT_g[:, j, k, :], w_cr[:, k, :], k == 0, False)
                    wait(pe, pT_ready, t + 1)
                    mm(ps4[:, 0:P], w_e[:], partT[0:EF, :], True, True).then_inc(e_mm, 1)
                    wait(pe, eT_ready, t + 1)
                    mm(ps6[:], eT[:], w_cr[:, KD, :], False, True).then_inc(c_mm, 1)

            pe.wait_ge(tab_ready, 1)
            gcn(0)
            with pe.Fori(1, NT // BG) as i:
                gcn(i)

            pe.sem_inc(agg_half, 2)

            def aggregate(b):
                lo = pe.value_load(qtab[0:1, bass.ds(b, 1)], min_val=0, max_val=QUADS - 1)
                hi = pe.value_load(qtab[0:1, bass.ds(b + 1, 1)], min_val=0, max_val=QUADS - 1)
                wait(pe, agg_read, b)
                mm(ps0[:, 0:D], zero_bf[:, 0:P], zero_bf[:, 0:D], True, False)
                with pe.Fori(lo, hi + 1) as q:
                    for h in range(2):
                        pe.wait_ge(oneh_ready, (q + b) * 2 + h + 1)
                        for jj in (2 * h, 2 * h + 1):
                            pe.wait_ge(gat[jj], q * 16 + 16)
                            ins = mm(ps0[:, 0:D], oh[:, jj, :], ring[:, bass.ds((q % RQ) * (4 * D) + jj * D, D)], False, False)
                        ins.then_inc(agg_half, 1)
                mm(ps0[:, 0:D], zero_bf[:, 0:P], zero_bf[:, 0:D], False, True).then_inc(agg_done, 1)

            THREE = ((0, 0), (1, 0), (0, 1))

            def experts(g, tiles, following):
                W = tiles * P
                wait(pe, xl_ready, GRP * g + tiles)
                wait(pe, comb_done, NEXP * g)
                for k in range(KD):
                    for r in range(tiles):
                        ins = T.transpose([ps2, ps3][k][:, r * P:(r + 1) * P], xl4[:, r, k * P:(k + 1) * P], ident[:])
                ins.then_inc(xlT_ps, 1)
                wait(pe, xlThi_ready, g + 1)
                wait(pe, xlTlo_ready, g + 1)
                wait(pe, maskT_ready, g)

                def up(u):
                    e, m = u // KH, u % KH
                    wait(pe, gelu_ready, NEXP * KH * g + max(u - 1, 0))
                    n = 0
                    for k in range(KD):
                        for a, b in THREE:
                            ins = mm([ps6, ps7][u % 2][:, 0:W], f_1[a][:, e, k * HID + m * P:k * HID + (m + 1) * P],
                                     xlT[b][:, k, 0:W], n == 0, n == 5)
                            n += 1
                    ins.then_inc(up_mm, 1)

                def down(u):
                    e, m = u // KH, u % KH
                    wait(pe, gelu_ready, NEXP * KH * g + u + 1)
                    wait(pe, lo_ready, NEXP * KH * g + u + 1)
                    if m == 0:
                        wait(pe, comb_done, NEXP * g + max(e - 1, 0))
                        if e == 1:
                            wait(pe, acc_ready, g + 1)
                    for r in range(tiles):
                        y = [[ps2, ps3], [ps4, ps5]][e % 2][r // 2][:, (r % 2) * D:(r % 2 + 1) * D]
                        for n, (a, b) in enumerate(THREE):
                            ins = T.matmul(y, hhl[a][:, u % 2, r * P:(r + 1) * P], f_2[b][:, e, m * D:(m + 1) * D],
                                           start=m == 0 and n == 0 and r % 2 == 0, stop=m == KH - 1 and n == 2,
                                           skip_group_check=True)
                    ins.then_inc(dn_mm, 1)

                up(0)
                up(1)
                for r in range(tiles):
                    n = 0
                    for k in range(KD):
                        for a, b in THREE:
                            ins = mm(ps1[:, r * NEXP:(r + 1) * NEXP], xlT[a][:, k, r * P:(r + 1) * P],
                                     [wg_hi, wg_lo][b][:, k, :], n == 0, n == 5)
                            n += 1
                ins.then_inc(gate_mm, 1)
                for u in range(NEXP * KH):
                    down(u)
                    if u + 2 < NEXP * KH:
                        up(u + 2)
                    if u == 1:
                        wait(pe, mask_ready, g + 1)
                        for r in range(tiles):
                            ins = T.transpose(ps1[0:NEXP, r * P:(r + 1) * P], mask[:, r, :], ident[:])
                        ins.then_inc(maskT_ps, 1)
                    if u == 2:
                        wait(pe, maskT_ready, g + 1)
                        for r in range(tiles):
                            ins = mm([ps4, ps5][r // 2][:, (r % 2) * D:(r % 2 + 1) * D], maskT[:, r * P:(r + 1) * P], fb2[:], True, True)
                        ins.then_inc(bias_mm, 1)
                    if u in INSERT and INSERT.index(u) < following:
                        aggregate(g * GRP + GRP + INSERT.index(u))

            pe.wait_ge(dstl_ready, 1)
            for b in range(GRP):
                aggregate(b)
            pe.wait_ge(f_in, 64)
            experts(0, GRP, GRP)
            with pe.Fori(1, NG - 1) as g:
                experts(g, GRP, GRP)
            experts(NG - 1, GRP, 1)
            experts(NG, 1, 0)

        @block.scalar
        def _(act):
            S = nc.scalar
            act.wait_ge(loaded, LOADS)
            act.wait_ge(const_ready, 1)

            def quad(i, k):
                h = k // 2
                if k % 2 == 0:
                    for s in scat:
                        wait(act, s, 16 * (4 * i - 4 + 2 * h + 2))
                    wait(act, idx_ready, 2 * i - 1 + h)
                wait(act, seg_summed, 4 * i + k + 1)
                S.copy(sums[:, h, 4 * (k % 2):4 * (k % 2) + 4, :],
                       ps2[:, 0:4 * EF].rearrange("p (j f) -> p j f", j=4))
                S.copy(cnt[:, 4 * k:4 * k + 4], ps2[:, 4 * EF:4 * EF + 4]).then_inc(sums_ready, 1)

            def pass1(i, tiles, c=None, q=0):
                def turned(j):
                    if j == 0:
                        wait(act, xnT_out, 16 * i)
                    wait(act, xT_ps, GRP * i + j + 1)
                    S.copy(xT_st[:, j].rearrange("p k r -> p (k r)"), [ps6, ps7][j % 2][:, 0:D]).then_inc(xT_ready, 1)

                turned(0)
                for j in range(tiles):
                    if j + 1 < tiles:
                        turned(j + 1)
                    wait(act, kmin_ready, GRP * i + j + 1)
                    S.activation(ke[:, j % 2, :], ke[:, j % 2, :], ACT.Exp).then_inc(kexp_ready, 1)
                    if c is not None and j == 1:
                        quad(c, q)
                if c is not None:
                    quad(c, q + 1)
                wait(act, xT_ready, GRP * i + tiles)
                act.dma_start(rows(xn_d, i * GRP, tiles), xng[:, 0:tiles] if tiles > 1 else xng[:, 0, :]).then_inc(xn_out, 16)
                act.dma_start(rows(xnT_d, i * GRP, tiles),
                              xT_st[:].rearrange("p n k r -> p n (k r)") if tiles > 1
                              else xT_st[:, 0].rearrange("p k r -> p (k r)")).then_inc(xnT_out, 16)

            def store(b):
                wait(act, mix_ready, b + 1)
                act.dma_start(rows(mix_d, b), mixo[:]).then_inc(mix_out, 16)

            def pass2(b, i=None):
                wait(act, qm_ready, b + 1)
                for m in range(KD):
                    ins = S.activation(qp[:, m, :], ps3[:, m * P:(m + 1) * P], ACT.Relu, bias=bq_c[:, m:m + 1])
                ins.then_inc(qp_ready, 1)
                S.activation(qm[:], qm[:], ACT.Exp).then_inc(qe_ready, 1)
                if i is not None:
                    quad(i, 0)
                    quad(i, 1)
                if not isinstance(b, int) or b:
                    store(b - 1)
                wait(act, y1T_ps, b + 1)
                S.copy(y1T[:].rearrange("p k r -> p (k r)"), ps4[:, 0:D]).then_inc(y1T_ready, 1)
                for m in range(KF):
                    if m % 4 == 0:
                        wait(act, h_mm, 2 * b + m // 4 + 1)
                    ins = S.activation(hT[:, m, :], [ps6, ps7][m // 4][:, (m % 4) * P:(m % 4 + 1) * P], ACT.Relu,
                                       bias=b1_c[:, m:m + 1])
                    if m % 4 == 3:
                        ins.then_inc(relu_ready, 1)
                        if i is not None:
                            quad(i, 2 + m // 4)

            def first_step(i):
                for h in range(2):
                    pass1(2 * i + h, GRP, i, 2 * h)

            first_step(0)
            for n_ in range(2 * NEXP):
                act.wait_ge(wst_in[n_ % 2], 16 * (n_ // 2 + 1))
                wait(act, f_out[n_ % 2], 32 * (n_ // 2))
                S.copy(whi[:, n_ % 2], wst[:, n_ % 2]).then_inc(whi_ready, 1)
                act.wait_ge(whi_ready, n_ + 1)
                act.dma_start(f_d[0][n_], whi[:, n_ % 2].bitcast(F32)).then_inc(f_out[n_ % 2], 16)
                act.wait_ge(wlo_ready, n_ + 1)
                act.dma_start(f_d[1][n_], wlo[:, n_ % 2].bitcast(F32)).then_inc(f_out[n_ % 2], 16)
            with act.Fori(1, NF) as i:
                first_step(i)
            pass1(NG, 1)
            pass2(0, NF)
            pass2(1, NF + 1)
            with act.Fori(NF + 2, NCH) as i:
                pass2(i - NF, i)
            with act.Fori(NCH - NF, NT) as b:
                pass2(b)
            store(NT - 1)

            def gcn(i):
                for j in range(BG):
                    t = BG * i + j
                    wait(act, pT_ps, t + 1)
                    S.copy(partT[:], ps5[:, 0:P]).then_inc(pT_ready, 1)
                    wait(act, e_mm, t + 1)
                    S.activation(e1[:], ps4[:, 0:P], ACT.Identity, bias=be_c[:, 0:1]).then_inc(e_ready, 1)
                wait(act, gb_ready, BG * i + BG)
                act.dma_start(rows(g_d, i * BG, BG), g_st[:]).then_inc(g_out_s, 16)
                act.dma_start(rows(base_d, i * BG, BG), b_out).then_inc(b_out_s, 16)

            gcn(0)
            with act.Fori(1, NT // BG) as i:
                gcn(i)

            act.wait_ge(g_out_s, 16 * (NT // BG))
            act.wait_ge(b_out_s, 16 * (NT // BG))

            def experts(g, tiles):
                W = tiles * P
                wait(act, xlT_ps, g + 1)
                for k in range(KD):
                    ins = S.copy(xlT[0][:, k, 0:W], [ps2, ps3][k][:, 0:W])
                ins.then_inc(xlThi_ready, 1)
                for u in range(NEXP * KH):
                    v = NEXP * KH * g + u
                    wait(act, up_mm, v + 1)
                    wait(act, dn_mm, v - min(u, 1))
                    wait(act, lo_ready, v)
                    for o in (hf[:, 0:W], hhl[0][:, u % 2, 0:W]):
                        ins = S.activation(o, [ps6, ps7][u % 2][:, 0:W], ACT.Gelu, bias=fb1_c[:, u:u + 1])
                    ins.then_inc(gelu_ready, 1)
                    if u == 3:
                        wait(act, maskT_ps, g + 1)
                        wait(act, stored, 16 * g)
                        S.copy(maskT[:, 0:W], ps1[0:NEXP, 0:W]).then_inc(maskT_ready, 1)

            experts(0, GRP)
            with act.Fori(1, NG) as g:
                experts(g, GRP)
            experts(NG, 1)

        @block.vector
        def _(dve):
            V = nc.vector

            def rsqrt(result, v, n, eps):
                a, y, t = rs[:, 0, 0:n], rs[:, 1, 0:n], rs[:, 2, 0:n]
                half = rs_i[:, 0:n]
                V.tensor_scalar(a, v, float(eps), None, ALU.add)
                dve.drain()
                V.tensor_single_scalar(half, a.bitcast(I32), 1, op=ALU.arith_shift_right)
                dve.drain()
                V.tensor_scalar(a, a, -0.5, None, ALU.mult)
                V.tensor_scalar(y.bitcast(I32), half, -1.0, float(0x5F3759DF), ALU.mult, ALU.add)
                dve.drain()
                for step in range(3):
                    if n == 1:
                        V.tensor_scalar(t, y, y, a, ALU.mult, ALU.mult)
                    else:
                        V.tensor_tensor(t, y, y, ALU.mult)
                        dve.drain()
                        V.tensor_tensor(t, t, a, ALU.mult)
                    dve.drain()
                    V.scalar_tensor_tensor(out=result if step == 2 else y, in0=t, scalar=1.5, in1=y,
                                           op0=ALU.add, op1=ALU.mult)
                    dve.drain()

            def normalise(dst, src):
                V.bn_stats(stats[:, 0, :], src)
                dve.drain()
                V.bn_aggr(mv[:, 0, :], stats[:, 0, :])
                dve.drain()
                rsqrt(rs[:, 3, 0:1], mv[:, 0, 1:2], 1, LN_EPS)
                return V.tensor_scalar(dst, src, mv[:, 0, 0:1], rs[:, 3, 0:1], ALU.subtract, ALU.mult)

            dve.wait_ge(idents, 8)
            V.memset(stage[:, 0:TROWS // P * EF], 0.0).then_inc(zeros_ready, 1)
            V.memset(headmask[:], 0.0)
            dve.drain()
            for h in range(P // HEAD):
                s = slice(HEAD * h, HEAD * h + HEAD)
                V.memset(headmask[s, s], 1.0)
            V.tensor_copy(iota_r[:], raw_iota[:])
            V.tensor_scalar(node0[:], raw_iotb[:], -1.0, None, ALU.mult)
            V.tensor_copy(iota_q[:], raw_iotq[:])
            V.tensor_copy(trash[:], raw_iotp[:])
            V.tensor_copy(iota_bf[:], raw_iota[:])
            V.memset(one_bf[:], 1.0)
            V.memset(deg[:], 0.0)
            V.memset(kv_acc[:], 0.0)
            V.memset(part[:], 0.0)
            V.memset(va[:], 1.0)
            V.memset(qtab[:], 0)
            dve.wait_ge(loaded, LOADS)
            V.tensor_tensor(bc["bc"][:], bc["bc"][:], bc["br"][:], ALU.add)
            V.tensor_copy(wg_hi[:], w_g[:])
            dve.drain()
            V.tensor_tensor(wg_lo[:], w_g[:], wg_hi[:].bitcast(F32), ALU.subtract)
            dve.drain()
            V.engine_nop().then_inc(const_ready, 1)
            dve.wait_ge(tables_zero, 16 * NTAB)
            dve.wait_ge(edges_in, 48)
            V.tensor_copy(src_pm[:], raw_i[:])
            for t in range(2):
                for c in range(8):
                    k = 8 * t + c
                    wait(dve, edge_ps, k - 1)
                    V.tensor_copy(edge_f[:, k % 2, :], edge_in[t][:, c, :]).then_inc(edge_rows, 1)
                    dve.wait_ge(edge_ps, k + 1)
                    cols = slice(c * TC, (c + 1) * TC)
                    if t == 0:
                        V.tensor_copy(dst_t[:, cols], psT[k % 2][:, 0:TC]).then_inc(edge_cols, 1)
                    else:
                        V.tensor_scalar(src_t[:, cols], psT[k % 2][:, 0:TC], float(NP - 1), None,
                                        ALU.min).then_inc(edge_cols, 1)
            dve.drain()
            raw2 = raw_i[:]
            V.tensor_copy(raw2, dst_t[:])
            dve.drain()
            V.tensor_single_scalar(raw2, raw2, 7, op=ALU.arith_shift_right)
            dve.drain()
            V.tensor_copy(dst_b[:], raw2)
            dve.drain()
            V.scalar_tensor_tensor(out=dst_r[:], in0=dst_b[:], scalar=-float(P), in1=dst_t[:], op0=ALU.mult, op1=ALU.add)
            dve.drain()

            def head(i):
                dve.drain()
                V.tensor_copy(src_st[:], src_pm[:, bass.ds(i * CH, CH)]).then_inc(src_staged, 1)

            def onehot_dst(i):
                c0 = i * CH
                wait(dve, deg_mm, i)
                V.tensor_tensor(oh_r[:], iota_bf[:].unsqueeze(1).to_broadcast([P, CH, P]),
                                dst_r[:, bass.ds(c0, CH)].unsqueeze(2).to_broadcast([P, CH, P]), ALU.is_equal)
                V.tensor_tensor(oh_b[:], iota_bf[:, 0:NT].unsqueeze(1).to_broadcast([P, CH, NT]),
                                dst_b[:, bass.ds(c0, CH)].unsqueeze(2).to_broadcast([P, CH, NT]),
                                ALU.is_equal).then_inc(oh_ready, 1)

            def degrees(i):
                wait(dve, deg_mm, i + 1)
                V.tensor_tensor(deg[:], deg[:], ps5[:, 0:NT], ALU.add).then_inc(deg_added, 1)

            def quad(i, k):
                wait(dve, src_bc, 4 * i + k + 1)
                wait(dve, seg_summed, 4 * i + k - 1)
                V.tensor_tensor(eq[:, k % 2], psT[k % 2][:].rearrange("p (j e) -> p j e", j=4),
                                src_st[:, 4 * k:4 * k + 4].unsqueeze(2).to_broadcast([P, 4, P]),
                                ALU.is_equal).then_inc(eq_ready, 1)
                dve.drain()
                V.tensor_tensor(dup[:, k % 2], eq[:, k % 2], before[:].unsqueeze(1).to_broadcast([P, 4, P]),
                                ALU.mult).then_inc(dup_ready, 1)

            def index(i, h):
                s = slice(8 * h, 8 * h + 8)
                V.tensor_scalar(shift[:, h], src_st[:, s], -1.0, trash[:, 0:1], ALU.mult, ALU.add)
                wait(dve, sums_ready, 4 * i + 2 * h + 2)
                V.tensor_scalar(again[:, h], cnt[:, s], 1.0, None, ALU.min)
                dve.drain()
                V.tensor_tensor(shift[:, h], shift[:, h], again[:, h], ALU.mult)
                dve.drain()
                for q in scat:
                    wait(dve, q, 16 * (4 * i - 4 + 2 * h + 2))
                V.tensor_tensor(idx_st[:, s], src_st[:, s], shift[:, h], ALU.add).then_inc(idx_ready, 1)

            def pass1(i, tiles, c=None, q=0):
                wait(dve, x_in, 16 * (i + 1))
                for j in range(tiles):
                    V.bn_stats(stats[:, j, :], xg[:, j, :])
                dve.drain()
                for j in range(tiles):
                    V.bn_aggr(mv[:, j, :], stats[:, j, :])
                dve.drain()
                rsqrt(rs[:, 3, 0:tiles], mv[:, 0:tiles, 1], tiles, LN_EPS)
                wait(dve, xn_out, 16 * i)
                for j in range(tiles):
                    ins = V.tensor_scalar(xng[:, j, :], xg[:, j, :], mv[:, j, 0:1], rs[:, 3, j:j + 1], ALU.subtract, ALU.mult)
                ins.then_inc(xn_ready, 1)

                def front(j):
                    wait(dve, kv_proj, GRP * i + j + 1)
                    wait(dve, kv_mm, GRP * i + j - 1)
                    V.tensor_tensor(kb[:, j % 2], ps3[:, 0:D], bc["bk"][:], ALU.add)
                    V.tensor_tensor(va[:, j % 2, :, 0:P], ps3[:, D:].rearrange("p (c e) -> p c e", c=KD),
                                    bc["bv"][:].rearrange("p (c e) -> p c e", c=KD), ALU.add)
                    dve.drain()
                    V.tensor_scalar(ke[:, j % 2], kb[:, j % 2], 0.0, None, ALU.min).then_inc(kmin_ready, 1)

                def back(j):
                    wait(dve, kexp_ready, GRP * i + j + 1)
                    V.scalar_tensor_tensor(out=kb[:, j % 2], in0=kb[:, j % 2], scalar=0.0, in1=ke[:, j % 2],
                                           op0=ALU.max, op1=ALU.add).then_inc(phi_ready, 1)

                def add(j):
                    wait(dve, kv_mm, GRP * i + j + 1)
                    V.tensor_tensor(kv_acc[:], kv_acc[:], ps4[:, 0:KD * (P + 1)].rearrange("p (c e) -> p c e", c=KD),
                                    ALU.add).then_inc(kv_added, 1)

                front(0)
                for j in range(tiles):
                    if c is not None and j < 2:
                        quad(c, q + j)
                    back(j)
                    if j + 1 < tiles:
                        front(j + 1)
                    add(j)
                    dve.drain()
                if c is not None:
                    index(c, q // 2)

            def pass2(b, i=None):
                if i is not None:
                    head(i)
                wait(dve, q_mm, b + 1)
                for m in range(KD):
                    ins = V.tensor_scalar(qm[:, m, :], ps3[:, m * P:(m + 1) * P], bq_c[:, m:m + 1], 0.0, ALU.add, ALU.min)
                ins.then_inc(qm_ready, 1)
                if i is not None:
                    quad(i, 0)
                wait(dve, qe_ready, b + 1)
                wait(dve, qp_ready, b + 1)
                V.tensor_tensor(qp[:], qp[:], qm[:], ALU.add).then_inc(qphi_ready, 1)
                if i is not None:
                    quad(i, 1)
                wait(dve, nd_mm, b + 1)
                den = qm[:].rearrange("p k r -> p (k r)")
                V.tensor_scalar(den, ps4[:, D:2 * D], 1e-6, None, ALU.add)
                dve.drain()
                V.reciprocal(den, den)
                wait(dve, xn2_in, 16 * (b + 1))
                V.tensor_tensor(xn2[:], xn2[:], bc["bo"][:], ALU.add)
                dve.drain()
                V.tensor_tensor(on[:].rearrange("p k r -> p (k r)"), ps4[:, 0:D], den, ALU.mult).then_inc(o_ready, 1)
                if not isinstance(b, int) or b:
                    finish(b - 1)
                    dve.drain()
                wait(dve, o_mm, b + 1)
                V.tensor_tensor(zt[:], ps3[:, D:2 * D], xn2[:], ALU.add)
                dve.drain()
                normalise(zt[:], zt[:])
                dve.drain()
                V.tensor_tensor(zt[:], zt[:], bc["g1"][:], ALU.mult)
                dve.drain()
                V.tensor_tensor(y1[:], zt[:], bc["c1"][:], ALU.add).then_inc(y1_ready, 1)
                dve.drain()
                V.tensor_tensor(zt[:], y1[:], bc["b2"][:], ALU.add)
                if i is not None:
                    quad(i, 2)
                    quad(i, 3)
                    index(i, 0)
                    onehot_dst(i)
                    index(i, 1)
                    degrees(i)
                dve.drain()

            def finish(b):
                wait(dve, z_mm, b + 1)
                V.tensor_tensor(zt[:], ps5[:, D:2 * D], zt[:], ALU.add)
                wait(dve, x2_in, 16 * (b + 1))
                V.tensor_tensor(x2[:], x2[:], bc["c2"][:], ALU.add)
                dve.drain()
                normalise(zt[:], zt[:])
                dve.drain()
                V.tensor_tensor(zt[:], zt[:], bc["g2"][:], ALU.mult)
                dve.drain()
                wait(dve, mix_out, 16 * b)
                V.tensor_tensor(mixo[:], zt[:], x2[:], ALU.add).then_inc(mix_ready, 1)

            def first_step(i):
                head(i)
                onehot_dst(i)
                for h in range(2):
                    pass1(2 * i + h, GRP, i, 2 * h)
                degrees(i)

            first_step(0)
            for n_ in range(2 * NEXP):
                dve.wait_ge(whi_ready, n_ + 1)
                wait(dve, f_out[n_ % 2], 32 * (n_ // 2))
                V.tensor_tensor(wlo[:, n_ % 2], wst[:, n_ % 2], whi[:, n_ % 2].bitcast(F32), ALU.subtract).then_inc(wlo_ready, 1)
            with dve.Fori(1, NF) as i:
                first_step(i)
            pass1(NG, 1)
            for c in range(KD):
                V.tensor_tensor(kv_bd[:, c, :], kv_acc[:, c, 0:P], headmask[:], ALU.mult)
                ins = V.tensor_scalar(ks_bd[:, c, :], headmask[:], kv_acc[:, c, P:P + 1], None, ALU.mult)
            ins.then_inc(bd_ready, 1)
            pass2(0, NF)
            pass2(1, NF + 1)
            with dve.Fori(NF + 2, NCH) as i:
                pass2(i - NF, i)
            with dve.Fori(NCH - NF, NT) as b:
                pass2(b)
            finish(NT - 1)

            dve.drain()
            rsqrt(dinv[:], deg[:], NT, 1.0)
            dve.wait_ge(count_mm, 1)
            V.tensor_copy(cum_f[:], ps5[:, 0:NT])
            dve.drain()
            V.tensor_tensor_scan(cum[:], ones[:, 0:NT], cum_f[:], 0.0, ALU.mult, ALU.add)
            dve.drain()
            V.tensor_scalar(cum_i[:], cum[:], 1.0, -1.0, ALU.max, ALU.add)
            dve.drain()
            V.tensor_single_scalar(cum_i[:], cum_i[:], 9, op=ALU.arith_shift_right)
            dve.drain()
            V.tensor_copy(qtab[:, 1:NT + 1], cum_i[0:1, :])
            V.tensor_copy(qlast[:], cum_i[0:1, :])
            dve.drain()
            step = QUADS // 16
            wide = oh_r[0:1].rearrange("p t e -> p (t e)").bitcast(F32)[:, 0:step * NT].rearrange("p (q b) -> p q b", b=NT)
            for c in range(16):
                s = slice(c * step, (c + 1) * step)
                V.tensor_tensor(wide, iota_q[:, s].unsqueeze(2).to_broadcast([1, step, NT]),
                                qlast[:].unsqueeze(1).to_broadcast([1, step, NT]), ALU.is_gt)
                dve.drain()
                V.tensor_reduce(nb[:, s], wide, AX_X, ALU.add)
                dve.drain()
            V.tensor_tensor(nb[:], nb[:], iota_q[:], ALU.add)
            V.memset(needtab[:], 2)
            dve.drain()
            V.tensor_scalar(needtab[:, RQ:], nb[:, 1:QUADS - RQ + 1], 2.0, 2.0, ALU.mult, ALU.add).then_inc(tab_ready, 1)

            def gcn(i):
                wait(dve, part_in, 16 * NTAB * (i + 1))
                wait(dve, c_mm, BG * i)
                V.tensor_tensor(part[:, :, 0:EF], part4[:, 0], part4[:, 1], ALU.add)
                V.tensor_tensor(part4[:, 2], part4[:, 2], part4[:, 3], ALU.add)
                dve.drain()
                V.tensor_tensor(part[:, :, 0:EF], part[:, :, 0:EF], part4[:, 2], ALU.add).then_inc(part_ready, 1)
                wait(dve, g_out_s, 16 * i)
                wait(dve, b_out_s, 16 * i)
                for j in range(BG):
                    t = BG * i + j
                    wait(dve, e_ready, t + 1)
                    V.scalar_tensor_tensor(out=eT[:], in0=e1[:], scalar=LRELU, in1=e1[:], op0=ALU.mult,
                                           op1=ALU.max).then_inc(eT_ready, 1)
                    wait(dve, c_mm, t + 1)
                    di = dinv[:, bass.ds(t, 1)]
                    V.tensor_scalar(g_st[:, j, :], ps6[:, 0:D], di, None, ALU.mult)
                    V.tensor_tensor(zt[:], ps6[:, D:], bc["bc"][:], ALU.add)
                    dve.drain()
                    V.scalar_tensor_tensor(out=b_out[:, j, :], in0=g_st[:, j, :], scalar=di, in1=zt[:],
                                           op0=ALU.mult, op1=ALU.add).then_inc(gb_ready, 1)

            gcn(0)
            with dve.Fori(1, NT // BG) as i:
                gcn(i)

            dve.wait_ge(g_out_s, 16 * (NT // BG))
            dve.wait_ge(b_out_s, 16 * (NT // BG))
            dve.drain()
            V.memset(acc[:], 0.0).then_inc(dstl_ready, 1)

            def onehots(b):
                lo = dve.value_load(qtab[0:1, bass.ds(b, 1)], min_val=0, max_val=QUADS - 1)
                hi = dve.value_load(qtab[0:1, bass.ds(b + 1, 1)], min_val=0, max_val=QUADS - 1)
                with dve.Fori(lo, hi + 1) as q:
                    for h in range(2):
                        dve.wait_ge(agg_half, (q + b) * 2 + h + 1)
                        for jj in (2 * h, 2 * h + 1):
                            ins = V.tensor_scalar(oh[:, jj, :], iota_r[:], dst_t[:, bass.ds(q * 4 + jj, 1)],
                                                  node0[:, bass.ds(b, 1)], ALU.subtract, ALU.is_equal)
                        ins.then_inc(oneh_ready, 1)

            def node_out(b, s, piece):
                y, t, a = rs[:, 1, 0:1], rs[:, 2, 0:1], rs[:, 0, 0:1]
                if piece == 0:
                    wait(dve, agg_done, b + 1)
                    wait(dve, base_in, 16 * (b + 1))
                    V.scalar_tensor_tensor(out=x_in4[:, s, :], in0=ps0[:, 0:D], scalar=dinv[:, bass.ds(b, 1)], in1=base_t[:],
                                           op0=ALU.mult, op1=ALU.add).then_inc(agg_read, 1)
                    dve.drain()
                    wait(dve, mixr_in, 16 * (b + 1))
                    V.scalar_tensor_tensor(out=x_in4[:, s, :], in0=x_in4[:, s, :], scalar=0.0, in1=mix_t[:],
                                           op0=ALU.max, op1=ALU.add).then_inc(nodein_read, 1)
                    dve.drain()
                    V.bn_stats(stats[:, 0, :], x_in4[:, s, :])
                if piece == 1:
                    dve.drain()
                    V.bn_aggr(mv[:, 0, :], stats[:, 0, :])
                    dve.drain()
                    V.tensor_scalar(a, mv[:, 0, 1:2], LN_EPS, None, ALU.add)
                    dve.drain()
                    V.tensor_single_scalar(rs_i[:, 0:1], a.bitcast(I32), 1, op=ALU.arith_shift_right)
                    dve.drain()
                    V.tensor_scalar(a, a, -0.5, None, ALU.mult)
                    V.tensor_scalar(y.bitcast(I32), rs_i[:, 0:1], -1.0, float(0x5F3759DF), ALU.mult, ALU.add)
                if piece in (2, 3, 4):
                    dve.drain()
                    V.tensor_scalar(t, y, y, a, ALU.mult, ALU.mult)
                    dve.drain()
                    V.scalar_tensor_tensor(out=y, in0=t, scalar=1.5, in1=y, op0=ALU.add, op1=ALU.mult)
                if piece == 4:
                    dve.drain()
                    V.tensor_scalar(xl4[:, s, :], x_in4[:, s, :], mv[:, 0, 0:1], y, ALU.subtract, ALU.mult).then_inc(xl_ready, 1)

            def route(g, tiles):
                t = slice(0, tiles)
                wait(dve, gate_mm, g + 1)
                V.tensor_tensor(score[:, t], ps1[:, 0:tiles * NEXP].rearrange("p (r e) -> p r e", e=NEXP),
                                bg_bc[:].unsqueeze(1).to_broadcast([P, tiles, NEXP]), ALU.add)
                dve.drain()
                for r in range(tiles):
                    V.max(top[:, r], score[:, r])
                dve.drain()
                for r in range(tiles):
                    V.max_index(topi[:, r], top[:, r], score[:, r])
                dve.drain()
                V.tensor_copy(topf[:, t], topi[:, t])
                dve.drain()
                number = iota_r[:, 0:NEXP].unsqueeze(1).to_broadcast([P, tiles, NEXP])
                V.tensor_tensor(mask1[:, t], number, topf[:, t, 0:1].to_broadcast([P, tiles, NEXP]), ALU.is_equal)
                V.tensor_tensor(mask[:, t], number, topf[:, t, 1:2].to_broadcast([P, tiles, NEXP]), ALU.is_equal)
                dve.drain()
                V.tensor_tensor(mask[:, t], mask[:, t], mask1[:, t], ALU.add).then_inc(mask_ready, 1)

            def experts(g, tiles, following):
                W = tiles * P
                wait(dve, xlThi_ready, g + 1)
                for k in range(KD):
                    ins = V.tensor_tensor(xlT[1][:, k, 0:W], [ps2, ps3][k][:, 0:W], xlT[0][:, k, 0:W].bitcast(F32), ALU.subtract)
                ins.then_inc(xlTlo_ready, 1)
                for u in range(NEXP * KH):
                    v = NEXP * KH * g + u
                    wait(dve, gelu_ready, v + 1)
                    wait(dve, dn_mm, v - min(u, 1))
                    V.tensor_tensor(hhl[1][:, u % 2, 0:W], hf[:, 0:W], hhl[0][:, u % 2, 0:W].bitcast(F32),
                                    ALU.subtract).then_inc(lo_ready, 1)
                    if u == 1:
                        route(g, tiles)
                    if u == 3:
                        wait(dve, stored, 16 * g)
                        wait(dve, bias_mm, g + 1)
                        for r in range(0, tiles, 2):
                            n = min(2, tiles - r)
                            ins = V.tensor_tensor(acc[:, r:r + n], x_in4[:, r:r + n],
                                                  [ps4, ps5][r // 2][:, 0:n * D].rearrange("p (n d) -> p n d", n=n), ALU.add)
                        ins.then_inc(acc_ready, 1)
                    if u % KH == 0 and u or u == NEXP * KH - 1:
                        for e in [u // KH - 1] if u < NEXP * KH - 1 else [NEXP - 1]:
                            dve.drain()
                            wait(dve, dn_mm, NEXP * KH * g + KH * (e + 1))
                            for r in range(tiles):
                                ins = V.scalar_tensor_tensor(
                                    out=acc[:, r, :], in0=[[ps2, ps3], [ps4, ps5]][e % 2][r // 2][:, (r % 2) * D:(r % 2 + 1) * D],
                                    scalar=mask[:, r, e:e + 1], in1=acc[:, r, :], op0=ALU.mult, op1=ALU.add)
                            ins.then_inc(comb_done, 1)
                    for s in range(following):
                        after = u - 1 - INSERT[s]
                        if after == 0:
                            onehots(g * GRP + GRP + s)
                            node_out(g * GRP + GRP + s, s, 0)
                        elif 1 <= after <= 4:
                            node_out(g * GRP + GRP + s, s, after)

            for b in range(GRP):
                onehots(b)
                for piece in range(5):
                    node_out(b, b, piece)
            experts(0, GRP, GRP)
            with dve.Fori(1, NG - 1) as g:
                experts(g, GRP, GRP)
            experts(NG - 1, GRP, 1)
            experts(NG, 1, 0)


_INS = ["x", "src", "dst", "edge_attr_64", "L0_gnn_W_edge", "L0_gnn_b_edge", "L0_gnn_W_conv", "L0_gnn_b_conv",
        "L0_gnn_W_res", "L0_gnn_b_res", "L0_mix_Wq", "L0_mix_bq", "L0_mix_Wk", "L0_mix_bk", "L0_mix_Wv", "L0_mix_bv",
        "L0_mix_Wo", "L0_mix_bo", "L0_mix_W1", "L0_mix_b1", "L0_mix_W2", "L0_mix_b2", "L0_mix_ln1_g", "L0_mix_ln1_b",
        "L0_mix_ln2_g", "L0_mix_ln2_b", "L0_ffn_Wg", "L0_ffn_bg", "L0_ffn_W1", "L0_ffn_b1", "L0_ffn_W2", "L0_ffn_b2"]


def kernel(**inputs):
    import numpy as np
    import concourse.bacc as bacc
    from concourse.bass_utils import run_bass_kernel_spmd

    def padded(a, n, value):
        tail = np.full((n - a.shape[0],) + a.shape[1:], value, a.dtype)
        return np.concatenate([a, tail])

    nc = bacc.Bacc("TRN2", target_bir_lowering=False, num_devices=1)
    arrays, aps = {}, {}
    for name in _INS:
        a = np.ascontiguousarray(inputs[name])
        if name == "x":
            a = padded(a, NP, 0)
        elif name in ("src", "dst"):
            a = padded(a, EP, NP)
        elif name == "edge_attr_64":
            a = padded(a, EP, 0)
        arrays[f"in_{name}"] = a
        aps[name] = nc.dram_tensor(f"in_{name}", a.shape, mybir.dt.from_np(a.dtype), kind="ExternalInput").ap()
    out = nc.dram_tensor("out", (NP, D), F32, kind="ExternalOutput").ap()
    build(nc, aps, out)
    result = run_bass_kernel_spmd(nc, [arrays], core_ids=[0])
    return result.results[0]["out"][:N]
```

```python
from contextlib import ExitStack

import concourse.bass as bass
from concourse import mybir

F32 = mybir.dt.float32
F32R = mybir.dt.float32r
BF16 = mybir.dt.bfloat16
I32 = mybir.dt.int32
U32 = mybir.dt.uint32
ALU = mybir.AluOpType
ACT = mybir.ActivationFunctionType
AX_X = mybir.AxisListType.X

P = 128
N = 6250
NT = -(-N // P)
NP = NT * P
LAST = N - (NT - 1) * P
E = 106250
CH = 16
NCH = -(-E // (P * CH))
ET = NCH * CH
EP = ET * P
D = 256
KD = D // P
EF = 64
FF = 1024
KF = FF // P
NEXP = 8
HID = 512
KH = HID // P
HEAD = 32
NTAB = 4
TROWS = NP + P
QUADS = ET // 4
RQ = 8
GRP = 4
NG = NT // GRP
NF = NG // 2
assert NG == 2 * NF
BG = 7
LN_EPS = 1e-5
LRELU = 0.01
INSERT = (5, 12, 18, 25)
LOADS = 26 * 16
TC = ET // 8


def wait(eng, sem, value):
    if isinstance(value, int) and value <= 0:
        return
    eng.wait_ge(sem, value)


def build(nc, A, out):
    with ExitStack() as ctx:
        def sb(name, shape, dt=F32):
            return ctx.enter_context(nc.sbuf_tensor(name, shape, dt))

        def bank(name, shape=(P, 512), dt=F32):
            return ctx.enter_context(nc.psum_tensor(name, list(shape), dt))

        def sem(name):
            return ctx.enter_context(nc.semaphore(name))

        early = ctx.enter_context(ExitStack())

        def sa(name, shape, dt=F32):
            return early.enter_context(nc.sbuf_tensor(name, shape, dt))

        def dram(name, shape, dt=F32):
            return nc.dram_tensor(name, shape, dt).ap()

        table = [dram(f"table{r}", (TROWS, EF)) for r in range(NTAB)]
        xn_d = dram("xn_d", (NP, D))
        xnT_d = dram("xnT_d", (NP, D))
        mix_d = dram("mix_d", (NP, D))
        g_d = dram("g_d", (NP, D))
        f_d = [dram(f"f{part}_d", (2 * NEXP, P, 1024)) for part in ("hi", "lo")]
        base_d = dram("base_d", (NP, D))

        def rows(t, b, n=1):
            if n == 1:
                return t[bass.ds(b * P, P), :]
            return t[bass.ds(b * P, n * P), :].rearrange("(n p) d -> p n d", p=P)

        ident = sb("ident", [P, P])
        iota_r = sb("iota_r", [P, P])
        node0 = sb("node0", [P, NT])
        zero_bf = sb("zero_bf", [P, 512], BF16)
        src_t = sb("src_t", [P, ET], I32)
        dst_t = sb("dst_t", [P, ET])
        dinv = sb("dinv", [P, NT])
        qtab = sb("qtab", [1, NT + 1], I32)
        needtab = sb("needtab", [1, QUADS], I32)
        bg_bc = sb("bg_bc", [P, NEXP])
        fb1_c = sb("fb1_c", [P, NEXP * KH])
        fb2 = sb("fb2", [NEXP, D])
        wg_hi = sb("wg_hi", [P, KD, NEXP], F32R)
        wg_lo = sb("wg_lo", [P, KD, NEXP], F32R)
        stats = sb("stats", [P, GRP, 6])
        mv = sb("mv", [P, GRP, 2])
        rs = sb("rs", [P, 4, NT])
        rs_i = sb("rs_i", [P, NT], I32)
        zt = sa("zt", [P, D])
        before = sa("before", [P, P])
        raw_iota = sa("raw_iota", [P, P], I32)
        raw_iotb = sa("raw_iotb", [P, NT], I32)
        raw_iotq = sa("raw_iotq", [1, QUADS], I32)
        raw_iotp = sa("raw_iotp", [P, 1], I32)
        iota_bf = sa("iota_bf", [P, P], BF16)
        iota_q = sa("iota_q", [1, QUADS])
        trash = sa("trash", [P, 1])
        ones = sa("ones", [P, P])
        headmask = sa("headmask", [P, P])
        w_g = sa("w_g", [P, KD, NEXP])
        w_kv = sa("w_kv", [P, KD, 512])
        w_q = sa("w_q", [P, KD, D])
        w_o = sa("w_o", [P, KD, D])
        w_1 = sa("w_1", [P, KD, FF])
        w_2 = sa("w_2", [P, KF, D])
        w_cr = sa("w_cr", [P, 3, 512])
        w_e = sa("w_e", [EF, P])
        bc = {n: sa("bc_" + n, [P, D]) for n in ("bk", "bv", "bo", "b2", "g1", "c1", "g2", "c2", "bc", "br")}
        bq_c = sa("bq_c", [P, KD])
        b1_c = sa("b1_c", [P, KF])
        be_c = sa("be_c", [P, 1])
        raw_i = sa("raw_i", [P, ET], I32)
        src_pm = sa("src_pm", [P, ET])
        dst_r = sa("dst_r", [P, ET], BF16)
        dst_b = sa("dst_b", [P, ET], BF16)
        attr = sa("attr", [P, 2, 8, EF])
        src_st = sa("src_st", [P, CH])
        idx_st = sa("idx_st", [P, CH], I32)
        eq = sa("eq", [P, 2, 4, P])
        dup = sa("dup", [P, 2, 4, P], BF16)
        one_bf = sa("one_bf", [P, 1], BF16)
        cnt = sa("cnt", [P, CH])
        shift = sa("shift", [P, 2, 8])
        again = sa("again", [P, 2, 8])
        sums = sa("sums", [P, 2, 8, EF])
        diff_r = sa("diff_r", [P, CH, P], BF16)
        diff_b = sa("diff_b", [P, CH, NT], BF16)
        sq_r = sa("sq_r", [P, CH, P], BF16)
        sq_b = sa("sq_b", [P, CH, NT], BF16)
        oh_r = sa("oh_r", [P, CH, P], BF16)
        oh_b = sa("oh_b", [P, CH, NT], BF16)
        deg = sa("deg", [P, NT])
        cum = sa("cum", [P, NT])
        cum_f = sa("cum_f", [P, NT])
        cum_i = sa("cum_i", [P, NT], I32)
        qlast = sa("qlast", [1, NT])
        nb = sa("nb", [1, QUADS])
        stage = sa("stage", [P, 3 * BG * D])
        bw = BG * D
        part4 = stage[:, 0:bw].rearrange("p (r n f) -> p r n f", r=NTAB, n=BG)
        xT_g = stage[:, bw:2 * bw].rearrange("p (n k r) -> p n k r", n=BG, k=KD)
        b_out = stage[:, 2 * bw:3 * bw].rearrange("p (n d) -> p n d", n=BG)
        g_st = sa("g_st", [P, BG, D])
        edge_raw = sa("edge_raw", [TC, 2, 8 * P], I32)
        edge_in = [edge_raw[:, n].rearrange("r (c q) -> r c q", c=8) for n in range(2)]
        edge_f = sa("edge_f", [TC, 2, P])
        wst = sa("wst", [P, 2, 1024])
        whi = sa("whi", [P, 2, 1024], F32R)
        wlo = sa("wlo", [P, 2, 1024], F32R)
        xg = sa("xg", [P, GRP, D])
        xng = sa("xng", [P, GRP, D])
        xT_st = sa("xT_st", [P, GRP, KD, P])
        kb = sa("kb", [P, 2, D])
        ke = sa("ke", [P, 2, D])
        va = sa("va", [P, 2, KD, P + 1])
        kv_acc = sa("kv_acc", [P, KD, P + 1])
        kv_bd = sa("kv_bd", [P, KD, P])
        ks_bd = sa("ks_bd", [P, KD, P])
        xT2 = sa("xT2", [P, KD, P])
        xn2 = sa("xn2", [P, D])
        x2 = sa("x2", [P, D])
        qm = sa("qm", [P, KD, P])
        qp = sa("qp", [P, KD, P])
        on = sa("on", [P, KD, P])
        y1 = sa("y1", [P, D])
        y1T = sa("y1T", [P, KD, P])
        hT = sa("hT", [P, KF, P])
        mixo = sa("mixo", [P, D])
        part = sa("part", [P, BG, P])
        partT = sa("partT", [P, P])
        e1 = sa("e1", [P, P])
        eT = sa("eT", [P, 2, P])
        early.close()
        f_1 = [sb(f"f1_{n}", [P, NEXP, KD * HID], F32R) for n in ("hi", "lo")]
        f_2 = [sb(f"f2_{n}", [P, NEXP, KH * D], F32R) for n in ("hi", "lo")]
        ring = sb("ring", [P, 4 * RQ * D])
        gidx = sb("gidx", [P, 2, 2 * RQ], I32)
        oh = sb("oh", [P, 4, P])
        base_t = sb("base_t", [P, D])
        mix_t = sb("mix_t", [P, D])
        x_in4 = sb("x_in4", [P, GRP, D])
        xl4 = sb("xl4", [P, GRP, D])
        xlT = [sb(f"xlT_{n}", [P, KD, 512], F32R) for n in ("hi", "lo")]
        acc = sb("acc", [P, GRP, D])
        hf = sb("hf", [P, 512])
        hhl = [sb(f"h_{n}", [P, 2, 512], F32R) for n in ("hi", "lo")]
        score = sb("score", [P, GRP, NEXP])
        top = sb("top", [P, GRP, 8])
        topi = sb("topi", [P, GRP, 8], U32)
        topf = top[:]
        mask = sb("mask", [P, GRP, NEXP])
        mask1 = score[:]
        maskT = acc[0:NEXP].rearrange("p n d -> p (n d)")[:, 0:512]

        ps0, ps1, ps2, ps3, ps4, ps5, ps6, ps7 = [bank(f"ps{i}") for i in range(8)]
        psT = [ps0, ps1]

        loaded, const_ready, idents, edges_in, edge_rows, edge_ps, edge_cols = (
            sem(n) for n in ("loaded", "const_ready", "idents", "edges_in", "edge_rows", "edge_ps", "edge_cols"))
        zeros_ready, tables_zero = sem("zeros_ready"), sem("tables_zero")
        attr_in = [sem(f"attr_in{h}") for h in range(2)]
        dup_ready, dst_ready, diff_ready, sq_ready = (
            sem(n) for n in ("dup_ready", "dst_ready", "diff_ready", "sq_ready"))
        src_staged, src_bc, eq_ready, seg_summed, sums_ready, idx_ready = (
            sem(n) for n in ("src_staged", "src_bc", "eq_ready", "seg_summed", "sums_ready", "idx_ready"))
        scat = [sem(f"scat{r}") for r in range(NTAB)]
        oh_ready, deg_mm, deg_added = sem("oh_ready"), sem("deg_mm"), sem("deg_added")
        x_in, xn_ready, xT_ps, xT_ready, xn_out, xnT_out = (
            sem(n) for n in ("x_in", "xn_ready", "xT_ps", "xT_ready", "xn_out", "xnT_out"))
        kv_proj, kmin_ready, kexp_ready, phi_ready, kv_mm, kv_added, bd_ready = (
            sem(n) for n in ("kv_proj", "kmin_ready", "kexp_ready", "phi_ready", "kv_mm", "kv_added", "bd_ready"))
        xT2_in, xn2_in, x2_in, q_mm, qp_ready, qm_ready, qe_ready, qphi_ready = (
            sem(n) for n in ("xT2_in", "xn2_in", "x2_in", "q_mm", "qp_ready", "qm_ready", "qe_ready", "qphi_ready"))
        nd_mm, o_ready, o_mm, y1_ready, y1T_ps, y1T_ready, h_mm, relu_ready, z_mm, mix_ready, mix_out = (
            sem(n) for n in ("nd_mm", "o_ready", "o_mm", "y1_ready", "y1T_ps", "y1T_ready", "h_mm",
                             "relu_ready", "z_mm", "mix_ready", "mix_out"))
        dinv_ready, count_mm, tab_ready = sem("dinv_ready"), sem("count_mm"), sem("tab_ready")
        part_in, xTg_in, part_ready, pT_ps, pT_ready, e_mm, e_ready, eT_ready, c_mm, gb_ready, g_out_s, b_out_s = (
            sem(n) for n in ("part_in", "xTg_in", "part_ready", "pT_ps", "pT_ready", "e_mm", "e_ready",
                             "eT_ready", "c_mm", "gb_ready", "g_stored", "base_stored"))
        f_in = sem("f_in")
        wst_in = [sem(f"wst_in{n}") for n in range(2)]
        whi_ready, wlo_ready = sem("whi_ready"), sem("wlo_ready")
        f_out = [sem(f"f_out{n}") for n in range(2)]
        gat = [sem(f"gat{j}") for j in range(4)]
        gidx_ready, pool_mark = sem("gidx_ready"), sem("pool_mark")
        dstl_ready, oneh_ready, agg_tile, agg_done, agg_read = (
            sem(n) for n in ("dstl_ready", "oneh_ready", "agg_tile", "agg_done", "agg_read"))
        base_in, mixr_in, nodein_read, xl_ready, xlT_ps, xlThi_ready, xlTlo_ready = (
            sem(n) for n in ("base_in", "mixr_in", "nodein_read", "xl_ready", "xlT_ps", "xlThi_ready", "xlTlo_ready"))
        gate_mm, mask_ready, maskT_ps, maskT_ready, bias_mm, acc_ready = (
            sem(n) for n in ("gate_mm", "mask_ready", "maskT_ps", "maskT_ready", "bias_mm", "acc_ready"))
        up_mm, gelu_ready, lo_ready, dn_mm, comb_done, stored = (
            sem(n) for n in ("up_mm", "gelu_ready", "lo_ready", "dn_mm", "comb_done", "stored"))

        attr_pm = A["edge_attr_64"].rearrange("(p t) f -> p t f", p=P)
        block = ctx.enter_context(nc.Block())

        @block.sync
        def _(sp):
            n = [0]

            def load(dst, src):
                sp.dma_start(dst, src).then_inc(loaded, 16)
                n[0] += 16

            sp.dma_start(raw_i[:], A["src"].rearrange("(p t) -> p t", p=P)).then_inc(edges_in, 16)
            for n_, name in enumerate(("dst", "src")):
                sp.dma_start(edge_in[n_], A[name].rearrange("(c r q) -> r c q", c=8, q=P)).then_inc(edges_in, 16)
            load(w_kv[:, :, 0:D], A["L0_mix_Wk"].rearrange("(k p) n -> p k n", p=P))
            load(w_kv[:, :, D:], A["L0_mix_Wv"].rearrange("(k p) n -> p k n", p=P))
            load(w_q[:], A["L0_mix_Wq"].rearrange("(k p) n -> p k n", p=P))
            load(w_o[:], A["L0_mix_Wo"].rearrange("(k p) n -> p k n", p=P))
            load(w_1[:], A["L0_mix_W1"].rearrange("(k p) n -> p k n", p=P))
            load(w_2[:], A["L0_mix_W2"].rearrange("(k p) n -> p k n", p=P))
            load(w_cr[:, :, 0:D], A["L0_gnn_W_conv"].rearrange("(k p) n -> p k n", p=P))
            load(w_cr[:, :, D:], A["L0_gnn_W_res"].rearrange("(k p) n -> p k n", p=P))
            load(w_e[:], A["L0_gnn_W_edge"])
            load(w_g[:], A["L0_ffn_Wg"].rearrange("(k p) n -> p k n", p=P))
            for b, name in (("bk", "L0_mix_bk"), ("bv", "L0_mix_bv"), ("bo", "L0_mix_bo"), ("b2", "L0_mix_b2"),
                            ("g1", "L0_mix_ln1_g"), ("c1", "L0_mix_ln1_b"), ("g2", "L0_mix_ln2_g"),
                            ("c2", "L0_mix_ln2_b"), ("bc", "L0_gnn_b_conv"), ("br", "L0_gnn_b_res")):
                load(bc[b][:], A[name].unsqueeze(0).to_broadcast([P, D]))
            load(bg_bc[:], A["L0_ffn_bg"].unsqueeze(0).to_broadcast([P, NEXP]))
            with nc.allow_non_contiguous_dma(reason="small bias columns"):
                load(bq_c[:], A["L0_mix_bq"].rearrange("(k p) -> p k", p=P))
                load(b1_c[:], A["L0_mix_b1"].rearrange("(k p) -> p k", p=P))
                load(be_c[:], A["L0_gnn_b_edge"].rearrange("(p k) -> p k", k=1))
                load(fb1_c[:], A["L0_ffn_b1"].rearrange("e (k p) -> p (e k)", p=P))
            load(fb2[:], A["L0_ffn_b2"])
            assert n[0] == LOADS
            sp.wait_ge(zeros_ready, 1)
            for t in table:
                sp.dma_start(t.rearrange("(p n) f -> p (n f)", p=P), stage[:, 0:TROWS // P * EF]).then_inc(tables_zero, 16)

            def pass1_loads(i, tiles):
                wait(sp, xn_ready, i)
                sp.dma_start(xg[:, 0:tiles] if tiles > 1 else xg[:, 0, :],
                             rows(A["x"], i * GRP, tiles)).then_inc(x_in, 16)

            def attr_load(i, h):
                wait(sp, seg_summed, 4 * i - 4 + 2 * h + 2)
                sp.dma_start(attr[:, h], attr_pm[:, bass.ds(i * CH + 8 * h, 8), :]).then_inc(attr_in[h], 16)

            def pass2_loads(b, i=None):
                wait(sp, q_mm, b)
                sp.dma_start(xT2[:].rearrange("p k r -> p (k r)"), rows(xnT_d, b)).then_inc(xT2_in, 16)
                if i is not None:
                    attr_load(i, 0)
                wait(sp, y1_ready, b)
                sp.dma_start(xn2[:], rows(xn_d, b)).then_inc(xn2_in, 16)
                if i is not None:
                    attr_load(i, 1)
                wait(sp, mix_ready, b)
                sp.dma_start(x2[:], rows(A["x"], b)).then_inc(x2_in, 16)

            def first_loads(i):
                for h in range(2):
                    attr_load(i, h)
                    pass1_loads(2 * i + h, GRP)

            def weight_loads(e):
                for n, name, k in ((0, "L0_ffn_W1", KD), (1, "L0_ffn_W2", KH)):
                    wait(sp, wlo_ready, 2 * e + n - 1)
                    sp.dma_start(wst[:, n].rearrange("p (k n) -> p k n", k=k),
                                 A[name][bass.ds(e, 1)].rearrange("o (k p) n -> p (o k) n", p=P)).then_inc(wst_in[n], 16)

            first_loads(0)
            with sp.Fori(1, NF) as i:
                first_loads(i)
            pass1_loads(NG, 1)
            sp.wait_ge(xn_out, 16 * (NG + 1))
            sp.wait_ge(xnT_out, 16 * (NG + 1))
            pass2_loads(0, NF)
            pass2_loads(1, NF + 1)
            weight_loads(0)
            with sp.Fori(NF + 2, NF + NEXP + 1) as i:
                pass2_loads(i - NF, i)
                weight_loads(i - NF - 1)
            with sp.Fori(NF + NEXP + 1, NCH) as i:
                pass2_loads(i - NF, i)
            with sp.Fori(NCH - NF, NT) as b:
                pass2_loads(b)
            for s in scat:
                sp.wait_ge(s, 16 * ET // NTAB)

            def gcn_loads(i):
                wait(sp, part_ready, i)
                for r in range(NTAB):
                    sp.dma_start(part4[:, r], rows(table[r], i * BG, BG)).then_inc(part_in, 16)
                wait(sp, c_mm, BG * i)
                sp.dma_start(xT_g.rearrange("p n k r -> p n (k r)"), rows(xnT_d, i * BG, BG)).then_inc(xTg_in, 16)

            gcn_loads(0)
            with sp.Fori(1, NT // BG) as i:
                gcn_loads(i)

            assert NEXP <= RQ
            sp.wait_ge(g_out_s, 16 * (NT // BG))
            sp.wait_ge(b_out_s, 16 * (NT // BG))
            sp.wait_ge(mix_out, 16 * NT)
            for s in f_out:
                sp.wait_ge(s, 32 * NEXP)

            def tile_loads(b):
                wait(sp, nodein_read, b)
                sp.dma_start(base_t[:], rows(base_d, b)).then_inc(base_in, 16)
                sp.dma_start(mix_t[:], rows(mix_d, b)).then_inc(mixr_in, 16)

            def store(g, tiles):
                wait(sp, comb_done, NEXP * g + NEXP)
                sp.dma_start(rows(out, g * GRP, tiles), acc[:, 0:tiles] if tiles > 1 else acc[:, 0, :]).then_inc(stored, 16)

            tile_loads(0)
            for e in range(NEXP):
                wait(sp, gat[3], 16 * e)
                for part_ in range(2):
                    for t, w in enumerate((f_1, f_2)):
                        sp.dma_start(w[part_][:, e].bitcast(F32), f_d[part_][2 * e + t]).then_inc(f_in, 16)
            for t in range(1, GRP):
                tile_loads(t)
            with sp.Fori(0, NG - 1) as g:
                for t in range(GRP):
                    tile_loads(g * GRP + GRP + t)
                store(g, GRP)
            tile_loads(NT - 1)
            store(NG - 1, GRP)
            store(NG, 1)
            sp.wait_ge(stored, 16 * (NG + 1))

        @block.gpsimd
        def _(pool):
            g = nc.gpsimd
            g.memset(ones[:], 1.0).then_inc(idents, 1)
            g.memset(zero_bf[:], 0.0).then_inc(idents, 1)
            g.iota(raw_iota[:], pattern=[[1, P]], base=0, channel_multiplier=0).then_inc(idents, 1)
            g.iota(raw_iotb[:], pattern=[[P, NT]], base=0, channel_multiplier=0).then_inc(idents, 1)
            g.iota(raw_iotq[:], pattern=[[1, QUADS]], base=0, channel_multiplier=0).then_inc(idents, 1)
            g.iota(raw_iotp[:], pattern=[[0, 1]], base=NP, channel_multiplier=1).then_inc(idents, 1)
            pool.wait_ge(idents, 6)
            g.affine_select(out=before[:], in_=ones[:], compare_op=ALU.is_gt, fill=0.0, base=0,
                            pattern=[[1, P]], channel_multiplier=-1).then_inc(idents, 1)
            g.affine_select(out=ident[:], in_=ones[:], compare_op=ALU.is_equal, fill=0.0, base=0,
                            pattern=[[-1, P]], channel_multiplier=1).then_inc(idents, 1)

            def alone(s, value):
                if isinstance(value, int):
                    return wait(pool, s, value)
                pool.wait_ge(s, value)
                pool.sem_inc(pool_mark, 1)

            def differences(i):
                c0 = i * CH
                alone(sq_ready, i)
                g.tensor_tensor(diff_r[:], iota_bf[:].unsqueeze(1).to_broadcast([P, CH, P]),
                                dst_r[:, bass.ds(c0, CH)].unsqueeze(2).to_broadcast([P, CH, P]), ALU.subtract).then_inc(diff_ready, 1)
                g.tensor_tensor(diff_b[:], iota_bf[:, 0:NT].unsqueeze(1).to_broadcast([P, CH, NT]),
                                dst_b[:, bass.ds(c0, CH)].unsqueeze(2).to_broadcast([P, CH, NT]), ALU.subtract).then_inc(diff_ready, 1)

            def scatter_chunk(i, following=True):
                for h in range(2):
                    if h and following:
                        differences(i + 1)
                    alone(idx_ready, 2 * i + h + 1)
                    for j in range(8):
                        if j % 4 == 0:
                            alone(sums_ready, 4 * i + 2 * h + j // 4 + 1)
                        alone(scat[j % NTAB], 16 * (4 * i + 2 * h + j // 4))
                        g.indirect_dma_start(
                            out=table[j % NTAB],
                            out_offset=bass.IndirectOffsetOnAxis(ap=idx_st[:, 8 * h + j:8 * h + j + 1], axis=0),
                            in_=sums[:, h, j, :], in_offset=None, bounds_check=TROWS - 1,
                            compute_op=ALU.add).then_inc(scat[j % NTAB], 16)

            pool.wait_ge(tables_zero, 16 * NTAB)
            pool.wait_ge(dst_ready, 1)
            differences(0)
            scatter_chunk(0)
            with pool.Fori(1, NCH - 1) as i:
                scatter_chunk(i)
            scatter_chunk(NCH - 1, following=False)

            pool.wait_ge(tab_ready, 1)
            pool.wait_ge(g_out_s, 16 * (NT // BG))
            pool.wait_ge(b_out_s, 16 * (NT // BG))

            def gather(i):
                for h in range(2):
                    for jj in range(4):
                        alone(gat[jj], 16 * (RQ * i - RQ + RQ // 2 * (h + 1)))
                    g.tensor_copy(gidx[:, h], src_t[:, bass.ds(i * 4 * RQ + 2 * RQ * h, 2 * RQ)]).then_inc(gidx_ready, 1)
                    alone(gidx_ready, 2 * i + h + 1)
                    for k in range(RQ // 2 * h, RQ // 2 * (h + 1)):
                        q = RQ * i + k
                        if not isinstance(i, int):
                            alone(agg_tile, pool.value_load(needtab[0:1, bass.ds(q, 1)], min_val=4, max_val=4 * (QUADS + NT) + 4))
                        for jj in range(4):
                            alone(gat[jj], 16 * q)
                            s = 4 * (k - RQ // 2 * h) + jj
                            g.indirect_dma_start(
                                out=ring[:, (4 * k + jj) * D:(4 * k + jj + 1) * D], out_offset=None,
                                in_=g_d, in_offset=bass.IndirectOffsetOnAxis(ap=gidx[:, h, s:s + 1], axis=0),
                            ).then_inc(gat[jj], 16)

            gather(0)
            with pool.Fori(1, QUADS // RQ) as i:
                gather(i)

        @block.tensor
        def _(pe):
            T = nc.tensor

            def mm(o, l, r, first, last):
                return T.matmul(o, l, r, start=first, stop=last)

            pe.wait_ge(idents, 8)
            for t in range(2):
                for c in range(8):
                    k = 8 * t + c
                    wait(pe, edge_cols, k - 1)
                    pe.wait_ge(edge_rows, k + 1)
                    T.transpose(psT[k % 2][:, 0:TC], edge_f[:, k % 2, :], ident[0:TC, 0:TC]).then_inc(edge_ps, 1)

            pe.wait_ge(loaded, LOADS)

            def src_rows(i, k):
                wait(pe, src_staged, i + 1)
                wait(pe, eq_ready, 4 * i + k - 1)
                for j in range(4):
                    ins = T.transpose(psT[k % 2][:, j * P:(j + 1) * P],
                                      src_st[:, 4 * k + j:4 * k + j + 1].to_broadcast([P, P]), ident[:])
                ins.then_inc(src_bc, 1)

            def seg_sum(i, k):
                if k % 2 == 0:
                    wait(pe, attr_in[k // 2], 16 * (i + 1))
                wait(pe, dup_ready, 4 * i + k + 1)
                wait(pe, sums_ready, 4 * i + k)
                for j in range(4):
                    mm(ps2[:, j * EF:(j + 1) * EF], eq[:, k % 2, j, :], attr[:, k // 2, 4 * (k % 2) + j, :], True, True)
                    ins = mm(ps2[:, 4 * EF + j:4 * EF + j + 1], dup[:, k % 2, j, :], one_bf[:], True, True)
                ins.then_inc(seg_summed, 1)

            def degrees(i):
                wait(pe, oh_ready, i + 1)
                wait(pe, deg_added, i)
                for t in range(CH):
                    ins = mm(ps5[:, 0:NT], oh_r[:, t, :], oh_b[:, t, :], t == 0, t == CH - 1)
                ins.then_inc(deg_mm, 1)

            def pass1(i, tiles, c=None, k=0):
                def turn(j):
                    wait(pe, xT_ready, GRP * i + j - 1)
                    for k in range(KD):
                        ins = T.transpose([ps6, ps7][j % 2][:, k * P:(k + 1) * P],
                                          xng[:, j, k * P:(k + 1) * P], ident[:])
                    ins.then_inc(xT_ps, 1)

                def project(j):
                    wait(pe, xT_ready, GRP * i + j + 1)
                    wait(pe, kmin_ready, GRP * i + j)
                    for k in range(KD):
                        ins = mm(ps3[:, 0:512], xT_st[:, j, k, :], w_kv[:, k, :], k == 0, k == KD - 1)
                    ins.then_inc(kv_proj, 1)

                def kv(j):
                    n = P if tiles > 1 else LAST
                    wait(pe, phi_ready, GRP * i + j + 1)
                    wait(pe, kv_added, GRP * i + j)
                    for c in range(KD):
                        ins = mm(ps4[:, c * (P + 1):(c + 1) * (P + 1)], kb[0:n, j % 2, c * P:(c + 1) * P],
                                 va[0:n, j % 2, c, :], True, True)
                    ins.then_inc(kv_mm, 1)

                if c is not None:
                    src_rows(c, k)
                    if k == 0:
                        degrees(c)
                wait(pe, xn_ready, i + 1)
                turn(0)
                for j in range(tiles):
                    if j + 1 < tiles:
                        turn(j + 1)
                    project(j)
                    if j:
                        kv(j - 1)
                    if c is not None and j == 0:
                        src_rows(c, k + 1)
                    if c is not None and j == 1:
                        seg_sum(c, k)
                kv(tiles - 1)
                if c is not None:
                    seg_sum(c, k + 1)

            def hidden(b, half):
                wait(pe, y1T_ready, b + 1)
                for m in range(4 * half, 4 * half + 4):
                    for k in range(KD):
                        ins = mm([ps6, ps7][half][:, (m % 4) * P:(m % 4 + 1) * P], w_1[:, k, m * P:(m + 1) * P],
                                 y1T[:, k, :], k == 0, k == KD - 1)
                ins.then_inc(h_mm, 1)

            def down(b, i):
                wait(pe, mix_ready, b)
                wait(pe, deg_added, i + 1)
                for m in range(KF):
                    if m % 4 == 0:
                        wait(pe, relu_ready, 2 * b + m // 4 + 1)
                    ins = mm(ps5[:, D:2 * D], hT[:, m, :], w_2[:, m, :], m == 0, m == KF - 1)
                ins.then_inc(z_mm, 1)

            def pass2(b, i=None):
                wait(pe, xT2_in, 16 * (b + 1))
                wait(pe, y1_ready, b)
                for m in range(KD):
                    for k in range(KD):
                        ins = mm(ps3[:, m * P:(m + 1) * P], w_q[:, k, m * P:(m + 1) * P], xT2[:, k, :], k == 0, k == KD - 1)
                ins.then_inc(q_mm, 1)
                if i is not None:
                    src_rows(i, 0)
                    src_rows(i, 1)
                if not isinstance(b, int) or b:
                    hidden(b - 1, 0)
                wait(pe, qphi_ready, b + 1)
                for m in range(KD):
                    mm(ps4[:, m * P:(m + 1) * P], kv_bd[:, m, :], qp[:, m, :], True, True)
                    ins = mm(ps4[:, D + m * P:D + (m + 1) * P], ks_bd[:, m, :], qp[:, m, :], True, True)
                ins.then_inc(nd_mm, 1)
                if not isinstance(b, int) or b:
                    hidden(b - 1, 1)
                    down(b - 1, i - 1 if i is not None else NCH - 1)
                if i is not None:
                    seg_sum(i, 0)
                    src_rows(i, 2)
                wait(pe, o_ready, b + 1)
                for k in range(KD):
                    ins = mm(ps3[:, D:2 * D], on[:, k, :], w_o[:, k, :], k == 0, k == KD - 1)
                ins.then_inc(o_mm, 1)
                if i is not None:
                    seg_sum(i, 1)
                    src_rows(i, 3)
                    seg_sum(i, 2)
                    seg_sum(i, 3)
                    wait(pe, mix_ready, b)
                    degrees(i)
                wait(pe, y1_ready, b + 1)
                for k in range(KD):
                    ins = T.transpose(ps4[:, k * P:(k + 1) * P], y1[:, k * P:(k + 1) * P], ident[:])
                ins.then_inc(y1T_ps, 1)

            def first_step(i):
                for h in range(2):
                    pass1(2 * i + h, GRP, i, 2 * h)

            first_step(0)
            with pe.Fori(1, NF) as i:
                first_step(i)
            pass1(NG, 1)
            pe.wait_ge(bd_ready, 1)
            pass2(0, NF)
            pass2(1, NF + 1)
            with pe.Fori(NF + 2, NCH) as i:
                pass2(i - NF, i)
            with pe.Fori(NCH - NF, NT) as b:
                pass2(b)
            for half in range(2):
                hidden(NT - 1, half)
            down(NT - 1, NCH - 1)
            pe.wait_ge(deg_added, NCH)
            pe.wait_ge(mix_ready, NT)
            mm(ps5[:, 0:NT], ones[:], deg[:], True, True).then_inc(count_mm, 1)

            def gcn(i):
                def turn(j):
                    wait(pe, pT_ready, BG * i + j)
                    T.transpose(ps5[:, 0:P], part[:, j, :], ident[:]).then_inc(pT_ps, 1)

                def edge_mlp(j):
                    wait(pe, pT_ready, BG * i + j + 1)
                    wait(pe, e_ready, BG * i + j)
                    mm(ps4[:, 0:P], w_e[:], partT[0:EF, :], True, True).then_inc(e_mm, 1)

                wait(pe, part_ready, i + 1)
                turn(0)
                edge_mlp(0)
                wait(pe, xTg_in, 16 * (i + 1))
                for j in range(BG):
                    t = BG * i + j
                    y = [ps6, ps7][j % 2]
                    if j + 1 < BG:
                        turn(j + 1)
                    wait(pe, gb_ready, t - min(j, 1))
                    for k in range(KD):
                        mm(y[:], xT_g[:, j, k, :], w_cr[:, k, :], k == 0, False)
                    if j + 1 < BG:
                        edge_mlp(j + 1)
                    wait(pe, eT_ready, t + 1)
                    mm(y[:], eT[:, j % 2], w_cr[:, KD, :], False, True).then_inc(c_mm, 1)

            pe.wait_ge(tab_ready, 1)
            gcn(0)
            with pe.Fori(1, NT // BG) as i:
                gcn(i)

            pe.sem_inc(agg_tile, 4)

            def quads_of(b):
                return [pe.value_load(qtab[0:1, bass.ds(b + n, 1)], min_val=0, max_val=QUADS - 1) for n in range(2)]

            def aggregate(b, lo, hi):
                wait(pe, agg_read, b)
                mm(ps0[:, 0:D], zero_bf[:, 0:P], zero_bf[:, 0:D], True, False)
                with pe.Fori(lo, hi + 1) as q:
                    for jj in range(4):
                        pe.wait_ge(oneh_ready, (q + b) * 4 + jj + 1)
                        pe.wait_ge(gat[jj], q * 16 + 16)
                        mm(ps0[:, 0:D], oh[:, jj, :], ring[:, bass.ds((q % RQ) * (4 * D) + jj * D, D)],
                           False, False).then_inc(agg_tile, 1)
                mm(ps0[:, 0:D], zero_bf[:, 0:P], zero_bf[:, 0:D], False, True).then_inc(agg_done, 1)

            THREE = ((0, 0), (1, 0), (0, 1))

            def experts(g, tiles, following):
                W = tiles * P
                wait(pe, xl_ready, GRP * g + tiles)
                wait(pe, comb_done, NEXP * g)
                for k in range(KD):
                    for r in range(tiles):
                        ins = T.transpose([ps2, ps3][k][:, r * P:(r + 1) * P], xl4[:, r, k * P:(k + 1) * P], ident[:])
                ins.then_inc(xlT_ps, 1)
                wait(pe, maskT_ready, g)

                def up(u):
                    e, m = u // KH, u % KH
                    wait(pe, gelu_ready, NEXP * KH * g + max(u - 1, 0))
                    for n, (a, b, k) in enumerate(((0, 0, 0), (1, 0, 0), (0, 0, 1), (1, 0, 1), (0, 1, 0), (0, 1, 1))):
                        if u == 0 and n in (0, 2):
                            wait(pe, xlThi_ready, KD * g + k + 1)
                        if u == 0 and n in (4, 5):
                            wait(pe, xlTlo_ready, KD * g + k + 1)
                        ins = mm([ps6, ps7][u % 2][:, 0:W], f_1[a][:, e, k * HID + m * P:k * HID + (m + 1) * P],
                                 xlT[b][:, k, 0:W], n == 0, n == 5)
                    ins.then_inc(up_mm, 1)

                def down(u):
                    e, m = u // KH, u % KH
                    wait(pe, gelu_ready, NEXP * KH * g + u + 1)
                    wait(pe, lo_ready, NEXP * KH * g + u + 1)
                    if m == 0:
                        wait(pe, comb_done, NEXP * g + max(e - 1, 0))
                        if e == 1:
                            wait(pe, acc_ready, g + 1)
                    for r in range(tiles):
                        y = [[ps2, ps3], [ps4, ps5]][e % 2][r // 2][:, (r % 2) * D:(r % 2 + 1) * D]
                        for n, (a, b) in enumerate(THREE):
                            ins = T.matmul(y, hhl[a][:, u % 2, r * P:(r + 1) * P], f_2[b][:, e, m * D:(m + 1) * D],
                                           start=m == 0 and n == 0 and r % 2 == 0, stop=m == KH - 1 and n == 2,
                                           skip_group_check=True)
                    ins.then_inc(dn_mm, 1)

                up(0)
                up(1)
                for r in range(tiles):
                    n = 0
                    for k in range(KD):
                        for a, b in THREE:
                            ins = mm(ps1[:, r * NEXP:(r + 1) * NEXP], xlT[a][:, k, r * P:(r + 1) * P],
                                     [wg_hi, wg_lo][b][:, k, :], n == 0, n == 5)
                            n += 1
                ins.then_inc(gate_mm, 1)
                for u in range(NEXP * KH):
                    insert = u in INSERT and INSERT.index(u) < following
                    if insert:
                        b = g * GRP + GRP + INSERT.index(u)
                        lo, hi = quads_of(b)
                    down(u)
                    if u + 2 < NEXP * KH:
                        up(u + 2)
                    if u == 1:
                        wait(pe, mask_ready, g + 1)
                        for r in range(tiles):
                            ins = T.transpose(ps1[0:NEXP, r * P:(r + 1) * P], mask[:, r, :], ident[:])
                        ins.then_inc(maskT_ps, 1)
                    if u == 2:
                        wait(pe, maskT_ready, g + 1)
                        for r in range(tiles):
                            ins = mm([ps4, ps5][r // 2][:, (r % 2) * D:(r % 2 + 1) * D], maskT[:, r * P:(r + 1) * P], fb2[:], True, True)
                        ins.then_inc(bias_mm, 1)
                    if insert:
                        aggregate(b, lo, hi)

            pe.wait_ge(dstl_ready, 1)
            for b in range(GRP):
                aggregate(b, *quads_of(b))
            pe.wait_ge(f_in, 64 * NEXP)
            experts(0, GRP, GRP)
            with pe.Fori(1, NG - 1) as g:
                experts(g, GRP, GRP)
            experts(NG - 1, GRP, 1)
            experts(NG, 1, 0)

        @block.scalar
        def _(act):
            S = nc.scalar
            act.wait_ge(loaded, LOADS)
            act.wait_ge(const_ready, 1)

            def squares(i):
                wait(act, diff_ready, 2 * i + 2)
                S.activation(sq_r[:], diff_r[:], ACT.Square)
                S.activation(sq_b[:], diff_b[:], ACT.Square).then_inc(sq_ready, 1)

            def onehot_dst(i):
                wait(act, deg_mm, i)
                wait(act, sq_ready, i + 1)
                S.activation(oh_r[:], sq_r[:], ACT.Relu, bias=ones[:, 0:1], scale=-1.0)
                S.activation(oh_b[:], sq_b[:], ACT.Relu, bias=ones[:, 0:1], scale=-1.0).then_inc(oh_ready, 1)

            def quad(i, k):
                h = k // 2
                if k % 2 == 0:
                    for s in scat:
                        wait(act, s, 16 * (4 * i - 4 + 2 * h + 2))
                    wait(act, idx_ready, 2 * i - 1 + h)
                wait(act, seg_summed, 4 * i + k + 1)
                S.copy(sums[:, h, 4 * (k % 2):4 * (k % 2) + 4, :],
                       ps2[:, 0:4 * EF].rearrange("p (j f) -> p j f", j=4))
                S.copy(cnt[:, 4 * k:4 * k + 4], ps2[:, 4 * EF:4 * EF + 4]).then_inc(sums_ready, 1)

            def pass1(i, tiles, c=None, q=0):
                def turned(j):
                    if j == 0:
                        wait(act, xnT_out, 16 * i)
                    wait(act, xT_ps, GRP * i + j + 1)
                    S.copy(xT_st[:, j].rearrange("p k r -> p (k r)"), [ps6, ps7][j % 2][:, 0:D]).then_inc(xT_ready, 1)

                turned(0)
                for j in range(tiles):
                    if j + 1 < tiles:
                        turned(j + 1)
                    wait(act, kmin_ready, GRP * i + j + 1)
                    S.activation(ke[:, j % 2, :], ke[:, j % 2, :], ACT.Exp).then_inc(kexp_ready, 1)
                    if c is not None and j == 1:
                        quad(c, q)
                if c is not None:
                    quad(c, q + 1)
                wait(act, xT_ready, GRP * i + tiles)
                act.dma_start(rows(xn_d, i * GRP, tiles), xng[:, 0:tiles] if tiles > 1 else xng[:, 0, :]).then_inc(xn_out, 16)
                act.dma_start(rows(xnT_d, i * GRP, tiles),
                              xT_st[:].rearrange("p n k r -> p n (k r)") if tiles > 1
                              else xT_st[:, 0].rearrange("p k r -> p (k r)")).then_inc(xnT_out, 16)

            def hidden(b):
                for m in range(KF):
                    if m % 4 == 0:
                        wait(act, h_mm, 2 * b + m // 4 + 1)
                    ins = S.activation(hT[:, m, :], [ps6, ps7][m // 4][:, (m % 4) * P:(m % 4 + 1) * P], ACT.Relu,
                                       bias=b1_c[:, m:m + 1])
                    if m % 4 == 3:
                        ins.then_inc(relu_ready, 1)

            def store(b):
                wait(act, mix_ready, b + 1)
                act.dma_start(rows(mix_d, b), mixo[:]).then_inc(mix_out, 16)

            def pass2(b, i=None):
                wait(act, qm_ready, b + 1)
                for m in range(KD):
                    ins = S.activation(qp[:, m, :], ps3[:, m * P:(m + 1) * P], ACT.Relu, bias=bq_c[:, m:m + 1])
                ins.then_inc(qp_ready, 1)
                S.activation(qm[:], qm[:], ACT.Exp).then_inc(qe_ready, 1)
                if not isinstance(b, int) or b:
                    hidden(b - 1)
                if i is not None:
                    squares(i)
                    quad(i, 0)
                    quad(i, 1)
                    onehot_dst(i)
                    quad(i, 2)
                    quad(i, 3)
                if not isinstance(b, int) or b:
                    store(b - 1)
                wait(act, y1T_ps, b + 1)
                S.copy(y1T[:].rearrange("p k r -> p (k r)"), ps4[:, 0:D]).then_inc(y1T_ready, 1)

            def first_step(i):
                squares(i)
                onehot_dst(i)
                for h in range(2):
                    pass1(2 * i + h, GRP, i, 2 * h)

            def split_weights(e):
                for n in range(2):
                    wait(act, wst_in[n], 16 * (e + 1))
                    wait(act, f_out[n], 32 * e)
                    S.copy(whi[:, n], wst[:, n]).then_inc(whi_ready, 1)
                for n in range(2):
                    row = bass.ds(2 * e + n, 1)
                    wait(act, whi_ready, 2 * e + 2)
                    act.dma_start(f_d[0][row].rearrange("o p n -> (o p) n"), whi[:, n].bitcast(F32)).then_inc(f_out[n], 16)
                    wait(act, wlo_ready, 2 * e + n + 1)
                    act.dma_start(f_d[1][row].rearrange("o p n -> (o p) n"), wlo[:, n].bitcast(F32)).then_inc(f_out[n], 16)

            first_step(0)
            with act.Fori(1, NF) as i:
                first_step(i)
            pass1(NG, 1)
            pass2(0, NF)
            pass2(1, NF + 1)
            split_weights(0)
            with act.Fori(NF + 2, NF + NEXP + 1) as i:
                pass2(i - NF, i)
                split_weights(i - NF - 1)
            with act.Fori(NF + NEXP + 1, NCH) as i:
                pass2(i - NF, i)
            with act.Fori(NCH - NF, NT) as b:
                pass2(b)
            hidden(NT - 1)
            store(NT - 1)

            def gcn(i):
                for j in range(BG):
                    t = BG * i + j
                    wait(act, pT_ps, t + 1)
                    wait(act, e_mm, t)
                    S.copy(partT[:], ps5[:, 0:P]).then_inc(pT_ready, 1)
                    wait(act, e_mm, t + 1)
                    wait(act, eT_ready, t)
                    S.activation(e1[:], ps4[:, 0:P], ACT.Identity, bias=be_c[:, 0:1]).then_inc(e_ready, 1)
                wait(act, gb_ready, BG * i + BG)
                act.dma_start(rows(g_d, i * BG, BG), g_st[:]).then_inc(g_out_s, 16)
                act.dma_start(rows(base_d, i * BG, BG), b_out).then_inc(b_out_s, 16)

            gcn(0)
            with act.Fori(1, NT // BG) as i:
                gcn(i)

            act.wait_ge(g_out_s, 16 * (NT // BG))
            act.wait_ge(b_out_s, 16 * (NT // BG))

            def experts(g, tiles):
                W = tiles * P
                wait(act, xlT_ps, g + 1)
                for k in range(KD):
                    S.copy(xlT[0][:, k, 0:W], [ps2, ps3][k][:, 0:W]).then_inc(xlThi_ready, 1)
                for u in range(NEXP * KH):
                    v = NEXP * KH * g + u
                    wait(act, up_mm, v + 1)
                    wait(act, dn_mm, v - min(u, 1))
                    wait(act, lo_ready, v)
                    for o in (hf[:, 0:W], hhl[0][:, u % 2, 0:W]):
                        ins = S.activation(o, [ps6, ps7][u % 2][:, 0:W], ACT.Gelu, bias=fb1_c[:, u:u + 1])
                    ins.then_inc(gelu_ready, 1)
                    if u == 3:
                        wait(act, maskT_ps, g + 1)
                        wait(act, stored, 16 * g)
                        S.copy(maskT[:, 0:W], ps1[0:NEXP, 0:W]).then_inc(maskT_ready, 1)

            experts(0, GRP)
            with act.Fori(1, NG) as g:
                experts(g, GRP)
            experts(NG, 1)

        @block.vector
        def _(dve):
            V = nc.vector

            def rsqrt(result, v, n, eps):
                a, y, t = rs[:, 0, 0:n], rs[:, 1, 0:n], rs[:, 2, 0:n]
                half = rs_i[:, 0:n]
                V.tensor_scalar(a, v, float(eps), None, ALU.add)
                dve.drain()
                V.tensor_single_scalar(half, a.bitcast(I32), 1, op=ALU.arith_shift_right)
                dve.drain()
                V.tensor_scalar(a, a, -0.5, None, ALU.mult)
                V.tensor_scalar(y.bitcast(I32), half, -1.0, float(0x5F3759DF), ALU.mult, ALU.add)
                dve.drain()
                for step in range(3):
                    if n == 1:
                        V.tensor_scalar(t, y, y, a, ALU.mult, ALU.mult)
                    else:
                        V.tensor_tensor(t, y, y, ALU.mult)
                        dve.drain()
                        V.tensor_tensor(t, t, a, ALU.mult)
                    dve.drain()
                    V.scalar_tensor_tensor(out=result if step == 2 else y, in0=t, scalar=1.5, in1=y,
                                           op0=ALU.add, op1=ALU.mult)
                    dve.drain()

            def normalise(dst, src):
                V.bn_stats(stats[:, 0, :], src)
                dve.drain()
                V.bn_aggr(mv[:, 0, :], stats[:, 0, :])
                dve.drain()
                rsqrt(rs[:, 3, 0:1], mv[:, 0, 1:2], 1, LN_EPS)
                return V.tensor_scalar(dst, src, mv[:, 0, 0:1], rs[:, 3, 0:1], ALU.subtract, ALU.mult)

            dve.wait_ge(idents, 8)
            V.memset(stage[:, 0:TROWS // P * EF], 0.0).then_inc(zeros_ready, 1)
            V.memset(headmask[:], 0.0)
            dve.drain()
            for h in range(P // HEAD):
                s = slice(HEAD * h, HEAD * h + HEAD)
                V.memset(headmask[s, s], 1.0)
            V.tensor_copy(iota_r[:], raw_iota[:])
            V.tensor_scalar(node0[:], raw_iotb[:], -1.0, None, ALU.mult)
            V.tensor_copy(iota_q[:], raw_iotq[:])
            V.tensor_copy(trash[:], raw_iotp[:])
            V.tensor_copy(iota_bf[:], raw_iota[:])
            V.memset(one_bf[:], 1.0)
            V.memset(deg[:], 0.0)
            V.memset(kv_acc[:], 0.0)
            V.memset(part[:], 0.0)
            V.memset(va[:], 1.0)
            V.memset(qtab[:], 0)
            dve.wait_ge(edges_in, 48)
            V.tensor_copy(src_pm[:], raw_i[:])
            for t in range(2):
                for c in range(8):
                    k = 8 * t + c
                    wait(dve, edge_ps, k - 1)
                    V.tensor_copy(edge_f[:, k % 2, :], edge_in[t][:, c, :]).then_inc(edge_rows, 1)
                    dve.wait_ge(edge_ps, k + 1)
                    cols = slice(c * TC, (c + 1) * TC)
                    if t == 0:
                        V.tensor_copy(dst_t[:, cols], psT[k % 2][:, 0:TC]).then_inc(edge_cols, 1)
                    else:
                        V.tensor_scalar(src_t[:, cols], psT[k % 2][:, 0:TC], float(NP - 1), None,
                                        ALU.min).then_inc(edge_cols, 1)
            dve.drain()
            raw2 = raw_i[:]
            V.tensor_copy(raw2, dst_t[:])
            dve.drain()
            V.tensor_single_scalar(raw2, raw2, 7, op=ALU.arith_shift_right)
            dve.drain()
            V.tensor_copy(dst_b[:], raw2)
            dve.drain()
            V.scalar_tensor_tensor(out=dst_r[:], in0=dst_b[:], scalar=-float(P), in1=dst_t[:], op0=ALU.mult,
                                   op1=ALU.add).then_inc(dst_ready, 1)
            dve.drain()
            dve.wait_ge(loaded, LOADS)
            V.tensor_tensor(bc["bc"][:], bc["bc"][:], bc["br"][:], ALU.add)
            V.tensor_copy(wg_hi[:], w_g[:])
            dve.drain()
            V.tensor_tensor(wg_lo[:], w_g[:], wg_hi[:].bitcast(F32), ALU.subtract)
            dve.drain()
            V.engine_nop().then_inc(const_ready, 1)

            def head(i):
                dve.drain()
                V.tensor_copy(src_st[:], src_pm[:, bass.ds(i * CH, CH)]).then_inc(src_staged, 1)

            def degrees(i):
                wait(dve, deg_mm, i + 1)
                V.tensor_tensor(deg[:], deg[:], ps5[:, 0:NT], ALU.add).then_inc(deg_added, 1)

            def quad(i, k):
                wait(dve, src_bc, 4 * i + k + 1)
                wait(dve, seg_summed, 4 * i + k - 1)
                V.tensor_tensor(eq[:, k % 2], psT[k % 2][:].rearrange("p (j e) -> p j e", j=4),
                                src_st[:, 4 * k:4 * k + 4].unsqueeze(2).to_broadcast([P, 4, P]),
                                ALU.is_equal).then_inc(eq_ready, 1)
                dve.drain()
                V.tensor_tensor(dup[:, k % 2], eq[:, k % 2], before[:].unsqueeze(1).to_broadcast([P, 4, P]),
                                ALU.mult).then_inc(dup_ready, 1)

            def index(i, h):
                s = slice(8 * h, 8 * h + 8)
                V.tensor_scalar(shift[:, h], src_st[:, s], -1.0, trash[:, 0:1], ALU.mult, ALU.add)
                wait(dve, sums_ready, 4 * i + 2 * h + 2)
                V.tensor_scalar(again[:, h], cnt[:, s], 1.0, None, ALU.min)
                dve.drain()
                V.tensor_tensor(shift[:, h], shift[:, h], again[:, h], ALU.mult)
                dve.drain()
                for q in scat:
                    wait(dve, q, 16 * (4 * i - 4 + 2 * h + 2))
                V.tensor_tensor(idx_st[:, s], src_st[:, s], shift[:, h], ALU.add).then_inc(idx_ready, 1)

            def pass1(i, tiles, c=None, q=0):
                wait(dve, x_in, 16 * (i + 1))
                for j in range(tiles):
                    V.bn_stats(stats[:, j, :], xg[:, j, :])
                dve.drain()
                for j in range(tiles):
                    V.bn_aggr(mv[:, j, :], stats[:, j, :])
                dve.drain()
                rsqrt(rs[:, 3, 0:tiles], mv[:, 0:tiles, 1], tiles, LN_EPS)
                wait(dve, xn_out, 16 * i)
                for j in range(tiles):
                    ins = V.tensor_scalar(xng[:, j, :], xg[:, j, :], mv[:, j, 0:1], rs[:, 3, j:j + 1], ALU.subtract, ALU.mult)
                ins.then_inc(xn_ready, 1)

                def front(j):
                    wait(dve, kv_proj, GRP * i + j + 1)
                    wait(dve, kv_mm, GRP * i + j - 1)
                    V.tensor_tensor(kb[:, j % 2], ps3[:, 0:D], bc["bk"][:], ALU.add)
                    V.tensor_tensor(va[:, j % 2, :, 0:P], ps3[:, D:].rearrange("p (c e) -> p c e", c=KD),
                                    bc["bv"][:].rearrange("p (c e) -> p c e", c=KD), ALU.add)
                    dve.drain()
                    V.tensor_scalar(ke[:, j % 2], kb[:, j % 2], 0.0, None, ALU.min).then_inc(kmin_ready, 1)

                def back(j):
                    wait(dve, kexp_ready, GRP * i + j + 1)
                    V.scalar_tensor_tensor(out=kb[:, j % 2], in0=kb[:, j % 2], scalar=0.0, in1=ke[:, j % 2],
                                           op0=ALU.max, op1=ALU.add).then_inc(phi_ready, 1)

                def add(j):
                    wait(dve, kv_mm, GRP * i + j + 1)
                    V.tensor_tensor(kv_acc[:], kv_acc[:], ps4[:, 0:KD * (P + 1)].rearrange("p (c e) -> p c e", c=KD),
                                    ALU.add).then_inc(kv_added, 1)

                front(0)
                for j in range(tiles):
                    if c is not None and j < 2:
                        quad(c, q + j)
                    back(j)
                    if j + 1 < tiles:
                        front(j + 1)
                    add(j)
                    dve.drain()
                if c is not None:
                    index(c, q // 2)

            def pass2(b, i=None):
                if i is not None:
                    head(i)
                wait(dve, q_mm, b + 1)
                for m in range(KD):
                    ins = V.tensor_scalar(qm[:, m, :], ps3[:, m * P:(m + 1) * P], bq_c[:, m:m + 1], 0.0, ALU.add, ALU.min)
                ins.then_inc(qm_ready, 1)
                if i is not None:
                    quad(i, 0)
                wait(dve, qe_ready, b + 1)
                wait(dve, qp_ready, b + 1)
                V.tensor_tensor(qp[:], qp[:], qm[:], ALU.add).then_inc(qphi_ready, 1)
                if i is not None:
                    quad(i, 1)
                wait(dve, nd_mm, b + 1)
                den = qm[:].rearrange("p k r -> p (k r)")
                V.tensor_scalar(den, ps4[:, D:2 * D], 1e-6, None, ALU.add)
                dve.drain()
                V.reciprocal(den, den)
                wait(dve, xn2_in, 16 * (b + 1))
                V.tensor_tensor(xn2[:], xn2[:], bc["bo"][:], ALU.add)
                dve.drain()
                V.tensor_tensor(on[:].rearrange("p k r -> p (k r)"), ps4[:, 0:D], den, ALU.mult).then_inc(o_ready, 1)
                if not isinstance(b, int) or b:
                    finish(b - 1)
                dve.drain()
                if i is not None:
                    quad(i, 2)
                    quad(i, 3)
                wait(dve, o_mm, b + 1)
                V.tensor_tensor(zt[:], ps3[:, D:2 * D], xn2[:], ALU.add)
                dve.drain()
                normalise(zt[:], zt[:])
                dve.drain()
                V.tensor_tensor(zt[:], zt[:], bc["g1"][:], ALU.mult)
                dve.drain()
                V.tensor_tensor(y1[:], zt[:], bc["c1"][:], ALU.add).then_inc(y1_ready, 1)
                dve.drain()
                V.tensor_tensor(zt[:], y1[:], bc["b2"][:], ALU.add)
                if i is not None:
                    index(i, 0)
                    index(i, 1)
                    degrees(i)
                dve.drain()

            def finish(b):
                wait(dve, z_mm, b + 1)
                V.tensor_tensor(zt[:], ps5[:, D:2 * D], zt[:], ALU.add)
                wait(dve, x2_in, 16 * (b + 1))
                V.tensor_tensor(x2[:], x2[:], bc["c2"][:], ALU.add)
                dve.drain()
                normalise(zt[:], zt[:])
                dve.drain()
                V.tensor_tensor(zt[:], zt[:], bc["g2"][:], ALU.mult)
                dve.drain()
                wait(dve, mix_out, 16 * b)
                V.tensor_tensor(mixo[:], zt[:], x2[:], ALU.add).then_inc(mix_ready, 1)

            def first_step(i):
                head(i)
                for h in range(2):
                    pass1(2 * i + h, GRP, i, 2 * h)
                degrees(i)

            def split_weights(e):
                for n in range(2):
                    wait(dve, whi_ready, 2 * e + n + 1)
                    wait(dve, f_out[n], 32 * e)
                    V.tensor_tensor(wlo[:, n], wst[:, n], whi[:, n].bitcast(F32), ALU.subtract).then_inc(wlo_ready, 1)

            first_step(0)
            with dve.Fori(1, NF) as i:
                first_step(i)
            pass1(NG, 1)
            for c in range(KD):
                V.tensor_tensor(kv_bd[:, c, :], kv_acc[:, c, 0:P], headmask[:], ALU.mult)
                ins = V.tensor_scalar(ks_bd[:, c, :], headmask[:], kv_acc[:, c, P:P + 1], None, ALU.mult)
            ins.then_inc(bd_ready, 1)
            pass2(0, NF)
            pass2(1, NF + 1)
            split_weights(0)
            with dve.Fori(NF + 2, NF + NEXP + 1) as i:
                pass2(i - NF, i)
                split_weights(i - NF - 1)
            with dve.Fori(NF + NEXP + 1, NCH) as i:
                pass2(i - NF, i)
            with dve.Fori(NCH - NF, NT) as b:
                pass2(b)
            finish(NT - 1)

            dve.drain()
            rsqrt(dinv[:], deg[:], NT, 1.0)
            dve.wait_ge(count_mm, 1)
            V.tensor_copy(cum_f[:], ps5[:, 0:NT])
            dve.drain()
            V.tensor_tensor_scan(cum[:], ones[:, 0:NT], cum_f[:], 0.0, ALU.mult, ALU.add)
            dve.drain()
            V.tensor_scalar(cum_i[:], cum[:], 1.0, -1.0, ALU.max, ALU.add)
            dve.drain()
            V.tensor_single_scalar(cum_i[:], cum_i[:], 9, op=ALU.arith_shift_right)
            dve.drain()
            V.tensor_copy(qtab[:, 1:NT + 1], cum_i[0:1, :])
            V.tensor_copy(qlast[:], cum_i[0:1, :])
            dve.drain()
            step = QUADS // 16
            wide = oh_r[0:1].rearrange("p t e -> p (t e)").bitcast(F32)[:, 0:step * NT].rearrange("p (q b) -> p q b", b=NT)
            for c in range(16):
                s = slice(c * step, (c + 1) * step)
                V.tensor_tensor(wide, iota_q[:, s].unsqueeze(2).to_broadcast([1, step, NT]),
                                qlast[:].unsqueeze(1).to_broadcast([1, step, NT]), ALU.is_gt)
                dve.drain()
                V.tensor_reduce(nb[:, s], wide, AX_X, ALU.add)
                dve.drain()
            V.tensor_tensor(nb[:], nb[:], iota_q[:], ALU.add)
            V.memset(needtab[:], 4)
            dve.drain()
            V.tensor_scalar(needtab[:, RQ:], nb[:, 1:QUADS - RQ + 1], 4.0, 4.0, ALU.mult, ALU.add).then_inc(tab_ready, 1)

            def gcn(i):
                wait(dve, part_in, 16 * NTAB * (i + 1))
                wait(dve, c_mm, BG * i)
                V.tensor_tensor(part[:, :, 0:EF], part4[:, 0], part4[:, 1], ALU.add)
                V.tensor_tensor(part4[:, 2], part4[:, 2], part4[:, 3], ALU.add)
                dve.drain()
                V.tensor_tensor(part[:, :, 0:EF], part[:, :, 0:EF], part4[:, 2], ALU.add).then_inc(part_ready, 1)
                wait(dve, g_out_s, 16 * i)
                wait(dve, b_out_s, 16 * i)
                def leaky(j):
                    wait(dve, e_ready, BG * i + j + 1)
                    wait(dve, c_mm, BG * i + j - min(j, 1))
                    V.scalar_tensor_tensor(out=eT[:, j % 2], in0=e1[:], scalar=LRELU, in1=e1[:], op0=ALU.mult,
                                           op1=ALU.max).then_inc(eT_ready, 1)

                leaky(0)
                for j in range(BG):
                    t = BG * i + j
                    y = [ps6, ps7][j % 2]
                    if j + 1 < BG:
                        leaky(j + 1)
                    dve.drain()
                    wait(dve, c_mm, t + 1)
                    di = dinv[:, bass.ds(t, 1)]
                    V.tensor_scalar(g_st[:, j, :], y[:, 0:D], di, None, ALU.mult)
                    V.tensor_tensor(zt[:], y[:, D:], bc["bc"][:], ALU.add)
                    dve.drain()
                    V.scalar_tensor_tensor(out=b_out[:, j, :], in0=g_st[:, j, :], scalar=di, in1=zt[:],
                                           op0=ALU.mult, op1=ALU.add).then_inc(gb_ready, 1)

            gcn(0)
            with dve.Fori(1, NT // BG) as i:
                gcn(i)

            dve.wait_ge(g_out_s, 16 * (NT // BG))
            dve.wait_ge(b_out_s, 16 * (NT // BG))
            dve.drain()
            V.memset(acc[:], 0.0).then_inc(dstl_ready, 1)

            def quads_of(b):
                return [dve.value_load(qtab[0:1, bass.ds(b + n, 1)], min_val=0, max_val=QUADS - 1) for n in range(2)]

            def onehots(b, lo, hi):
                with dve.Fori(lo, hi + 1) as q:
                    for jj in range(4):
                        dve.wait_ge(agg_tile, (q + b) * 4 + jj + 1)
                        V.tensor_scalar(oh[:, jj, :], iota_r[:], dst_t[:, bass.ds(q * 4 + jj, 1)],
                                        node0[:, bass.ds(b, 1)], ALU.subtract, ALU.is_equal).then_inc(oneh_ready, 1)

            def node_out(b, s, piece):
                y, t, a = rs[:, 1, 0:1], rs[:, 2, 0:1], rs[:, 0, 0:1]
                if piece == 0:
                    wait(dve, agg_done, b + 1)
                    wait(dve, base_in, 16 * (b + 1))
                    V.scalar_tensor_tensor(out=x_in4[:, s, :], in0=ps0[:, 0:D], scalar=dinv[:, bass.ds(b, 1)], in1=base_t[:],
                                           op0=ALU.mult, op1=ALU.add).then_inc(agg_read, 1)
                    dve.drain()
                    wait(dve, mixr_in, 16 * (b + 1))
                    V.scalar_tensor_tensor(out=x_in4[:, s, :], in0=x_in4[:, s, :], scalar=0.0, in1=mix_t[:],
                                           op0=ALU.max, op1=ALU.add).then_inc(nodein_read, 1)
                    dve.drain()
                    V.bn_stats(stats[:, 0, :], x_in4[:, s, :])
                if piece == 1:
                    dve.drain()
                    V.bn_aggr(mv[:, 0, :], stats[:, 0, :])
                    dve.drain()
                    V.tensor_scalar(a, mv[:, 0, 1:2], LN_EPS, None, ALU.add)
                    dve.drain()
                    V.tensor_single_scalar(rs_i[:, 0:1], a.bitcast(I32), 1, op=ALU.arith_shift_right)
                    dve.drain()
                    V.tensor_scalar(a, a, -0.5, None, ALU.mult)
                    V.tensor_scalar(y.bitcast(I32), rs_i[:, 0:1], -1.0, float(0x5F3759DF), ALU.mult, ALU.add)
                if piece in (2, 3, 4):
                    dve.drain()
                    V.tensor_scalar(t, y, y, a, ALU.mult, ALU.mult)
                    dve.drain()
                    V.scalar_tensor_tensor(out=y, in0=t, scalar=1.5, in1=y, op0=ALU.add, op1=ALU.mult)
                if piece == 4:
                    dve.drain()
                    V.tensor_scalar(xl4[:, s, :], x_in4[:, s, :], mv[:, 0, 0:1], y, ALU.subtract, ALU.mult).then_inc(xl_ready, 1)

            def route(g, tiles):
                t = slice(0, tiles)
                wait(dve, gate_mm, g + 1)
                V.tensor_tensor(score[:, t], ps1[:, 0:tiles * NEXP].rearrange("p (r e) -> p r e", e=NEXP),
                                bg_bc[:].unsqueeze(1).to_broadcast([P, tiles, NEXP]), ALU.add)
                dve.drain()
                for r in range(tiles):
                    V.max(top[:, r], score[:, r])
                dve.drain()
                for r in range(tiles):
                    V.max_index(topi[:, r], top[:, r], score[:, r])
                dve.drain()
                V.tensor_copy(topf[:, t], topi[:, t])
                dve.drain()
                number = iota_r[:, 0:NEXP].unsqueeze(1).to_broadcast([P, tiles, NEXP])
                V.tensor_tensor(mask1[:, t], number, topf[:, t, 0:1].to_broadcast([P, tiles, NEXP]), ALU.is_equal)
                V.tensor_tensor(mask[:, t], number, topf[:, t, 1:2].to_broadcast([P, tiles, NEXP]), ALU.is_equal)
                dve.drain()
                V.tensor_tensor(mask[:, t], mask[:, t], mask1[:, t], ALU.add).then_inc(mask_ready, 1)

            def experts(g, tiles, following):
                W = tiles * P
                for k in range(KD):
                    wait(dve, xlThi_ready, KD * g + k + 1)
                    V.tensor_tensor(xlT[1][:, k, 0:W], [ps2, ps3][k][:, 0:W], xlT[0][:, k, 0:W].bitcast(F32),
                                    ALU.subtract).then_inc(xlTlo_ready, 1)
                for u in range(NEXP * KH):
                    v = NEXP * KH * g + u
                    if u - 1 in INSERT[:following]:
                        lo, hi = quads_of(g * GRP + GRP + INSERT.index(u - 1))
                    wait(dve, gelu_ready, v + 1)
                    wait(dve, dn_mm, v - min(u, 1))
                    V.tensor_tensor(hhl[1][:, u % 2, 0:W], hf[:, 0:W], hhl[0][:, u % 2, 0:W].bitcast(F32),
                                    ALU.subtract).then_inc(lo_ready, 1)
                    if u == 1:
                        route(g, tiles)
                    if u == 3:
                        wait(dve, stored, 16 * g)
                        wait(dve, bias_mm, g + 1)
                        for r in range(0, tiles, 2):
                            n = min(2, tiles - r)
                            ins = V.tensor_tensor(acc[:, r:r + n], x_in4[:, r:r + n],
                                                  [ps4, ps5][r // 2][:, 0:n * D].rearrange("p (n d) -> p n d", n=n), ALU.add)
                        ins.then_inc(acc_ready, 1)
                    if u % KH == 0 and u or u == NEXP * KH - 1:
                        for e in [u // KH - 1] if u < NEXP * KH - 1 else [NEXP - 1]:
                            dve.drain()
                            wait(dve, dn_mm, NEXP * KH * g + KH * (e + 1))
                            for r in range(tiles):
                                ins = V.scalar_tensor_tensor(
                                    out=acc[:, r, :], in0=[[ps2, ps3], [ps4, ps5]][e % 2][r // 2][:, (r % 2) * D:(r % 2 + 1) * D],
                                    scalar=mask[:, r, e:e + 1], in1=acc[:, r, :], op0=ALU.mult, op1=ALU.add)
                            ins.then_inc(comb_done, 1)
                    for s in range(following):
                        after = u - 1 - INSERT[s]
                        if after == 0:
                            onehots(g * GRP + GRP + s, lo, hi)
                            node_out(g * GRP + GRP + s, s, 0)
                        elif 1 <= after <= 4:
                            node_out(g * GRP + GRP + s, s, after)

            for b in range(GRP):
                onehots(b, *quads_of(b))
                for piece in range(5):
                    node_out(b, b, piece)
            experts(0, GRP, GRP)
            with dve.Fori(1, NG - 1) as g:
                experts(g, GRP, GRP)
            experts(NG - 1, GRP, 1)
            experts(NG, 1, 0)


_INS = ["x", "src", "dst", "edge_attr_64", "L0_gnn_W_edge", "L0_gnn_b_edge", "L0_gnn_W_conv", "L0_gnn_b_conv",
        "L0_gnn_W_res", "L0_gnn_b_res", "L0_mix_Wq", "L0_mix_bq", "L0_mix_Wk", "L0_mix_bk", "L0_mix_Wv", "L0_mix_bv",
        "L0_mix_Wo", "L0_mix_bo", "L0_mix_W1", "L0_mix_b1", "L0_mix_W2", "L0_mix_b2", "L0_mix_ln1_g", "L0_mix_ln1_b",
        "L0_mix_ln2_g", "L0_mix_ln2_b", "L0_ffn_Wg", "L0_ffn_bg", "L0_ffn_W1", "L0_ffn_b1", "L0_ffn_W2", "L0_ffn_b2"]


def kernel(**inputs):
    import numpy as np
    import concourse.bacc as bacc
    from concourse.bass_utils import run_bass_kernel_spmd

    def padded(a, n, value):
        tail = np.full((n - a.shape[0],) + a.shape[1:], value, a.dtype)
        return np.concatenate([a, tail])

    nc = bacc.Bacc("TRN2", target_bir_lowering=False, num_devices=1)
    arrays, aps = {}, {}
    for name in _INS:
        a = np.ascontiguousarray(inputs[name])
        if name == "x":
            a = padded(a, NP, 0)
        elif name in ("src", "dst"):
            a = padded(a, EP, NP)
        elif name == "edge_attr_64":
            a = padded(a, EP, 0)
        arrays[f"in_{name}"] = a
        aps[name] = nc.dram_tensor(f"in_{name}", a.shape, mybir.dt.from_np(a.dtype), kind="ExternalInput").ap()
    out = nc.dram_tensor("out", (NP, D), F32, kind="ExternalOutput").ap()
    build(nc, aps, out)
    result = run_bass_kernel_spmd(nc, [arrays], core_ids=[0])
    return result.results[0]["out"][:N]
```
